# Optimizing a Trainium2 kernel written in Bass

```python
import numpy as np
import jax
import jax.numpy as jnp

def _softmax(x, axis=-1):
    return jax.nn.softmax(x, axis=axis)

def _gelu(x):
    return jax.nn.gelu(x, approximate=True)

def _silu(x):
    return jax.nn.silu(x)

def _sigmoid(x):
    return jax.nn.sigmoid(x)

def _layernorm(x, axis=-1, eps=1e-05):
    m = jnp.mean(x, axis=axis, keepdims=True)
    v = jnp.var(x, axis=axis, keepdims=True)
    return (x - m) / jnp.sqrt(v + eps)

def _scatter_add(tgt, idx, src, axis=0):
    return tgt.at[idx].add(src)

def _segment_sum(src, seg, n):
    return jax.ops.segment_sum(src, seg, n)
kernel_name = 'mk_conv_attn_hybrid_d4_conv_nchw512_r4_86cd5a'

def setup_inputs(seed: int=0):
    np.random.seed(seed)
    _w = jnp.asarray

    def _rec_inputs():
        import jax
        import jax.numpy as jnp
        _gk = jax.random.key(seed)
        x = -0.000125 + 0.9999 * jax.random.normal(jax.random.fold_in(_gk, 1), (16, 128, 32, 32), jnp.float32)
        return x
    x = _rec_inputs()

    def _L0_conv_setup():
        import jax, jax.numpy as jnp
        import numpy as np
        TIME_STEP = 8
        VTH = 1.0
        A = 1.0
        TAU = 0.5

        def _conv1d(x, w, pad):
            return jax.lax.conv_general_dilated(x, w, (1,), [(pad, pad)], dimension_numbers=('NCH', 'OIH', 'NCH'))

        def _conv2d(x, w, pad):
            return jax.lax.conv_general_dilated(x, w, (1, 1), [(pad, pad), (pad, pad)], dimension_numbers=('NCHW', 'OIHW', 'NCHW'))
        key = jax.random.key(seed)
        k1, k2, k3, k4 = jax.random.split(key, 4)
        x = jax.random.normal(k1, (16, 128, 32, 32), jnp.float32)
        w_channel = jax.random.normal(k2, (1, 1, 5), jnp.float32) * 0.1
        w_spatial = jax.random.normal(k3, (1, 2, 5, 5), jnp.float32) * 0.1
        w_temporal = jax.random.normal(k4, (1, 1, 5), jnp.float32) * 0.1
        return {'x': x, 'w_channel': w_channel, 'w_spatial': w_spatial, 'w_temporal': w_temporal}
    _L0_conv_all = _L0_conv_setup()
    _L0_conv_in = {k: v for k, v in _L0_conv_all.items() if k in ('w_channel', 'w_spatial', 'w_temporal')}
    del _L0_conv_all

    def _L1_conv_setup():
        import jax, jax.numpy as jnp
        import numpy as np
        from jax import lax
        DN = ('NCHW', 'OIHW', 'NCHW')
        key = jax.random.key(seed)
        ks = jax.random.split(key, 5)
        B, C, H, W = (32, 128, 56, 56)
        R = 16
        return {'x': jax.random.normal(ks[0], (B, C, H, W), jnp.float32), 'w1': jax.random.normal(ks[1], (1, 3, 3, 3), jnp.float32) * 0.2, 'w2': jax.random.normal(ks[2], (1, 1, 3, 3), jnp.float32) * 0.2, 'fc1_w': jax.random.normal(ks[3], (C // R, C), jnp.float32) * 0.05, 'fc2_w': jax.random.normal(ks[4], (C, C // R), jnp.float32) * 0.05}
    _L1_conv_all = _L1_conv_setup()
    _L1_conv_in = {k: v for k, v in _L1_conv_all.items() if k in ('w1', 'w2', 'fc1_w', 'fc2_w')}
    del _L1_conv_all

    def _L2_attn_setup():
        import jax, jax.numpy as jnp
        import numpy as np
        D_MODEL = 128
        N_HEADS = 8
        N_KV = 2
        D_K = D_MODEL // N_HEADS
        N_GROUPS = N_HEADS // N_KV
        B, S = (32, 256)
        key = jax.random.key(seed)
        k = jax.random.split(key, 5)
        scale = 1.0 / np.sqrt(D_MODEL)
        return {'x': jax.random.normal(k[0], (B, S, D_MODEL), dtype=jnp.float32), 'Wq': jax.random.normal(k[1], (D_MODEL, D_MODEL), dtype=jnp.float32) * scale, 'Wk': jax.random.normal(k[2], (D_MODEL, N_KV * D_K), dtype=jnp.float32) * scale, 'Wv': jax.random.normal(k[3], (D_MODEL, N_KV * D_K), dtype=jnp.float32) * scale, 'Wo': jax.random.normal(k[4], (D_MODEL, D_MODEL), dtype=jnp.float32) * scale}
    _L2_attn_all = _L2_attn_setup()
    _L2_attn_in = {k: v for k, v in _L2_attn_all.items() if k in ('Wq', 'Wk', 'Wv', 'Wo')}
    del _L2_attn_all

    def _L2_ffn_setup():
        import jax, jax.numpy as jnp
        import numpy as np
        B, S, D, DFF, E, K = (4, 512, 128, 256, 8, 2)
        key = jax.random.key(seed)
        ks = jax.random.split(key, 5)
        x = jax.random.normal(ks[0], (B, S, D), dtype=jnp.float32)
        Wg = jax.random.normal(ks[1], (D, E), dtype=jnp.float32) * 0.02
        bg = jnp.zeros((E,), dtype=jnp.float32)
        W1 = jax.random.normal(ks[2], (E, D, 2 * DFF), dtype=jnp.float32) * 0.02
        b1 = jnp.zeros((E, 2 * DFF), dtype=jnp.float32)
        W2 = jax.random.normal(ks[3], (E, DFF, D), dtype=jnp.float32) * 0.02
        b2 = jnp.zeros((E, D), dtype=jnp.float32)
        return {'x': x, 'Wg': Wg, 'bg': bg, 'W1': W1, 'b1': b1, 'W2': W2, 'b2': b2}
    _L2_ffn_all = _L2_ffn_setup()
    _L2_ffn_in = {k: v for k, v in _L2_ffn_all.items() if k in ('Wg', 'bg', 'W1', 'b1', 'W2', 'b2')}
    del _L2_ffn_all

    def _L3_attn_setup():
        import jax, jax.numpy as jnp
        import numpy as np
        B, L, H, D = (2, 256, 8, 16)
        DIM = H * D
        key = jax.random.key(seed)
        ks = jax.random.split(key, 12)
        s = 0.02
        return {'x': jax.random.normal(ks[0], (B, L, DIM), dtype=jnp.float32), 'wq_w': jax.random.normal(ks[1], (DIM, DIM), dtype=jnp.float32) * s, 'wq_b': jax.random.normal(ks[2], (DIM,), dtype=jnp.float32) * s, 'wk_w': jax.random.normal(ks[3], (DIM, DIM), dtype=jnp.float32) * s, 'wk_b': jax.random.normal(ks[4], (DIM,), dtype=jnp.float32) * s, 'wv_w': jax.random.normal(ks[5], (DIM, DIM), dtype=jnp.float32) * s, 'wv_b': jax.random.normal(ks[6], (DIM,), dtype=jnp.float32) * s, 'phazor_re': jax.random.normal(ks[7], (H, D), dtype=jnp.float32), 'phazor_im': jax.random.normal(ks[8], (H, D), dtype=jnp.float32), 'amplitude': jax.random.normal(ks[9], (H,), dtype=jnp.float32), 'last_conv_re': jax.random.normal(ks[10], (H, D, D), dtype=jnp.float32), 'last_conv_im': jax.random.normal(ks[11], (H, D, D), dtype=jnp.float32)}
    _L3_attn_all = _L3_attn_setup()
    _L3_attn_in = {k: v for k, v in _L3_attn_all.items() if k in ('wq_w', 'wq_b', 'wk_w', 'wk_b', 'wv_w', 'wv_b', 'phazor_re', 'phazor_im', 'amplitude', 'last_conv_re', 'last_conv_im')}
    del _L3_attn_all

    def _L3_ffn_setup():
        import jax, jax.numpy as jnp
        import numpy as np
        NUM_EXPERTS = 8
        TOP_K = 2
        key = jax.random.key(seed)
        ks = jax.random.split(key, 5)
        B, N, E, H, X = (8, 512, 128, 192, NUM_EXPERTS)
        s_in = 0.02
        return {'x': jax.random.normal(ks[0], (B, N, E), dtype=jnp.float32), 'Wg': jax.random.normal(ks[1], (E, X), dtype=jnp.float32) * s_in, 'bg': jnp.zeros((X,), dtype=jnp.float32), 'W1': jax.random.normal(ks[2], (X, E, H), dtype=jnp.float32) * (1.0 / np.sqrt(E)), 'b1': jnp.zeros((X, H), dtype=jnp.float32), 'W2': jax.random.normal(ks[3], (X, H, E), dtype=jnp.float32) * (1.0 / np.sqrt(H)), 'b2': jnp.zeros((X, E), dtype=jnp.float32)}
    _L3_ffn_all = _L3_ffn_setup()
    _L3_ffn_in = {k: v for k, v in _L3_ffn_all.items() if k in ('Wg', 'bg', 'W1', 'b1', 'W2', 'b2')}
    del _L3_ffn_all
    return {'x': x, 'L0_conv_w_channel': _L0_conv_in['w_channel'], 'L0_conv_w_spatial': _L0_conv_in['w_spatial'], 'L0_conv_w_temporal': _L0_conv_in['w_temporal'], 'L1_conv_w1': _L1_conv_in['w1'], 'L1_conv_w2': _L1_conv_in['w2'], 'L1_conv_fc1_w': _L1_conv_in['fc1_w'], 'L1_conv_fc2_w': _L1_conv_in['fc2_w'], 'L2_attn_Wq': _L2_attn_in['Wq'], 'L2_attn_Wk': _L2_attn_in['Wk'], 'L2_attn_Wv': _L2_attn_in['Wv'], 'L2_attn_Wo': _L2_attn_in['Wo'], 'L2_ffn_Wg': _L2_ffn_in['Wg'], 'L2_ffn_bg': _L2_ffn_in['bg'], 'L2_ffn_W1': _L2_ffn_in['W1'], 'L2_ffn_b1': _L2_ffn_in['b1'], 'L2_ffn_W2': _L2_ffn_in['W2'], 'L2_ffn_b2': _L2_ffn_in['b2'], 'L3_attn_wq_w': _L3_attn_in['wq_w'], 'L3_attn_wq_b': _L3_attn_in['wq_b'], 'L3_attn_wk_w': _L3_attn_in['wk_w'], 'L3_attn_wk_b': _L3_attn_in['wk_b'], 'L3_attn_wv_w': _L3_attn_in['wv_w'], 'L3_attn_wv_b': _L3_attn_in['wv_b'], 'L3_attn_phazor_re': _L3_attn_in['phazor_re'], 'L3_attn_phazor_im': _L3_attn_in['phazor_im'], 'L3_attn_amplitude': _L3_attn_in['amplitude'], 'L3_attn_last_conv_re': _L3_attn_in['last_conv_re'], 'L3_attn_last_conv_im': _L3_attn_in['last_conv_im'], 'L3_ffn_Wg': _L3_ffn_in['Wg'], 'L3_ffn_bg': _L3_ffn_in['bg'], 'L3_ffn_W1': _L3_ffn_in['W1'], 'L3_ffn_b1': _L3_ffn_in['b1'], 'L3_ffn_W2': _L3_ffn_in['W2'], 'L3_ffn_b2': _L3_ffn_in['b2']}

def reference(x, L0_conv_w_channel, L0_conv_w_spatial, L0_conv_w_temporal, L1_conv_w1, L1_conv_w2, L1_conv_fc1_w, L1_conv_fc2_w, L2_attn_Wq, L2_attn_Wk, L2_attn_Wv, L2_attn_Wo, L2_ffn_Wg, L2_ffn_bg, L2_ffn_W1, L2_ffn_b1, L2_ffn_W2, L2_ffn_b2, L3_attn_wq_w, L3_attn_wq_b, L3_attn_wk_w, L3_attn_wk_b, L3_attn_wv_w, L3_attn_wv_b, L3_attn_phazor_re, L3_attn_phazor_im, L3_attn_amplitude, L3_attn_last_conv_re, L3_attn_last_conv_im, L3_ffn_Wg, L3_ffn_bg, L3_ffn_W1, L3_ffn_b1, L3_ffn_W2, L3_ffn_b2):
    import jax
    import jax.numpy as jnp

    def _L0_conv_ref(x, w_channel, w_spatial, w_temporal):
        import jax, jax.numpy as jnp
        import numpy as np
        TIME_STEP = 8
        VTH = 1.0
        A = 1.0
        TAU = 0.5

        def _conv1d(x, w, pad):
            return jax.lax.conv_general_dilated(x, w, (1,), [(pad, pad)], dimension_numbers=('NCH', 'OIH', 'NCH'))

        def _conv2d(x, w, pad):
            return jax.lax.conv_general_dilated(x, w, (1, 1), [(pad, pad), (pad, pad)], dimension_numbers=('NCHW', 'OIHW', 'NCHW'))
        TB, C, H, W = x.shape
        bs = TB // TIME_STEP
        xs = x.reshape(TIME_STEP, bs, C, H, W)

        def scan_fn(u, xt):
            u = TAU * u + xt
            s = (u > VTH).astype(u.dtype)
            avg = jnp.mean(s, axis=(1, 2, 3))
            return (u - s, (s, avg))
        u0 = jnp.zeros((bs, C, H, W), x.dtype)
        _, (o, avg) = jax.lax.scan(scan_fn, u0, xs)
        o_flat = o.reshape(TB, C, H, W)
        channel_avg = jnp.mean(o_flat, axis=(2, 3))[:, None, :]
        ch_att = _conv1d(channel_avg, w_channel, 2)[:, 0, :, None, None]
        sp_in = jnp.stack([jnp.mean(o_flat, axis=1), jnp.max(o_flat, axis=1)], axis=1)
        sp_att = _conv2d(sp_in, w_spatial, 2)
        temporal_avgo = avg.T[:, None, :]
        tm_att = _conv1d(temporal_avgo, w_temporal, 2)
        tem = tm_att[:, 0, :].T.reshape(TB)
        prod = tem[:, None, None, None] * ch_att * sp_att
        mask = (prod >= 0).astype(x.dtype)
        return o_flat * mask

    def _L1_conv_ref(x, w1, w2, fc1_w, fc2_w):
        import jax, jax.numpy as jnp
        import numpy as np
        from jax import lax
        DN = ('NCHW', 'OIHW', 'NCHW')
        b, c, h, w = x.shape
        y1 = jnp.broadcast_to(x.mean(axis=(2, 3), keepdims=True), (b, c, 4, 4))
        y2 = x.reshape(b, c, 2, h // 2, 2, w // 2).mean(axis=(3, 5))
        y2 = jnp.repeat(jnp.repeat(y2, 2, axis=2), 2, axis=3)
        y4 = x.reshape(b, c, 4, h // 4, 4, w // 4).mean(axis=(3, 5))
        t = jnp.stack([y1, y2, y4], axis=2).reshape(b * c, 3, 4, 4)
        z = lax.conv_general_dilated(t, w1, (1, 1), 'VALID', dimension_numbers=DN)
        z = lax.conv_general_dilated(z, w2, (3, 3), [(1, 1), (1, 1)], dimension_numbers=DN)
        s = z.reshape(b, c)
        s = jax.nn.relu(s @ fc1_w.T) @ fc2_w.T
        s = jax.nn.sigmoid(s).reshape(b, c, 1, 1)
        return x * s

    def _L2_attn_ref(x, Wq, Wk, Wv, Wo):
        import jax, jax.numpy as jnp
        import numpy as np
        D_MODEL = 128
        N_HEADS = 8
        N_KV = 2
        D_K = D_MODEL // N_HEADS
        N_GROUPS = N_HEADS // N_KV
        B, S = (32, 256)
        b, s, _ = x.shape
        q = (x @ Wq).reshape(b, s, N_HEADS, D_K)
        kk = (x @ Wk).reshape(b, s, N_KV, D_K)
        v = (x @ Wv).reshape(b, s, N_KV, D_K)
        q = q.reshape(b, s, N_KV, N_GROUPS, D_K)
        inv_sqrt_dk = 1.0 / np.sqrt(D_K)
        scores = jnp.einsum('bqkgd,btkd->bkgqt', q, kk) * inv_sqrt_dk
        attn = jax.nn.softmax(scores, axis=-1)
        out = jnp.einsum('bkgqt,btkd->bqkgd', attn, v)
        out = out.reshape(b, s, D_MODEL)
        return out @ Wo

    def _L2_ffn_ref(x, Wg, bg, W1, b1, W2, b2):
        import jax, jax.numpy as jnp
        import numpy as np
        B, S, D, DFF, E, K = (4, 512, 128, 256, 8, 2)
        n_experts = W1.shape[0]
        logits = jnp.einsum('bsd,de->bse', x, Wg) + bg
        topk_vals, topk_idx = jax.lax.top_k(logits, K)
        topk_w = jax.nn.softmax(topk_vals, axis=-1)
        one_hot = jax.nn.one_hot(topk_idx, n_experts, dtype=x.dtype)
        weights_per_expert = jnp.einsum('bske,bsk->bse', one_hot, topk_w)
        h = jnp.einsum('bsd,edf->bsef', x, W1) + b1
        a, g = jnp.split(h, 2, axis=-1)
        act = jax.nn.silu(a) * g
        expert_out = jnp.einsum('bsef,efd->bsed', act, W2) + b2
        return jnp.einsum('bse,bsed->bsd', weights_per_expert, expert_out)

    def _L3_attn_ref(x, wq_w, wq_b, wk_w, wk_b, wv_w, wv_b, phazor_re, phazor_im, amplitude, last_conv_re, last_conv_im):
        import jax, jax.numpy as jnp
        import numpy as np
        B, L, H, D = (2, 256, 8, 16)
        DIM = H * D
        b, l, _ = x.shape
        h, d = phazor_re.shape
        cplx = jnp.complex64
        q = (x @ wq_w.T + wq_b).reshape(b, l, h, d)
        k = (x @ wk_w.T + wk_b).reshape(b, l, h, d)
        v = (x @ wv_w.T + wv_b).reshape(b, l, h, d)
        phazor_p = (phazor_re + 1j * phazor_im).astype(cplx)
        phase = phazor_p / jnp.abs(phazor_p)
        amp = jax.nn.sigmoid(amplitude)
        phazor = phase * amp[:, None]
        t = jnp.arange(l)
        phase_prog = phase[None] ** t[:, None, None]
        phase_prog_inv = phase[None] ** (-t)[:, None, None]
        phazor_prog = phazor[None] ** t[:, None, None]
        last_conv = (last_conv_re + 1j * last_conv_im).astype(cplx)
        qc = q.astype(cplx) * (phazor_prog * phazor[None])[None]
        cross = jnp.einsum('blhd,hde->blhe', qc, last_conv)
        diff = t[:, None] - t[None, :]
        tril = diff >= 0
        mask = jnp.where(tril[None], amp[:, None, None] ** jnp.where(tril, diff, 0)[None], 0.0)
        qph = q.astype(cplx) * phase_prog[None]
        kph = k.astype(cplx) * phase_prog_inv[None]
        qk = jnp.einsum('blhd,bmhd->bhlm', qph, kph)
        qk_mask = qk * mask[None].astype(cplx)
        inner = jnp.einsum('bhlm,bmhd->blhd', qk_mask, v.astype(cplx))
        out = (inner + cross).real.astype(x.dtype).reshape(b, l, h * d)
        return out

    def _L3_ffn_ref(x, Wg, bg, W1, b1, W2, b2):
        import jax, jax.numpy as jnp
        import numpy as np
        NUM_EXPERTS = 8
        TOP_K = 2
        scores = jnp.einsum('bne,ex->bnx', x, Wg) + bg
        topk_vals, topk_idx = jax.lax.top_k(scores, TOP_K)
        gates = jax.nn.softmax(topk_vals, axis=-1)
        h = jnp.einsum('bne,xeh->bnxh', x, W1) + b1
        h = jax.nn.gelu(h, approximate=False)
        expert_out = jnp.einsum('bnxh,xhe->bnxe', h, W2) + b2
        onehot = jax.nn.one_hot(topk_idx, NUM_EXPERTS, dtype=x.dtype)
        combine = jnp.einsum('bnk,bnkx->bnx', gates, onehot)
        out = jnp.einsum('bnx,bnxe->bne', combine, expert_out)
        return out

    def _gn(v, G=32, eps=1e-05):
        B_, C_, H_, W_ = v.shape
        g = v.reshape(B_, G, C_ // G, H_, W_)
        m = jnp.mean(g, axis=(2, 3, 4), keepdims=True)
        s = jnp.var(g, axis=(2, 3, 4), keepdims=True)
        return ((g - m) / jnp.sqrt(s + eps)).reshape(v.shape)

    def _ln_c(v, eps=1e-06):
        m = jnp.mean(v, axis=1, keepdims=True)
        s = jnp.var(v, axis=1, keepdims=True)
        return (v - m) / jnp.sqrt(s + eps)

    def _ln_t(v, eps=1e-05):
        m = jnp.mean(v, axis=-1, keepdims=True)
        s = jnp.var(v, axis=-1, keepdims=True)
        return (v - m) / jnp.sqrt(s + eps)

    def _to_tokens(v):
        B_, C_, H_, W_ = v.shape
        return v.reshape(B_, C_, H_ * W_).transpose(0, 2, 1)

    def _from_tokens(t, like):
        B_, C_, H_, W_ = like.shape
        return t.transpose(0, 2, 1).reshape(B_, C_, H_, W_)
    x = x + _L0_conv_ref(_gn(x), L0_conv_w_channel, L0_conv_w_spatial, L0_conv_w_temporal)
    x = x + _L1_conv_ref(_gn(x), L1_conv_w1, L1_conv_w2, L1_conv_fc1_w, L1_conv_fc2_w)
    t = _to_tokens(x)
    t = t + _L2_attn_ref(_ln_t(t), L2_attn_Wq, L2_attn_Wk, L2_attn_Wv, L2_attn_Wo)
    t = t + _L2_ffn_ref(_ln_t(t), L2_ffn_Wg, L2_ffn_bg, L2_ffn_W1, L2_ffn_b1, L2_ffn_W2, L2_ffn_b2)
    t = t + _L3_attn_ref(_ln_t(t), L3_attn_wq_w, L3_attn_wq_b, L3_attn_wk_w, L3_attn_wk_b, L3_attn_wv_w, L3_attn_wv_b, L3_attn_phazor_re, L3_attn_phazor_im, L3_attn_amplitude, L3_attn_last_conv_re, L3_attn_last_conv_im)
    t = t + _L3_ffn_ref(_ln_t(t), L3_ffn_Wg, L3_ffn_bg, L3_ffn_W1, L3_ffn_b1, L3_ffn_W2, L3_ffn_b2)
    x = _from_tokens(t, x)
    return x

_drawn_inputs = setup_inputs


def setup_inputs(seed=0):
    import zlib

    import numpy as np

    out = dict(_drawn_inputs(seed))
    spreads = {'L2_ffn_bg': (0.0, 0.1),
     'L2_ffn_b1': (0.0, 0.767),
     'L2_ffn_b2': (0.0, 0.1),
     'L3_ffn_bg': (0.0, 0.1),
     'L3_ffn_b1': (0.0, 0.293),
     'L3_ffn_b2': (0.0, 0.1)}
    factors = {'L1_conv_w1': 8.0,
     'L1_conv_w2': 8.0,
     'L1_conv_fc1_w': 8.0,
     'L1_conv_fc2_w': 8.0,
     'L2_ffn_W1': 3.872,
     'L2_ffn_W2': 3.971,
     'L3_attn_wq_b': 4.606,
     'L3_attn_wk_b': 4.895,
     'L3_attn_wv_b': 4.841,
     'L3_attn_last_conv_re': 3.938,
     'L3_attn_last_conv_im': 3.978}
    for name, (base, spread) in spreads.items():
        noise = np.random.default_rng([zlib.crc32(name.encode()), seed]).standard_normal(out[name].shape)
        drawn = base * np.exp(spread * noise) if base else spread * noise
        out[name] = jnp.asarray(drawn.astype(out[name].dtype))
    for name, factor in factors.items():
        out[name] = (out[name] * factor).astype(out[name].dtype)
    return out
```

```python
from contextlib import ExitStack

import concourse.bass as bass
from concourse import mybir

F32 = mybir.dt.float32
BF16 = mybir.dt.bfloat16
U32 = mybir.dt.uint32
ALU = mybir.AluOpType
ACT = mybir.ActivationFunctionType
AX = mybir.AxisListType

P = 128
IMAGES = 16
C = 128
SIDE = 32
PX = SIDE * SIDE
TOK = IMAGES * PX
TILES = PX // P
HALF = 512
EPS_T = 1e-5
E = 8


def ds(at, n):
    return bass.ds(at, n)


def allocator(nc, ctx):
    def sb(name, shape, dt=F32):
        return ctx.enter_context(nc.sbuf_tensor(name, shape, dt))

    def ps(name, shape, dt=F32):
        return ctx.enter_context(nc.psum_tensor(name, shape, dt))

    def sem(name):
        return nc.alloc_semaphore(name)

    return sb, ps, sem


def wait_apart(eng, s, value, passed):
    eng.wait_ge(s, value)
    eng.sem_inc(passed, 1)


TIME = 8
PER_STEP = IMAGES // TIME
TAPS = 5
EPS_G = 1e-5
CH_GROUP = 4
SQUEEZED = 8


def convolution_stage(nc, T, ident, dram):
    with ExitStack() as ctx:
        sb, ps, sem = allocator(nc, ctx)
        X = sb("a_x", [P, IMAGES * PX])
        spikes = sb("a_spikes", [P, IMAGES * PX], BF16)
        u = sb("a_u", [P, PER_STEP * PX])
        xh = T[:, 0:2 * PER_STEP * PX].rearrange("p (k x) -> p k x", k=2)
        strips = T[:, 2 * PER_STEP * PX:2 * PER_STEP * PX + IMAGES * SIDE * 4]
        wide = T[:, TOK // 2:TOK // 2 + P * TAPS].rearrange("p (o k) -> p o k", k=TAPS)
        stats = sb("a_stats", [P, IMAGES, 2, 6])
        mv = sb("a_mv", [P, IMAGES, 2])
        both = sb("a_both", [P, 2, IMAGES])
        group = sb("a_group", [P, P])
        tmp = sb("a_tmp", [P, IMAGES])
        scale = sb("a_scale", [P, IMAGES])
        shift = sb("a_shift", [P, IMAGES])
        mhalf = sb("a_mhalf", [P, IMAGES])
        eps = sb("a_eps", [P, IMAGES])
        zero = sb("a_zero", [P, IMAGES])
        counts = sb("a_counts", [P, IMAGES])
        average = sb("a_average", [P, IMAGES])
        picks = sb("a_picks", [P, 63], BF16)
        maps = sb("a_maps", [2 * IMAGES, 2, HALF])
        rows = sb("a_rows", [2 * SIDE, IMAGES, SIDE + TAPS - 1])
        ones = sb("a_ones", [P, TAPS, P])
        near = sb("a_near", [P, TAPS, P])
        near_y = sb("a_near_y", [2 * SIDE, TAPS, SIDE])
        w_ch = sb("a_w_ch", [P, TAPS])
        w_t = sb("a_w_t", [P, TAPS])
        w_sp = sb("a_w_sp", [2 * SIDE, TAPS * TAPS])
        wide_y = sb("a_wide_y", [2 * SIDE, TAPS, SIDE, TAPS])
        band_ch = sb("a_band_ch", [P, P])
        band_sp = sb("a_band_sp", [2 * SIDE, TAPS, SIDE])
        mean_all = sb("a_mean_all", [P, P])
        times = sb("a_times", [P, TIME + TAPS - 1, PER_STEP])
        temporal = sb("a_temporal", [P, IMAGES])
        factor = sb("a_factor", [P, IMAGES])
        sp_att = sb("a_sp_att", [SIDE, HALF])
        product = sb("a_product", [P, 2, HALF])
        kept = sb("a_kept", [P, 2, HALF])
        y4s = sb("a_y4s", [P, IMAGES, 16])
        pyr = sb("a_pyr", [P, 3, 16, IMAGES])
        y2h = sb("a_y2h", [P, 4, 2, IMAGES])
        y2 = sb("a_y2", [P, 2, 2, IMAGES])
        y1h = sb("a_y1h", [P, 2, IMAGES])
        w1 = sb("a_w1", [P, 27])
        w2 = sb("a_w2", [P, 9])
        z1 = sb("a_z1", [P, 4, IMAGES])
        z2 = sb("a_z2", [P, IMAGES])
        fc1 = sb("a_fc1", [P, SQUEEZED])
        fc2 = sb("a_fc2", [SQUEEZED, P])
        squeezed = sb("a_squeezed", [SQUEEZED, IMAGES])
        expo = sb("a_expo", [P, IMAGES])
        gate = sb("a_gate", [P, IMAGES])

        ps_small = ps("a_ps_small", [P, HALF])
        ps_maps = ps("a_ps_maps", [2 * IMAGES, HALF])
        ps_rows = ps("a_ps_rows", [SIDE, HALF])
        ps_big = ps("a_ps_big", [P, 2, HALF])
        map_dram = nc.dram_tensor("a_map", [2, IMAGES, PX], F32, kind="Internal").ap()

        x_in = [sem(f"a_x_in{t}") for t in range(TIME)]
        weights_in = sem("a_weights_in")
        const = sem("a_const")
        step = sem("a_step")
        moments = sem("a_moments")
        grouped = sem("a_grouped")
        variance = sem("a_variance")
        scale_step = sem("a_scale_step")
        xh_done = sem("a_xh_done")
        u_added = sem("a_u_added")
        spiked = sem("a_spiked")
        averaged = sem("a_averaged")
        att_sums = sem("a_att_sums")
        summed = sem("a_summed")
        maps_done = sem("a_maps_done")
        map_out = sem("a_map_out")
        rows_in = sem("a_rows_in")
        bands = sem("a_bands")
        rows_conv = sem("a_rows_conv")
        sp_done = sem("a_sp_done")
        spread = sem("a_spread")
        spread_used = sem("a_spread_used")
        kept_done = sem("a_kept_done")
        x_added = sem("a_x_added")
        pooled = sem("a_pooled")
        fc1_done = sem("a_fc1_done")
        relu_done = sem("a_relu_done")
        fc2_done = sem("a_fc2_done")
        exp_done = sem("a_exp_done")
        gated = sem("a_gated")
        flipped = sem("a_flipped")
        flip_used = sem("a_flip_used")
        passed = sem("a_passed")

        WEIGHTS = 7
        block = ctx.enter_context(nc.Block())

        @block.sync
        def _(sp):
            x_v = dram["x"].rearrange("(t i) c h w -> t c i (h w)", i=PER_STEP)
            for t in range(TIME):
                sp.dma_start(X[:, t * PER_STEP * PX:(t + 1) * PER_STEP * PX]
                             .rearrange("c (i p) -> c i p", p=PX), x_v[t]).then_inc(x_in[t], 16)
            sp.dma_start(w_ch[:], dram["L0_conv_w_channel"][0].broadcast_to([P, TAPS])).then_inc(weights_in, 16)
            sp.dma_start(w_t[:], dram["L0_conv_w_temporal"][0].broadcast_to([P, TAPS])).then_inc(weights_in, 16)
            w_sp_v = dram["L0_conv_w_spatial"].rearrange("a c h w -> a c (h w)")
            for c in range(2):
                sp.dma_start(w_sp[c * SIDE:(c + 1) * SIDE, :],
                             w_sp_v[:, c].broadcast_to([SIDE, TAPS * TAPS])).then_inc(weights_in, 16)
            sp.dma_start(w1[:], dram["L1_conv_w1"].rearrange("a c h w -> a (c h w)").broadcast_to([P, 27])
                         ).then_inc(weights_in, 16)
            sp.dma_start(w2[:], dram["L1_conv_w2"].rearrange("a c h w -> a (c h w)").broadcast_to([P, 9])
                         ).then_inc(weights_in, 16)
            with nc.allow_non_contiguous_dma("two small matrices, turned"):
                sp.dma_start(fc1[:], dram["L1_conv_fc1_w"].rearrange("r c -> c r")).then_inc(weights_in, 16)
                sp.dma_start(fc2[:], dram["L1_conv_fc2_w"].rearrange("c r -> r c")).then_inc(weights_in, 16)
            sp.wait_ge(maps_done, 2)
            sp.dma_start(map_dram.rearrange("m i (h p) -> (i h) m p", h=2), maps[:]).then_inc(map_out, 16)
            sp.wait_ge(map_out, 16)
            sp.wait_ge(const, 11)
            for m in range(2):
                sp.dma_start(rows[m * SIDE:(m + 1) * SIDE, :, 2:2 + SIDE],
                             map_dram[m].rearrange("i (y x) -> y i x", x=SIDE)).then_inc(rows_in, 16)

        @block.gpsimd
        def _(pool):
            steps = [0]

            def made(ins):
                steps[0] += 1
                ins.then_inc(const, 1)
                pool.wait_ge(const, steps[0])

            made(pool.memset(mhalf[:], -0.5))
            made(pool.memset(eps[:], EPS_G))
            made(pool.memset(zero[:], 0.0))
            made(pool.memset(ones[:], 1.0))
            made(pool.affine_select(out=near[:], in_=ones[:], compare_op=ALU.is_equal, fill=0.0, base=2,
                                    pattern=[[-1, TAPS], [-1, P]], channel_multiplier=1))
            for c in range(2):
                made(pool.affine_select(out=near_y[c * SIDE:(c + 1) * SIDE], in_=ones[c * SIDE:(c + 1) * SIDE, :, 0:SIDE],
                                        compare_op=ALU.is_equal, fill=0.0, base=2,
                                        pattern=[[-1, TAPS], [-1, SIDE]], channel_multiplier=1))
            made(pool.memset(group[:], 1.0 / CH_GROUP))
            gv = group[:].rearrange("p (g k) -> p g k", k=CH_GROUP)
            made(pool.affine_select(out=gv, in_=gv, compare_op=ALU.is_ge, fill=0.0, base=0,
                                    pattern=[[-CH_GROUP, P // CH_GROUP], [0, CH_GROUP]], channel_multiplier=1))
            made(pool.affine_select(out=gv, in_=gv, compare_op=ALU.is_ge, fill=0.0, base=CH_GROUP - 1,
                                    pattern=[[CH_GROUP, P // CH_GROUP], [0, CH_GROUP]], channel_multiplier=-1))
            made(pool.memset(rows[:], 0.0))
            made(pool.memset(times[:], 0.0))
            made(pool.memset(picks[:], 0.0))
            made(pool.memset(picks[:, 31:32], 1.0))
            made(pool.memset(mean_all[:], 1.0 / C))
            for norm in range(2):
                pool.wait_ge(variance, norm + 1)
                nc.gpsimd.tensor_tensor(tmp[:], tmp[:], eps[:], ALU.add).then_inc(scale_step, 1)
                pool.wait_ge(scale_step, 2 * norm + 1)
                nc.gpsimd.tensor_tensor(scale[:], tmp[:], mhalf[:], ALU.pow).then_inc(scale_step, 1)
                if norm == 0:
                    x_v = X[:].rearrange("c (i y x) -> c i (y x)", i=IMAGES, x=SIDE)
                    with pool.Fori(0, SIDE // 2) as pair:
                        for k in range(2):
                            y = 2 * pair + k
                            pool.wait_ge(kept_done, y + 1)
                            xs = x_v[:, :, ds(y * SIDE, SIDE)]
                            nc.gpsimd.tensor_tensor(xs, xs, kept[:, k].rearrange("c (i x) -> c i x", x=SIDE),
                                                    ALU.add).then_inc(x_added, 1)

        @block.vector
        def _(dve):
            count = [0]

            def link(ins):
                count[0] += 1
                ins.then_inc(step, 1)
                dve.wait_ge(step, count[0])

            def norm_scales(norm):
                link(nc.vector.tensor_copy(both[:, 0], mv[:, :, 0]))
                link(nc.vector.tensor_tensor(both[:, 1], mv[:, :, 0], mv[:, :, 0], ALU.mult))
                nc.vector.tensor_tensor(both[:, 1], both[:, 1], mv[:, :, 1], ALU.add).then_inc(moments, 1)
                dve.wait_ge(grouped, norm + 1)
                link(nc.vector.tensor_copy(shift[:], ps_small[:, 0:IMAGES]))
                link(nc.vector.tensor_tensor(tmp[:], shift[:], shift[:], ALU.mult))
                nc.vector.tensor_tensor(tmp[:], ps_small[:, IMAGES:2 * IMAGES], tmp[:], ALU.subtract
                                        ).then_inc(variance, 1)
                dve.wait_ge(scale_step, 2 * norm + 2)
                link(nc.vector.scalar_tensor_tensor(shift[:], shift[:], -1.0, scale[:], ALU.mult, ALU.mult))

            dve.wait_ge(weights_in, 16 * (WEIGHTS + 1))
            dve.wait_ge(const, 15)
            link(nc.vector.tensor_tensor(
                wide, near[:].rearrange("p k o -> p o k"),
                w_ch[:].rearrange("p (a k) -> p a k", a=1).broadcast_to([P, P, TAPS]), ALU.mult))
            link(nc.vector.tensor_reduce(band_ch[:], wide, AX.X, ALU.add))
            w_v = w_sp[:].rearrange("p (dy dx) -> p dx dy", dx=TAPS)
            for dx in range(TAPS):
                last = nc.vector.tensor_tensor(
                    wide_y[:, dx], near_y[:].rearrange("p k o -> p o k"),
                    w_v[:, dx:dx + 1, :].broadcast_to([2 * SIDE, SIDE, TAPS]), ALU.mult)
            link(last)
            nc.vector.tensor_reduce(band_sp[:], wide_y[:], AX.X, ALU.add).then_inc(bands, 1)

            for t in range(TIME):
                dve.wait_ge(x_in[t], 16)
                for i in range(t * PER_STEP, (t + 1) * PER_STEP):
                    for h in range(2):
                        last = nc.vector.bn_stats(stats[:, i, h], X[:, i * PX + h * HALF:i * PX + (h + 1) * HALF])
            link(last)
            for i in range(IMAGES):
                last = nc.vector.bn_aggr(mv[:, i], stats[:, i])
            link(last)
            norm_scales(0)
            nc.vector.tensor_copy(gate[:], scale[:]).then_inc(gated, 1)

            for t in range(TIME):
                dve.wait_ge(xh_done, PER_STEP * (t + 1))
                if t == 0:
                    nc.vector.tensor_copy(u[:], xh[:, 0]).then_inc(u_added, 1)
                else:
                    nc.vector.scalar_tensor_tensor(u[:], u[:], 0.5, xh[:, t % 2], ALU.mult, ALU.add
                                                   ).then_inc(u_added, 1)
                dve.wait_ge(u_added, t + 1)
                for k in range(PER_STEP):
                    i = t * PER_STEP + k
                    last = nc.vector.tensor_scalar(spikes[:, i * PX:(i + 1) * PX], u[:, k * PX:(k + 1) * PX],
                                                   1.0, 0.0, ALU.is_gt, ALU.add, accum_out=counts[:, i:i + 1])
                last.then_inc(spiked, 1)
                dve.wait_ge(spiked, t + 1)
                if t < TIME - 1:
                    link(nc.vector.tensor_tensor(
                        u[:], u[:], spikes[:, t * PER_STEP * PX:(t + 1) * PER_STEP * PX], ALU.subtract))

            nc.vector.tensor_scalar(average[:], counts[:], 1.0 / PX, None, ALU.mult).then_inc(averaged, 1)
            dve.wait_ge(summed, 1)
            nc.vector.tensor_scalar(maps[:, 0], ps_maps[:], 1.0 / C, None, ALU.mult).then_inc(maps_done, 1)
            nc.vector.tensor_scalar(maps[:, 1], ps_maps[:], 0.5, None, ALU.is_gt).then_inc(maps_done, 1)
            dve.wait_ge(att_sums, 1)
            link(nc.vector.tensor_copy(times[:, 2:2 + TIME, :],
                                       ps_small[:, 64:64 + IMAGES].rearrange("c (t b) -> c t b", b=PER_STEP)))
            for k in range(TAPS):
                window = times[:, k:k + TIME, :].rearrange("c t b -> c (t b)")
                if k == 0:
                    link(nc.vector.tensor_scalar(temporal[:], window, w_t[:, 0:1], None, ALU.mult))
                else:
                    link(nc.vector.scalar_tensor_tensor(temporal[:], window, w_t[:, k:k + 1], temporal[:],
                                                        ALU.mult, ALU.add))
            link(nc.vector.tensor_tensor(factor[:], temporal[:], ps_small[:, 96:96 + IMAGES], ALU.mult))
            dve.wait_ge(rows_conv, 1)
            nc.vector.tensor_copy(sp_att[:], ps_rows[:]).then_inc(sp_done, 1)

            s_v = spikes[:].rearrange("c (i p) -> c i p", i=IMAGES)
            f_v = factor[:].rearrange("c (i a) -> c i a", a=1).broadcast_to([P, IMAGES, SIDE])

            def keep_row(y, k, first):
                if not first:
                    dve.wait_ge(kept_done, y - 1)
                dve.wait_ge(spread, y + 1)
                nc.vector.tensor_tensor(product[:, k].rearrange("c (i x) -> c i x", x=SIDE),
                                        ps_big[:, k].rearrange("c (i x) -> c i x", x=SIDE), f_v,
                                        ALU.mult).then_inc(spread_used, 1)
                if not first:
                    dve.wait_ge(x_added, y - 1)
                dve.wait_ge(spread_used, y + 1)
                nc.vector.scalar_tensor_tensor(kept[:, k].rearrange("c (i x) -> c i x", x=SIDE),
                                               product[:, k].rearrange("c (i x) -> c i x", x=SIDE), 0.0,
                                               s_v[:, :, ds(y * SIDE, SIDE)], ALU.is_ge, ALU.mult
                                               ).then_inc(kept_done, 1)

            for y in range(2):
                keep_row(y, y, True)
            with dve.Fori(1, SIDE // 2) as pair:
                for k in range(2):
                    keep_row(2 * pair + k, k, False)
            dve.wait_ge(x_added, SIDE)

            with dve.Fori(0, IMAGES) as i:
                for h in range(2):
                    nc.vector.bn_stats(stats[:, ds(i, 1), h].rearrange("c a s -> c (a s)"),
                                       X[:, ds(i * PX + h * HALF, HALF)])
            link(nc.vector.tensor_reduce(strips, X[:].rearrange("c (s e) -> c s e", e=8), AX.X, ALU.add))
            for i in range(IMAGES):
                last = nc.vector.bn_aggr(mv[:, i], stats[:, i])
            link(last)
            sv = strips.rearrange("c (i b y x) -> c (i b) x y", b=4, y=8, x=4)
            link(nc.vector.tensor_reduce(y4s[:].rearrange("c i (b x) -> c (i b) x", x=4), sv, AX.X, ALU.add))
            norm_scales(1)
            sc = scale[:].rearrange("c (a i) -> c a i", a=1).broadcast_to([P, 16, IMAGES])
            sh = shift[:].rearrange("c (a i) -> c a i", a=1).broadcast_to([P, 16, IMAGES])
            link(nc.vector.scalar_tensor_tensor(pyr[:, 2], y4s[:].rearrange("c i q -> c q i"), 1.0 / 64, sc,
                                                ALU.mult, ALU.mult))
            link(nc.vector.tensor_tensor(pyr[:, 2], pyr[:, 2], sh, ALU.add))
            cells = pyr[:, 2].rearrange("c (y x) i -> c y x i", x=4)
            for x in range(2):
                last = nc.vector.tensor_tensor(y2h[:, :, x], cells[:, :, 2 * x], cells[:, :, 2 * x + 1], ALU.add)
            link(last)
            for y in range(2):
                last = nc.vector.tensor_tensor(y2[:, y], y2h[:, 2 * y], y2h[:, 2 * y + 1], ALU.add)
            link(last)
            link(nc.vector.tensor_tensor(y1h[:], y2[:, 0], y2[:, 1], ALU.add))
            link(nc.vector.tensor_tensor(tmp[:], y1h[:, 0], y1h[:, 1], ALU.add))
            link(nc.vector.tensor_scalar(pyr[:, 0], tmp[:].rearrange("c (a i) -> c a i", a=1)
                                         .broadcast_to([P, 16, IMAGES]), 1.0 / 16, None, ALU.mult))
            twos = pyr[:, 1].rearrange("c (y x) i -> c y x i", x=4)
            for y in range(4):
                for x in range(2):
                    last = nc.vector.tensor_scalar(
                        twos[:, y, 2 * x:2 * x + 2],
                        y2[:, y // 2, x:x + 1].broadcast_to([P, 2, IMAGES]), 0.25, None, ALU.mult)
            link(last)
            z_v = z1[:].rearrange("c (y x) i -> c y (x i)", x=2)
            for n in range(27):
                m, a, b = n // 9, n // 3 % 3, n % 3
                window = (pyr[:, m].rearrange("c (y x) i -> c y (x i)", x=4)
                          [:, a:a + 2, b * IMAGES:(b + 2) * IMAGES])
                if n == 0:
                    link(nc.vector.tensor_scalar(z_v, window, w1[:, 0:1], None, ALU.mult))
                else:
                    link(nc.vector.scalar_tensor_tensor(z_v, window, w1[:, n:n + 1], z_v, ALU.mult, ALU.add))
            for n in range(4):
                w = w2[:, 3 * (1 + n // 2) + 1 + n % 2:][:, 0:1]
                if n == 0:
                    ins = nc.vector.tensor_scalar(z2[:], z1[:, 0], w, None, ALU.mult)
                else:
                    ins = nc.vector.scalar_tensor_tensor(z2[:], z1[:, n], w, z2[:], ALU.mult, ALU.add)
                if n < 3:
                    link(ins)
            ins.then_inc(pooled, 1)
            dve.wait_ge(fc1_done, 1)
            nc.vector.tensor_scalar(squeezed[:], ps_small[0:SQUEEZED, 128:128 + IMAGES], 0.0, None, ALU.max
                                    ).then_inc(relu_done, 1)
            dve.wait_ge(exp_done, 1)
            link(nc.vector.tensor_scalar(expo[:], expo[:], 1.0, None, ALU.add))
            link(nc.vector.reciprocal(gate[:], expo[:]))
            link(nc.vector.tensor_tensor(scale[:], scale[:], gate[:], ALU.mult))
            link(nc.vector.tensor_scalar(scale[:], scale[:], 1.0, None, ALU.add))
            nc.vector.tensor_tensor(shift[:], shift[:], gate[:], ALU.mult).then_inc(gated, 1)
            dve.wait_ge(gated, 2)
            with dve.Fori(0, IMAGES) as i:
                xs = X[:, ds(i * PX, PX)]
                nc.vector.tensor_scalar(xs, xs, scale[:, ds(i, 1)], shift[:, ds(i, 1)], ALU.mult, ALU.add
                                        ).then_inc(kept_done, 1)

        @block.scalar
        def _(act):
            act.wait_ge(gated, 1)
            for t in range(TIME):
                if t >= 2:
                    act.wait_ge(u_added, t - 1)
                for k in range(PER_STEP):
                    i = t * PER_STEP + k
                    nc.scalar.activation(xh[:, t % 2, k * PX:(k + 1) * PX], X[:, i * PX:(i + 1) * PX], ACT.Identity,
                                         scale=scale[:, i:i + 1], bias=shift[:, i:i + 1]).then_inc(xh_done, 1)
            act.wait_ge(fc2_done, 1)
            nc.scalar.activation(expo[:], ps_small[:, 160:160 + IMAGES], ACT.Exp, scale=-1.0).then_inc(exp_done, 1)
            with act.Fori(0, IMAGES) as i:
                for h in range(2):
                    act.wait_ge(flipped, 2 * i + h + 1)
                    nc.scalar.activation(T[:, ds(i * PX + h * HALF, HALF)], ps_big[:, h], ACT.Copy
                                         ).then_inc(flip_used, 1)

        @block.tensor
        def _(pe):
            pe.wait_ge(const, 15)
            pe.wait_ge(moments, 1)
            nc.tensor.matmul(ps_small[:, 0:2 * IMAGES], group[:], both[:].rearrange("p a i -> p (a i)"),
                             start=True, stop=True).then_inc(grouped, 1)
            for n in range(2 * IMAGES):
                if n % (2 * PER_STEP) == 0:
                    pe.wait_ge(spiked, n // (2 * PER_STEP) + 1)
                last = nc.tensor.matmul(ps_maps[:], picks[:, 31 - n:63 - n],
                                        spikes[:, n * HALF:(n + 1) * HALF],
                                        start=(n == 0), stop=(n == 2 * IMAGES - 1))
            last.then_inc(summed, 1)
            pe.wait_ge(averaged, 1)
            pe.wait_ge(bands, 1)
            nc.tensor.matmul(ps_small[:, 64:64 + IMAGES], mean_all[:], average[:], start=True, stop=True)
            nc.tensor.matmul(ps_small[:, 96:96 + IMAGES], band_ch[:], average[:], start=True, stop=True
                             ).then_inc(att_sums, 1)
            pe.wait_ge(rows_in, 32)
            for dx in range(TAPS):
                last = nc.tensor.matmul(ps_rows[:], band_sp[:, dx], rows[:, :, dx:dx + SIDE],
                                        start=(dx == 0), stop=(dx == TAPS - 1))
            last.then_inc(rows_conv, 1)
            pe.wait_ge(sp_done, 1)

            def spread_row(y):
                nc.tensor.matmul(ps_big[:, y % 2], ident[0:SIDE, y:y + 1].broadcast_to([SIDE, P]), sp_att[:],
                                 start=True, stop=True).then_inc(spread, 1)

            for y in range(SIDE):
                if y >= 2:
                    pe.wait_ge(spread_used, y - 1)
                spread_row(y)
            pe.wait_ge(moments, 2)
            nc.tensor.matmul(ps_small[:, 0:2 * IMAGES], group[:], both[:].rearrange("p a i -> p (a i)"),
                             start=True, stop=True).then_inc(grouped, 1)
            pe.wait_ge(pooled, 1)
            nc.tensor.matmul(ps_small[0:SQUEEZED, 128:128 + IMAGES], fc1[:], z2[:], start=True, stop=True
                             ).then_inc(fc1_done, 1)
            pe.wait_ge(relu_done, 1)
            nc.tensor.matmul(ps_small[:, 160:160 + IMAGES], fc2[:], squeezed[:], start=True, stop=True
                             ).then_inc(fc2_done, 1)

            for i in range(IMAGES):
                pe.wait_ge(kept_done, SIDE + i + 1)
                for h in range(2):
                    if i:
                        pe.wait_ge(flip_used, 2 * i + h - 1)
                    for j in range(4):
                        c = i * PX + h * HALF + j * P
                        last = nc.tensor.transpose(ps_big[:, h, j * P:(j + 1) * P], X[:, c:c + P], ident[:])
                    last.then_inc(flipped, 1)


HEADS = 8
KV = 2
GROUP = HEADS // KV
DK = 16
STACK = 6 * DK
SPLIT_Q = (0, 0, 1, 0, 1, 2)
SPLIT_K = (0, 1, 0, 2, 1, 0)
STEPS = KV * 2 * TILES
MAXES = GROUP * TILES
MAX_PER_STEP = 5
FINISH_FILLS = {"wo0": 0, "wo1": 1, "x20": 10, "x21": 11, "logits": 12}
PREPARE_FILLS = {"xt0": 2, "xt1": 3, "q0": 4, "q1": 5, "k0": 6, "k1": 7, "v": 8, "mt0": 30}
OWN_FILLS = {"mt1": 14}
USES = len(FINISH_FILLS) + len(PREPARE_FILLS) + len(OWN_FILLS)


def attention_stage(nc, T, xT_dram, gates, ident, dram):
    with ExitStack() as ctx:
        sb, ps, sem = allocator(nc, ctx)
        wq = sb("b_wq", [P, C])
        wk = sb("b_wk", [P, KV * DK])
        wv = sb("b_wv", [P, KV * DK])
        wo = sb("b_wo", [P, KV, C])
        wg = sb("b_wg", [P, E])
        bg = sb("b_bg", [P, E])
        iota = sb("b_iota", [P, E])
        eps = sb("b_eps", [P, TILES])
        zero = sb("b_zero", [P, TILES])
        mhalf = sb("b_mhalf", [P, TILES])
        stats = [sb(f"b_stats{k}", [P, TILES, 6]) for k in range(2)]
        mv = [sb(f"b_mv{k}", [P, TILES, 2]) for k in range(2)]
        shift = [sb(f"b_shift{k}", [P, TILES]) for k in range(2)]
        rstd = [sb(f"b_rstd{k}", [P, TILES]) for k in range(2)]
        xn = [sb(f"b_xn{k}", [P, PX]) for k in range(2)]
        xT = [sb(f"b_xT{k}", [P, PX]) for k in range(2)]
        q_parts = sb("b_qparts", [P, 3, PX], BF16)
        k_parts = sb("b_kparts", [KV * DK, 3, PX], BF16)
        rest = sb("b_rest", [P, 2, HALF])
        qs = sb("b_qs", [P, 2, HEADS * PX], BF16)
        ks = sb("b_ks", [P, 2, KV * PX], BF16)
        vs = sb("b_vs", [P, 2, TILES, KV, 2 * DK])
        half_max = sb("b_halfmax", [P, MAXES, 2])
        maxes = sb("b_maxes", [P, MAXES])
        m_parts = sb("b_mparts", [MAXES, 3, P], BF16)
        m_rest = sb("b_mrest", [MAXES, P])
        m_rest2 = sb("b_mrest2", [MAXES, P])
        probs = sb("b_probs", [P, 2, 2 * 2 * HALF])
        o_flip = sb("b_oflip", [P, HALF])
        o_scale = sb("b_oscale", [P, HALF // (2 * DK)])
        o_norm = sb("b_onorm", [P, KV, PX])
        logits = sb("b_logits", [P, TILES, E])
        top = sb("b_top", [P, TILES, 8])
        top_at = sb("b_topat", [P, TILES, 8], U32)
        top_atf = sb("b_topatf", [P, TILES, 2])
        gap = sb("b_gap", [P, TILES])
        expo = sb("b_expo", [P, TILES])
        gsum = sb("b_gsum", [P, TILES])
        w1 = sb("b_w1", [P, TILES])
        w2 = sb("b_w2", [P, TILES])
        hit = sb("b_hit", [P, 2, TILES, E])

        ps_s = ps("b_ps_s", [P, 2, 2 * HALF])
        ps_m = ps("b_ps_m", [P, 2, HALF])
        ps_o = ps("b_ps_o", [P, HALF])
        ps_x = ps("b_ps_x", [P, HALF])

        q_dram = nc.dram_tensor("b_q_parts", [2, 3, P, PX], BF16, kind="Internal").ap()
        k_dram = nc.dram_tensor("b_k_parts", [2, 3, KV * DK, PX], BF16, kind="Internal").ap()
        m_dram = nc.dram_tensor("b_m_parts", [2, 3, HEADS * PX], BF16, kind="Internal").ap()

        loaded = sem("b_loaded")
        wo_loaded = sem("b_wo_loaded")
        const = sem("b_const")
        passed = sem("b_passed")
        wo_zero = sem("b_wo_zero")
        stats_done = [sem(f"b_stats_done{k}") for k in range(2)]
        mv_done = [sem(f"b_mv_done{k}") for k in range(2)]
        rstd_done = [sem(f"b_rstd_done{k}") for k in range(2)]
        xn_done = [sem(f"b_xn_done{k}") for k in range(2)]
        xn_used = [sem(f"b_xn_used{k}") for k in range(2)]
        x_ready = sem("b_x_ready")
        x_free = sem("b_x_free")
        part1_done = sem("b_part1")
        rest_done = sem("b_rest_done")
        part2_done = sem("b_part2")
        part3_done = sem("b_part3")
        stacked = sem("b_stacked")
        spilled = sem("b_spilled")
        m_spilled = sem("b_m_spilled")
        v_done = sem("b_v_done")
        m_ready = sem("b_m_ready")
        m_free = sem("b_m_free")
        maxes_done = sem("b_maxes_done")
        mp_step = sem("b_mp_step")
        m_rows = sem("b_m_rows")
        s_ready = sem("b_s_ready")
        exp_done = sem("b_exp_done")
        pv_done = sem("b_pv_done")
        o_free = sem("b_o_free")
        o_done = sem("b_o_done")
        o_step = sem("b_o_step")
        t_added = sem("b_t_added")
        xT_copied = sem("b_xT_copied")
        g_step = sem("b_g_step")
        gap_exp = sem("b_gap_exp")

        def uses(n):
            finish, prepare, steps = parts_of(n)
            fills = FINISH_FILLS if finish else {}
            fills = fills | (PREPARE_FILLS if prepare else {}) | (OWN_FILLS if steps else {})
            ahead = len(PREPARE_FILLS)
            if isinstance(n, int) and n < 0:
                start = 0
            elif isinstance(n, int) and n == 0:
                start = ahead
            elif isinstance(n, int) and n == IMAGES:
                start = (n - 1) * USES + ahead + len(OWN_FILLS)
            else:
                start = (n - 1) * USES + 2 * ahead + len(OWN_FILLS)
            return start, fills

        def use(n, name):
            start, fills = uses(n)
            return start + sorted(fills, key=fills.get).index(name)

        def filled_at(n, s):
            return [name for name, step in uses(n)[1].items() if step == s]

        def positive(eng, s, value):
            if not (isinstance(value, int) and value <= 0):
                eng.wait_ge(s, value)

        def images(eng, body):
            body(-1, 1)
            body(0, 0)
            with eng.Fori(0, IMAGES // 2 - 1) as pair:
                body(2 * pair + 1, 1)
                body(2 * pair + 2, 0)
            body(IMAGES - 1, 1)
            body(IMAGES, 0)

        def parts_of(n):
            finish, prepare, steps = True, True, True
            if isinstance(n, int):
                finish, prepare, steps = n >= 1, n < IMAGES - 1, 0 <= n < IMAGES
            return finish, prepare, steps

        def max_units(n, s):
            prepare, steps = parts_of(n)[1:]
            if not steps:
                return [(n + 1, 0, u) for u in range(2 * MAXES)] if prepare and s == STEPS // 2 + 1 else []
            later = s >= STEPS // 2
            if later and not prepare:
                return []
            a = (s % (STEPS // 2) - 1) * MAX_PER_STEP
            units = range(max(a, 0), min(max(a + MAX_PER_STEP, 0), 2 * MAXES))
            return [(n + 1 if later else n, 0 if later else 1, u) for u in units]

        block = ctx.enter_context(nc.Block())

        @block.sync
        def _(sp):
            sp.dma_start(wq[:], dram["L2_attn_Wq"]).then_inc(loaded, 16)
            sp.dma_start(wk[:], dram["L2_attn_Wk"]).then_inc(loaded, 16)
            sp.dma_start(wv[:], dram["L2_attn_Wv"]).then_inc(loaded, 16)
            sp.dma_start(wg[:], dram["L2_ffn_Wg"]).then_inc(loaded, 16)
            sp.dma_start(bg[:], dram["L2_ffn_bg"].rearrange("(a e) -> a e", a=1)
                         .broadcast_to([P, E])).then_inc(loaded, 16)
            sp.wait_ge(wo_zero, 1)
            wo_rows = dram["L2_attn_Wo"].rearrange("(h e) n -> h e n", e=DK)
            for h in range(HEADS):
                j = h % GROUP
                sp.dma_start(wo[32 * j:32 * j + DK, h // GROUP, :], wo_rows[h]).then_inc(wo_loaded, 16)

            def place_maxima(m, kv, buffer):
                n = 2 * m + kv
                cols = slice(kv * GROUP * PX, (kv + 1) * GROUP * PX)
                sp.wait_ge(mp_step, 5 * n + 5)
                sp.dma_start(m_dram[buffer, :, cols].rearrange("s (r q) -> r s q", q=P), m_parts[:]
                             ).then_inc(m_spilled, 16)
                sp.wait_ge(m_spilled, 16 * n + 16)
                sp.dma_start(qs[STACK:STACK + 3, buffer, cols], m_dram[buffer, :, cols]).then_inc(m_rows, 16)

            def body(n, parity):
                finish, prepare, steps = parts_of(n)
                m = n + 1
                other = 1 - parity
                if prepare:
                    sp.wait_ge(part3_done, 4 * m + 2)
                    sp.dma_start(q_dram[other].rearrange("s p t -> p s t"), q_parts[:]).then_inc(spilled, 16)
                    sp.wait_ge(part3_done, 4 * m + 4)
                    sp.dma_start(k_dram[other].rearrange("s p t -> p s t"), k_parts[:]).then_inc(spilled, 16)
                    sp.wait_ge(spilled, 32 * m + 32)
                    for g, part in enumerate(SPLIT_Q):
                        sp.dma_start(
                            qs[DK * g:DK * g + DK, other, :].rearrange("d (h t) -> d h t", h=HEADS),
                            q_dram[other, part].rearrange("(h d) t -> d h t", d=DK),
                        ).then_inc(stacked, 16)
                    for g, part in enumerate(SPLIT_K):
                        sp.dma_start(
                            ks[DK * g:DK * g + DK, other, :].rearrange("d (h t) -> d h t", h=KV),
                            k_dram[other, part].rearrange("(h d) t -> d h t", d=DK),
                        ).then_inc(stacked, 16)
                if finish:
                    sp.wait_ge(x_free, use(n, "x21") + 1)
                    sp.dma_start(xT_dram[:, ds((n - 1) * PX, PX)], xT[1][:]).then_inc(xT_copied, 16)
                if steps:
                    place_maxima(n, 1, parity)
                if prepare:
                    place_maxima(m, 0, other)

            images(sp, body)
            sp.wait_ge(xT_copied, 16 * IMAGES)

        @block.gpsimd
        def _(pool):
            pool.memset(wo[:], 0.0).then_inc(wo_zero, 1)
            pool.memset(mhalf[:], -0.5).then_inc(const, 1)
            pool.memset(eps[:], EPS_T).then_inc(const, 1)
            pool.memset(zero[:], 0.0).then_inc(const, 1)
            pool.memset(vs[:], 1.0).then_inc(const, 1)
            pool.wait_ge(const, 4)
            pool.memset(ks[STACK:P, :, :], 1.0).then_inc(const, 1)
            pool.wait_ge(const, 5)
            pool.iota(iota[:], [[1, E]], base=0, channel_multiplier=0,
                      allow_small_or_imprecise_dtypes=True).then_inc(const, 1)

            def scales(m, k):
                wait_apart(pool, mv_done[k], m + 1, passed)
                positive(pool, xn_done[k], TILES * m)
                nc.gpsimd.tensor_tensor(rstd[k][:], mv[k][:, :, 1], eps[:], ALU.add).then_inc(rstd_done[k], 1)
                pool.wait_ge(rstd_done[k], 4 * m + 1)
                nc.gpsimd.tensor_tensor(rstd[k][:], rstd[k][:], mhalf[:], ALU.pow).then_inc(rstd_done[k], 1)
                pool.wait_ge(rstd_done[k], 4 * m + 2)
                nc.gpsimd.tensor_tensor(shift[k][:], mv[k][:, :, 0], rstd[k][:], ALU.mult).then_inc(rstd_done[k], 1)
                pool.wait_ge(rstd_done[k], 4 * m + 3)
                nc.gpsimd.tensor_tensor(shift[k][:], zero[:], shift[k][:], ALU.subtract).then_inc(rstd_done[k], 1)

            def part_three(dst, rows, m, k, half):
                n = 4 * m + 2 * k + half
                cols = slice(half * HALF, half * HALF + HALF)
                wait_apart(pool, part2_done, n + 1, passed)
                nc.gpsimd.tensor_tensor(dst[:, 2, cols], rest[0:rows, half, :], dst[:, 1, cols],
                                        ALU.subtract).then_inc(part3_done, 1)

            def body(n, parity):
                finish, prepare, steps = parts_of(n)
                if prepare:
                    scales(n + 1, 0)
                if finish:
                    scales(n - 1, 1)
                if prepare:
                    for k, dst, rows in ((0, q_parts, P), (1, k_parts, KV * DK)):
                        for half in range(2):
                            part_three(dst, rows, n + 1, k, half)
            pool.wait_ge(const, 6)
            images(pool, body)

        @block.vector
        def _(dve):
            def statistics(m, k):
                for j in range(TILES):
                    last = nc.vector.bn_stats(stats[k][:, j, :], T[:, ds(m * PX + j * P, P)])
                last.then_inc(stats_done[k], 1)
                positive(dve, xn_done[k], TILES * m)
                wait_apart(dve, stats_done[k], m + 1, passed)
                for j in range(TILES):
                    last = nc.vector.bn_aggr(mv[k][:, j, :], stats[k][:, j, :])
                last.then_inc(mv_done[k], 1)

            def left_over(dst, rows, m, k, half, n, name, scale):
                at = 4 * m + 2 * k + half
                dve.wait_ge(part1_done, at + 1)
                positive(dve, part3_done, at - 1)
                nc.vector.scalar_tensor_tensor(
                    rest[0:rows, half, :], ps_x[0:rows, :], scale,
                    dst[:, 0, half * HALF:half * HALF + HALF], ALU.mult, ALU.subtract,
                ).then_inc(rest_done, 1)
                dve.wait_ge(rest_done, at + 1)
                dve.sem_inc(x_free, 1)
                nc.vector.tensor_copy(dst[:, 1, half * HALF:half * HALF + HALF], rest[0:rows, half, :]
                                      ).then_inc(part2_done, 1)

            def reduce_unit(m, kv, u):
                wait_at = m * (4 * MAXES) + kv * 2 * MAXES + u
                dve.wait_ge(m_ready, wait_at + 1)
                nc.vector.tensor_reduce(half_max[:, u // 2, u % 2:u % 2 + 1], ps_m[:, u % 2, :], AX.X,
                                        ALU.max).then_inc(m_free, 1)

            def out_of(n, g):
                kv, half = g // 2, g % 2
                dve.wait_ge(pv_done, STEPS * n + TILES * (g + 1))
                positive(dve, o_done, 4 * n + g)
                nc.vector.transpose(o_flip[:], ps_o[:]).then_inc(o_free, 1)
                dve.wait_ge(o_free, 4 * n + g + 1)
                block = o_flip[:].rearrange("p (b r) -> p b r", r=2 * DK)
                nc.vector.reciprocal(o_scale[:], block[:, :, DK]).then_inc(o_step, 1)
                dve.wait_ge(o_step, 8 * n + 2 * g + 1)
                nc.vector.tensor_tensor(
                    block, block, o_scale[:].rearrange("p (b a) -> p b a", a=1)
                    .broadcast_to([P, HALF // (2 * DK), 2 * DK]), ALU.mult).then_inc(o_step, 1)
                dve.wait_ge(o_step, 8 * n + 2 * g + 2)
                nc.vector.transpose(o_norm[:, kv, half * HALF:half * HALF + HALF], o_flip[:]).then_inc(o_done, 1)

            def add_out(n, half):
                dve.wait_ge(x_ready, use(n, f"wo{half}") + 1)
                tt = T[:, ds((n - 1) * PX + half * HALF, HALF)]
                nc.vector.tensor_tensor(tt, tt, ps_x[:], ALU.add).then_inc(t_added, 1)
                dve.wait_ge(t_added, 2 * (n - 1) + half + 1)
                dve.sem_inc(x_free, 1)

            def gate(n):
                m = n - 1
                g0 = 9 * m
                dve.wait_ge(x_ready, use(n, "logits") + 1)
                nc.vector.tensor_tensor(
                    logits[:], ps_x[:, 0:TILES * E].rearrange("p (t e) -> p t e", e=E),
                    bg[:].rearrange("p (a e) -> p a e", a=1).broadcast_to([P, TILES, E]),
                    ALU.add).then_inc(g_step, 1)
                dve.wait_ge(g_step, g0 + 1)
                dve.sem_inc(x_free, 1)
                for j in range(TILES):
                    last = nc.vector.max(top[:, j, :], logits[:, j, :])
                last.then_inc(g_step, 1)
                dve.wait_ge(g_step, g0 + 2)
                nc.vector.tensor_tensor(gap[:], top[:, :, 1], top[:, :, 0], ALU.subtract).then_inc(g_step, 1)
                for j in range(TILES):
                    last = nc.vector.max_index(top_at[:, j, :], top[:, j, :], logits[:, j, :])
                last.then_inc(g_step, 1)
                dve.wait_ge(g_step, g0 + 4)
                nc.vector.tensor_copy(top_atf[:], top_at[:, :, 0:2]).then_inc(g_step, 1)
                dve.wait_ge(gap_exp, m + 1)
                nc.vector.tensor_scalar(gsum[:], expo[:], 1.0, None, ALU.add).then_inc(g_step, 1)
                dve.wait_ge(g_step, g0 + 6)
                nc.vector.reciprocal(w1[:], gsum[:]).then_inc(g_step, 1)
                for k in range(2):
                    nc.vector.tensor_tensor(
                        hit[:, k], iota[:].rearrange("p (a e) -> p a e", a=1).broadcast_to([P, TILES, E]),
                        top_atf[:, :, k:k + 1].broadcast_to([P, TILES, E]), ALU.is_equal)
                dve.wait_ge(g_step, g0 + 7)
                nc.vector.tensor_tensor(w2[:], w1[:], expo[:], ALU.mult).then_inc(g_step, 1)
                dve.wait_ge(g_step, g0 + 8)
                for k, w in ((0, w1), (1, w2)):
                    last = nc.vector.tensor_tensor(
                        hit[:, k], hit[:, k],
                        w[:].rearrange("p (t a) -> p t a", a=1).broadcast_to([P, TILES, E]), ALU.mult)
                last.then_inc(g_step, 1)
                dve.wait_ge(g_step, g0 + 9)
                nc.vector.tensor_tensor(
                    gates[:, ds(m * TILES * E, TILES * E)],
                    hit[:, 0].rearrange("p t e -> p (t e)"), hit[:, 1].rearrange("p t e -> p (t e)"), ALU.add)

            def minus_maxima(n, m, kv):
                g0 = 5 * (2 * m + kv)
                dve.wait_ge(x_ready, use(n, f"mt{kv}") + 1)
                positive(dve, m_rows, 16 * (2 * m + kv))
                nc.vector.tensor_scalar(m_parts[:, 0, :], ps_x[0:MAXES, 0:P], -1.0, None,
                                        ALU.mult).then_inc(mp_step, 1)
                dve.wait_ge(mp_step, g0 + 1)
                nc.vector.scalar_tensor_tensor(m_rest[:], ps_x[0:MAXES, 0:P], -1.0, m_parts[:, 0, :],
                                               ALU.mult, ALU.subtract).then_inc(mp_step, 1)
                dve.wait_ge(mp_step, g0 + 2)
                dve.sem_inc(x_free, 1)
                nc.vector.tensor_copy(m_parts[:, 1, :], m_rest[:]).then_inc(mp_step, 1)
                dve.wait_ge(mp_step, g0 + 3)
                nc.vector.tensor_tensor(m_rest2[:], m_rest[:], m_parts[:, 1, :], ALU.subtract).then_inc(mp_step, 1)
                dve.wait_ge(mp_step, g0 + 4)
                nc.vector.tensor_copy(m_parts[:, 2, :], m_rest2[:]).then_inc(mp_step, 1)

            def whole_maxima(m, kv):
                dve.wait_ge(m_free, m * (4 * MAXES) + (kv + 1) * 2 * MAXES)
                nc.vector.tensor_tensor(maxes[:], half_max[:, :, 0], half_max[:, :, 1],
                                        ALU.max).then_inc(maxes_done, 1)

            def read_out(n, name):
                m = n + 1
                if name[:2] == "wo":
                    add_out(n, int(name[2]))
                elif name[0] == "q":
                    left_over(q_parts, P, m, 0, int(name[1]), n, name, DK ** -0.5)
                elif name[0] == "k":
                    left_over(k_parts, KV * DK, m, 1, int(name[1]), n, name, 1.0)
                elif name == "logits":
                    gate(n)

            def body(n, parity):
                finish, prepare, steps = parts_of(n)
                m = n + 1
                if prepare:
                    statistics(m, 0)
                for s in range(STEPS + 1):
                    if s < STEPS:
                        for name in filled_at(n, s - 1):
                            read_out(n, name)
                    if s == 2 and finish:
                        statistics(n - 1, 1)
                    for unit in max_units(n, s) if s < STEPS else ():
                        reduce_unit(*unit)
                    if steps and s and s % TILES == 0:
                        out_of(n, s // TILES - 1)
                    if s == STEPS:
                        break
                    for name in filled_at(n, s):
                        if name == "mt1":
                            whole_maxima(n, 1)
                            minus_maxima(n, n, 1)
                        if name == "mt0":
                            whole_maxima(m, 0)
                            minus_maxima(n, m, 0)

            dve.wait_ge(loaded, 16 * 5)
            dve.wait_ge(const, 6)
            images(dve, body)

        @block.scalar
        def _(act):
            def evacuate(n, name, dst):
                u = use(n, name)
                act.wait_ge(x_ready, u + 1)
                nc.scalar.activation(dst, ps_x[:], ACT.Copy).then_inc(x_free, 1)

            def normalise(m, k, half):
                if half == 0:
                    act.wait_ge(rstd_done[k], 4 * m + 4)
                    positive(act, xn_used[k], m)
                for j in range(half * TILES // 2, (half + 1) * TILES // 2):
                    nc.scalar.activation(xn[k][:, j * P:(j + 1) * P], T[:, ds(m * PX + j * P, P)], ACT.Identity,
                                         scale=rstd[k][:, j:j + 1], bias=shift[k][:, j:j + 1],
                                         ).then_inc(xn_done[k], 1)

            def part_one(dst, rows, m, k, half, n, name, scale):
                act.wait_ge(x_ready, use(n, name) + 1)
                positive(act, stacked, 192 * m)
                nc.scalar.activation(dst[:, 0, half * HALF:half * HALF + HALF], ps_x[0:rows, :], ACT.Copy,
                                     scale=scale).then_inc(part1_done, 1)

            def read_out(n, name, other):
                m = n + 1
                if name[:2] == "xt":
                    half = int(name[2])
                    evacuate(n, name, xT[0][:, half * HALF:half * HALF + HALF])
                elif name[:2] == "x2":
                    half = int(name[2])
                    if half == 0:
                        positive(act, xT_copied, 16 * (n - 1))
                    evacuate(n, name, xT[1][:, half * HALF:half * HALF + HALF])
                elif name[0] == "q":
                    part_one(q_parts, P, m, 0, int(name[1]), n, name, DK ** -0.5)
                elif name[0] == "k":
                    part_one(k_parts, KV * DK, m, 1, int(name[1]), n, name, 1.0)
                elif name == "v":
                    act.wait_ge(x_ready, use(n, "v") + 1)
                    nc.scalar.activation(
                        vs[:, other, :, :, 0:DK],
                        ps_x[:, 0:TILES * KV * DK].rearrange("p (t k d) -> p t k d", k=KV, d=DK),
                        ACT.Copy).then_inc(v_done, 1)
                    act.wait_ge(v_done, m + 1)
                    act.sem_inc(x_free, 1)

            def body(n, parity):
                finish, prepare, steps = parts_of(n)
                m = n + 1
                for s in range(STEPS):
                    for name in filled_at(n, s - 1):
                        read_out(n, name, 1 - parity)
                    for at, there, image, k in ((1, prepare, m, 0), (8, finish, n - 1, 1)):
                        if there and s in (at, at + 1):
                            normalise(image, k, s - at)
                    if s == FINISH_FILLS["logits"] + 2 and finish:
                        act.wait_ge(g_step, 9 * (n - 1) + 3)
                        nc.scalar.activation(expo[:], gap[:], ACT.Exp).then_inc(gap_exp, 1)
                    if steps:
                        for pair in range(2):
                            v = 2 * s + pair
                            act.wait_ge(s_ready, 2 * STEPS * n + v + 1)
                            positive(act, pv_done, STEPS * n + s - 1)
                            nc.scalar.activation(
                                probs[:, s % 2, pair * 2 * HALF:(pair + 1) * 2 * HALF], ps_s[:, pair, :],
                                ACT.Exp).then_inc(exp_done, 1)

            act.wait_ge(const, 6)
            images(act, body)

        @block.tensor
        def _(pe):
            def fill(n, name):
                positive(pe, x_free, use(n, name))

            def transposes(n, m, k, name, half):
                pe.wait_ge(xn_done[k], TILES * m + 4 * (half + 1))
                fill(n, name)
                for j in range(4):
                    c = half * HALF + j * P
                    last = nc.tensor.transpose(ps_x[:, j * P:(j + 1) * P], xn[k][:, c:c + P], ident[:])
                last.then_inc(x_ready, 1)
                if half:
                    pe.wait_ge(x_ready, use(n, name) + 1)
                    pe.sem_inc(xn_used[k], 1)

            def project(n, w, rows, name, half):
                fill(n, name)
                nc.tensor.matmul(ps_x[0:rows, :], w[:], xT[0][:, half * HALF:half * HALF + HALF],
                                 start=True, stop=True).then_inc(x_ready, 1)

            def max_unit(m, kv, u, buffer):
                h, qt, half = kv * GROUP + u // 2 // TILES, u // 2 % TILES, u % 2
                positive(pe, m_free, m * (4 * MAXES) + kv * 2 * MAXES + u - 1)
                nc.tensor.matmul(
                    ps_m[:, u % 2, :], qs[0:STACK, buffer, h * PX + qt * P:h * PX + qt * P + P],
                    ks[0:STACK, buffer, kv * PX + half * HALF:kv * PX + half * HALF + HALF],
                    start=True, stop=True).then_inc(m_ready, 1)

            def scores(n, s, parity, pair):
                g, tt = s // TILES, s % TILES
                kv, half = g // 2, g % 2
                rows = STACK + 3
                positive(pe, exp_done, 2 * STEPS * n + 2 * s + pair - 1)
                for j in range(2):
                    h = kv * GROUP + 2 * pair + j
                    last = nc.tensor.matmul(
                        ps_s[:, pair, j * HALF:(j + 1) * HALF],
                        ks[0:rows, parity, kv * PX + tt * P:kv * PX + tt * P + P],
                        qs[0:rows, parity, h * PX + half * HALF:h * PX + half * HALF + HALF],
                        start=True, stop=True)
                last.then_inc(s_ready, 1)

            def products(n, s, parity):
                g, tt = s // TILES, s % TILES
                pe.wait_ge(exp_done, 2 * STEPS * n + 2 * s + 2)
                if tt == 0:
                    positive(pe, o_free, 4 * n + g)
                for j in range(GROUP):
                    last = nc.tensor.matmul(
                        ps_o[32 * j:32 * j + 32, :], vs[:, parity, tt, g // 2, :],
                        probs[:, s % 2, j * HALF:(j + 1) * HALF], start=(tt == 0), stop=(tt == TILES - 1))
                last.then_inc(pv_done, 1)

            def use_x(n, name):
                m = n + 1
                half = int(name[-1]) if name[-1] in "01" else 0
                if name[:2] == "wo":
                    pe.wait_ge(o_done, 4 * n)
                    fill(n, name)
                    for j in range(4):
                        c = half * HALF + j * P
                        for kv in range(KV):
                            last = nc.tensor.matmul(
                                ps_x[:, j * P:(j + 1) * P], o_norm[:, kv, c:c + P], wo[:, kv, :],
                                start=(kv == 0), stop=(kv == KV - 1))
                    last.then_inc(x_ready, 1)
                elif name[:2] == "xt":
                    transposes(n, m, 0, name, half)
                elif name[:2] == "x2":
                    transposes(n, n - 1, 1, name, half)
                elif name[0] == "q":
                    project(n, wq, P, name, half)
                elif name[0] == "k":
                    project(n, wk, KV * DK, name, half)
                elif name == "v":
                    fill(n, "v")
                    w = KV * DK
                    for j in range(TILES):
                        last = nc.tensor.matmul(ps_x[:, j * w:(j + 1) * w], xT[0][:, j * P:(j + 1) * P],
                                                wv[:], start=True, stop=True)
                    last.then_inc(x_ready, 1)
                elif name == "logits":
                    fill(n, "logits")
                    for j in range(TILES):
                        last = nc.tensor.matmul(ps_x[:, j * E:(j + 1) * E], xT[1][:, j * P:(j + 1) * P],
                                                wg[:], start=True, stop=True)
                    last.then_inc(x_ready, 1)
                else:
                    fill(n, name)
                    wait_apart(pe, maxes_done, 2 * n + 2 if name == "mt1" else 2 * m + 1, passed)
                    nc.tensor.transpose(ps_x[0:MAXES, 0:P], maxes[:], ident[:]).then_inc(x_ready, 1)

            def body(n, parity):
                finish, prepare, steps = parts_of(n)
                if steps:
                    pe.wait_ge(m_rows, 16 * (2 * n + 1))
                    pe.wait_ge(v_done, n + 1)
                for s in range(STEPS + 1):
                    if steps and s == STEPS // 2:
                        pe.wait_ge(m_rows, 16 * (2 * n + 2))
                    if prepare and s == STEPS // 2 + 1:
                        pe.wait_ge(stacked, 192 * (n + 2))
                    between = [(m, kv, u, 1 - parity if kv == 0 else parity) for m, kv, u in max_units(n, s)]
                    for pair in range(2 if steps and s < STEPS else 0):
                        for unit in between[:1]:
                            max_unit(*unit)
                        del between[:1]
                        scores(n, s, parity, pair)
                    for unit in between[:1]:
                        max_unit(*unit)
                    del between[:1]
                    if steps and s:
                        products(n, s - 1, parity)
                    if s == STEPS:
                        break
                    for unit in between:
                        max_unit(*unit)
                    for name in filled_at(n, s):
                        use_x(n, name)

            pe.wait_ge(const, 6)
            pe.wait_ge(loaded, 16 * 5)
            pe.wait_ge(wo_loaded, 16 * HEADS)
            images(pe, body)


BLOCKS = TOK // HALF
BT = HALF // P


def mixture_stage(nc, T, xT_dram, gates, ident, W1, b1, W2, b2, gated, out=None):
    hidden = W2.shape[1]
    if gated:
        n_units = E * hidden // P
        tiles_of = [[[(u // 2, (u % 2) * P, P)], [(u // 2, hidden + (u % 2) * P, P)]] for u in range(n_units)]
        pieces_of = [[(2 * e, 0, P), (2 * e + 1, 0, P)] for e in range(E)]
        rows_of = [[(u // 2, (u % 2) * P, P)] for u in range(n_units)]
        ring_h, ring_a = 2, 4
    else:
        n_units = E * hidden // P
        rest = hidden - P
        rows_of = []
        for pair in range(E // 2):
            a, b = 2 * pair, 2 * pair + 1
            rows_of += [[(a, 0, P)], [(b, 0, P)], [(a, P, rest), (b, P, rest)]]
        tiles_of = [[r] for r in rows_of]
        pieces_of = [[(3 * (e // 2) + e % 2, 0, P), (3 * (e // 2) + 2, (e % 2) * rest, rest)] for e in range(E)]
        ring_h, ring_a = 4, 6
    per_unit = 2 if gated else 1
    needs = [max(u for u, _, _ in pieces) for pieces in pieces_of]
    pre = "c" if gated else "e"

    with ExitStack() as ctx:
        sb, ps, sem = allocator(nc, ctx)
        w1 = sb(pre + "_w1", [P, n_units, per_unit, P])
        w2 = sb(pre + "_w2", [P, n_units, C])
        bias = sb(pre + "_bias", [P, n_units, per_unit])
        b2_in = sb(pre + "_b2_in", [3, E, C])
        b2_part = [sb(f"{pre}_b2_part{k}", [3, E, C], BF16) for k in range(3)]
        b2_rest = [sb(f"{pre}_b2_rest{k}", [3, E, C]) for k in range(2)]
        b2_rows = sb(pre + "_b2_rows", [3, E, C], BF16)
        ones = sb(pre + "_ones", [3, P], BF16)
        xb = sb(pre + "_xb", [P, 2, HALF])
        half_way = sb(pre + "_half_way", [P, 2, HALF])
        act_buf = sb(pre + "_act", [P, ring_a, HALF])
        total = sb(pre + "_total", [P, 2, HALF])
        turned = sb(pre + "_turned", [P, 2, HALF])
        ps_h = ps(pre + "_ps_h", [P, ring_h, per_unit, HALF])
        ps_y = ps(pre + "_ps_y", [P, 2, HALF])
        ps_t = ps(pre + "_ps_t", [P, HALF])

        w_in = sem(pre + "_w_in")
        one_set = sem(pre + "_one_set")
        b2_step = sem(pre + "_b2_step")
        x_in = [sem(f"{pre}_x_in{k}") for k in range(2)]
        x_used = sem(pre + "_x_used")
        h_ready = sem(pre + "_h_ready")
        half_done = sem(pre + "_half_done")
        a_ready = sem(pre + "_a_ready")
        y_ready = sem(pre + "_y_ready")
        y_added = sem(pre + "_y_added")
        turn_ready = sem(pre + "_turn_ready")
        turn_done = sem(pre + "_turn_done")
        out_sent = [sem(f"{pre}_out_sent{k}") for k in range(2)]

        n_loads = sum(len(t) for unit in tiles_of for t in unit) * 2 + sum(len(r) for r in rows_of) + 1

        def positive(eng, s, value):
            if not (isinstance(value, int) and value <= 0):
                eng.wait_ge(s, value)

        def blocks(eng, body):
            for k in range(2):
                body(0, k)
            with eng.Fori(1, IMAGES) as image:
                for k in range(2):
                    body(image, k)

        def number(image, k):
            return 2 * image + k

        def before(image, k):
            if k:
                return image, 0
            return None if isinstance(image, int) and image == 0 else (image - 1, 1)

        block = ctx.enter_context(nc.Block())

        @block.sync
        def _(sp):
            with nc.allow_non_contiguous_dma("biases, one hidden unit to a partition"):
                for u, tiles in enumerate(tiles_of):
                    for k, parts in enumerate(tiles):
                        at = 0
                        for e, first, count in parts:
                            sp.dma_start(w1[:, u, k, at:at + count], W1[e, :, first:first + count]).then_inc(w_in, 16)
                            sp.dma_start(bias[at:at + count, u, k:k + 1],
                                         b1[e, first:first + count].rearrange("(p a) -> p a", a=1)).then_inc(w_in, 16)
                            at += count
            for u, parts in enumerate(rows_of):
                at = 0
                for e, first, count in parts:
                    sp.dma_start(w2[at:at + count, u, :], W2[e, first:first + count, :]).then_inc(w_in, 16)
                    at += count
            sp.dma_start(b2_in[:], b2.rearrange("(a e) c -> a e c", a=1).broadcast_to([3, E, C])).then_inc(w_in, 16)

            def body(image, k):
                b = number(image, k)
                positive(sp, x_used, b - 1)
                sp.dma_start(xb[:, k], xT_dram[:, ds(b * HALF, HALF)]).then_inc(x_in[k], 16)
                if out is not None and before(image, k):
                    send(*before(image, k))

            def send(image, k):
                sp.wait_ge(turn_done, number(image, k) + 1)
                sp.dma_start(out.rearrange("i c y x -> c i (y x)")[:, ds(image, 1), k * HALF:(k + 1) * HALF],
                             turned[:, k].rearrange("c (a p) -> c a p", a=1)).then_inc(out_sent[k], 16)

            blocks(sp, body)
            if out is not None:
                send(IMAGES - 1, 1)
                for k in range(2):
                    sp.wait_ge(out_sent[k], 16 * IMAGES)

        @block.gpsimd
        def _(pool):
            pool.memset(ones[:], 1.0).then_inc(one_set, 1)

        @block.vector
        def _(dve):
            dve.wait_ge(w_in, 16 * n_loads)
            left = b2_in
            steps = 0
            for k in range(3):
                nc.vector.tensor_copy(b2_part[k][:], left[:]).then_inc(b2_step, 1)
                steps += 1
                dve.wait_ge(b2_step, steps)
                if k < 2:
                    nc.vector.tensor_tensor(b2_rest[k][:], left[:], b2_part[k][:], ALU.subtract).then_inc(b2_step, 1)
                    steps += 1
                    dve.wait_ge(b2_step, steps)
                    left = b2_rest[k]
            for k in range(3):
                if k == 0:
                    ins = nc.vector.tensor_scalar(b2_rows[:], b2_part[0][:], ident[0:3, 0:1], None, ALU.mult)
                else:
                    ins = nc.vector.scalar_tensor_tensor(b2_rows[:], b2_part[k][:], ident[0:3, k:k + 1],
                                                         b2_rows[:], ALU.mult, ALU.add)
                ins.then_inc(b2_step, 1)
                steps += 1
                dve.wait_ge(b2_step, steps)

            def multiply(b, u):
                at = b * n_units + u
                dve.wait_ge(half_done, at + 1)
                if not (isinstance(b, int) and b * E + u // 2 - 2 < 0):
                    dve.wait_ge(y_ready, b * E + u // 2 - 1)
                nc.vector.scalar_tensor_tensor(
                    act_buf[:, u % ring_a], ps_h[:, u % ring_h, 1], bias[:, u, 1:2], half_way[:, u % 2],
                    ALU.add, ALU.mult).then_inc(a_ready, 1)

            def add_expert(b, k, e):
                at = b * E + e
                dve.wait_ge(y_ready, at + 1)
                positive(dve, y_added, at)
                if e == 0 and out is not None:
                    positive(dve, turn_ready, b - 1)
                for j in range(BT):
                    tt = T[:, ds(b * HALF + j * P, P)]
                    own = total[:, k, j * P:(j + 1) * P]
                    last = nc.vector.scalar_tensor_tensor(
                        tt if e == E - 1 and out is None else own, ps_y[:, e % 2, j * P:(j + 1) * P],
                        gates[:, ds((b * BT + j) * E + e, 1)], tt if e == 0 else own, ALU.mult, ALU.add)
                last.then_inc(y_added, 1)

            def body(image, k):
                b = number(image, k)
                for e in range(E):
                    if gated:
                        multiply(b, 2 * e)
                        multiply(b, 2 * e + 1)
                    if e:
                        add_expert(b, k, e - 1)
                add_expert(b, k, E - 1)

            blocks(dve, body)

        @block.scalar
        def _(act):
            act.wait_ge(w_in, 16 * n_loads)

            def body(image, k):
                b = number(image, k)
                for u in range(n_units):
                    at = b * n_units + u
                    act.wait_ge(h_ready, at + 1)
                    if gated:
                        positive(act, a_ready, at - 1)
                        nc.scalar.activation(half_way[:, u % 2], ps_h[:, u % ring_h, 0], ACT.Silu,
                                             bias=bias[:, u, 0:1]).then_inc(half_done, 1)
                    else:
                        if u % 3 == 0 and not (isinstance(b, int) and b * (E // 2) + u // 3 < 2):
                            act.wait_ge(y_ready, b * E + 2 * (u // 3) - 2)
                        nc.scalar.activation(act_buf[:, u % ring_a], ps_h[:, u % ring_h, 0], ACT.Gelu,
                                             bias=bias[:, u, 0:1]).then_inc(a_ready, 1)
                    if out is not None and u == 5 and before(image, k):
                        turn_out(*before(image, k))

            def turn_out(image, k):
                act.wait_ge(turn_ready, number(image, k) + 1)
                positive(act, out_sent[k], 16 * image)
                nc.scalar.activation(turned[:, k], ps_t[:], ACT.Copy).then_inc(turn_done, 1)

            blocks(act, body)
            if out is not None:
                turn_out(IMAGES - 1, 1)

        @block.tensor
        def _(pe):
            pe.wait_ge(w_in, 16 * n_loads)
            pe.wait_ge(one_set, 1)
            pe.wait_ge(b2_step, 8)

            def unit(b, k, u):
                at = b * n_units + u
                positive(pe, a_ready, at - ring_h + 1)
                for t in range(per_unit):
                    last = nc.tensor.matmul(ps_h[:, u % ring_h, t], w1[:, u, t], xb[:, k], start=True, stop=True)
                last.then_inc(h_ready, 1)

            def expert(b, e):
                at = b * E + e
                positive(pe, y_added, at - 1)
                pe.wait_ge(a_ready, b * n_units + needs[e] + 1)
                for n, (u, first, rows) in enumerate(pieces_of[e]):
                    for j in range(BT):
                        nc.tensor.matmul(
                            ps_y[:, e % 2, j * P:(j + 1) * P],
                            act_buf[first:first + rows, u % ring_a, j * P:(j + 1) * P],
                            w2[first:first + rows, u], start=(n == 0 and j == 0), stop=False,
                            skip_group_check=True)
                nc.tensor.matmul(ps_y[:, e % 2], ones[:], b2_rows[:, e:e + 1].broadcast_to([3, BT, C]),
                                 start=False, stop=True, skip_group_check=True).then_inc(y_ready, 1)

            def turn(image, k):
                b = number(image, k)
                pe.wait_ge(y_added, b * E + E)
                positive(pe, turn_done, b)
                for j in range(BT):
                    last = nc.tensor.transpose(ps_t[:, j * P:(j + 1) * P], total[:, k, j * P:(j + 1) * P], ident[:])
                last.then_inc(turn_ready, 1)

            def body(image, k):
                b = number(image, k)
                pe.wait_ge(x_in[k], 16 * (image + 1))
                waiting = []
                for u in range(n_units):
                    unit(b, k, u)
                    if u == n_units - 1:
                        pe.wait_ge(h_ready, b * n_units + n_units)
                        pe.sem_inc(x_used, 1)
                    for e in list(waiting):
                        if u >= needs[e] + (2 if gated else 1):
                            expert(b, e)
                            waiting.remove(e)
                    waiting += [e for e in range(E) if needs[e] == u]
                    if out is not None and u == 4 and before(image, k):
                        turn(*before(image, k))
                for e in waiting:
                    expert(b, e)

            blocks(pe, body)
            if out is not None:
                turn(IMAGES - 1, 1)


HD = 8
DH = 16
GH = 4
CHUNKS = 4
TABLE_STEPS = 123
ROW_STEPS = 9
FIN3 = {"x20": (1, 2), "x21": (1, 3), "logits": (2, 1)}
PREP3 = {"xt0": (2, 2), "xt1": (2, 3)}
USES3 = len(FIN3) + len(PREP3)
STATES = 14
MIX_COLS = 3 * P


def decay_stage(nc, T, xT_dram, gates, ident, dram):
    with ExitStack() as ctx:
        sb, ps, sem = allocator(nc, ctx)
        w_in = [sb(f"d_w_in{k}", [P, C]) for k in range(3)]
        cols = sb("d_cols", [P, 6])
        conv = sb("d_conv", [P, 2, DH])
        spread_m = sb("d_spread", [P, 2, P])
        ones = sb("d_ones", [P, P])
        own = sb("d_own", [P, 2 * GH])
        is_part = sb("d_is_part", [P, 2])
        is_head = sb("d_is_head", [P, GH])
        mirror = sb("d_mirror", [P, P])
        swap = sb("d_swap", [P, 2, P])
        signs = sb("d_signs", [P, P])
        row = sb("d_row", [P, 2, 5])
        norm2 = sb("d_norm2", [P, 2, 1])
        norm2b = sb("d_norm2b", [P, 2, 1])
        mhalf = sb("d_mhalf", [P, TILES])
        eps = sb("d_eps", [P, TILES])
        zero = sb("d_zero", [P, TILES])
        pw = sb("d_pw", [P, 3, 2, P + 1])
        pt = sb("d_pt", [P, 4, 2, P])
        z = sb("d_z", [P, 2, 2, P + 1])
        amp_all = sb("d_amp_all", [P, HD])
        amp_exp = sb("d_amp_exp", [P, HD])
        row_exp = sb("d_row_exp", [P, 2])
        amp_pow = sb("d_amp_pow", [P, 7, HD])
        lag = sb("d_lag", [P, P], mybir.dt.int32)
        bit_i = sb("d_bit_i", [P, P], mybir.dt.int32)
        bit = sb("d_bit", [P, P])
        no_bit = sb("d_no_bit", [P, P])
        factor = sb("d_factor", [P, HD, P])
        ta = sb("d_ta", [P, 2, P])
        ta_t = sb("d_ta_t", [P, 2, P])
        wq = sb("d_wq", [P, 2, P])
        wkv = sb("d_wkv", [P, MIX_COLS])
        bias_in = sb("d_bias_in", [3, MIX_COLS])
        bias_part = [sb(f"d_bias_part{k}", [3, MIX_COLS], BF16) for k in range(3)]
        bias_rest = [sb(f"d_bias_rest{k}", [3, MIX_COLS]) for k in range(2)]
        bias_rows = sb("d_bias_rows", [3, MIX_COLS], BF16)
        ones3 = sb("d_ones3", [3, P], BF16)
        tab_k = sb("d_tab_k", [P, 2, P])
        tab_q = sb("d_tab_q", [P, 2, GH, P])
        tab_s = sb("d_tab_s", [P, 2, P])
        tab_end = sb("d_tab_end", [P, 2, P])
        decay = sb("d_decay", [P, HD, P])
        turn_m = sb("d_turn", [P, 2, P])
        start = sb("d_start", [P, 2, P])
        state = sb("d_state", [P, 2, 2, P])
        block_mask = sb("d_block_mask", [P, P])
        wg = sb("d_wg", [P, E])
        bg = sb("d_bg", [P, E])
        iota = sb("d_iota", [P, E])
        stats = [sb(f"d_stats{k}", [P, TILES, 6]) for k in range(2)]
        mv = [sb(f"d_mv{k}", [P, TILES, 2]) for k in range(2)]
        rstd = [sb(f"d_rstd{k}", [P, TILES]) for k in range(2)]
        shift = [sb(f"d_shift{k}", [P, TILES]) for k in range(2)]
        xn = [sb(f"d_xn{k}", [P, PX]) for k in range(2)]
        xT = [sb(f"d_xT{k}", [P, PX]) for k in range(2)]
        raw = sb("d_raw", [P, 2, HALF])
        q_wide = sb("d_q_wide", [P, 2, CHUNKS, GH * P])
        q_state = sb("d_q_state", [P, 2, HALF])
        k_chan = sb("d_k_chan", [P, 2, HALF])
        k_tok = sb("d_k_tok", [P, 2, CHUNKS, 2 * P])
        v_tok = sb("d_v_tok", [P, 2, CHUNKS, HD, 2 * DH])
        inner = sb("d_inner", [P, 2, HALF])
        o_chan = sb("d_o_chan", [P, 2, HALF])
        logits = sb("d_logits", [P, TILES, E])
        top = sb("d_top", [P, TILES, 8])
        top_at = sb("d_topat", [P, TILES, 8], U32)
        top_atf = sb("d_topatf", [P, TILES, 2])
        gap = sb("d_gap", [P, TILES])
        expo = sb("d_expo", [P, TILES])
        gsum = sb("d_gsum", [P, TILES])
        w1 = sb("d_w1", [P, TILES])
        w2 = sb("d_w2", [P, TILES])
        hit = sb("d_hit", [P, 2, TILES, E])

        ps_x = ps("d_ps_x", [P, HALF])
        ps_q = ps("d_ps_q", [P, HALF])
        ps_k = ps("d_ps_k", [P, HALF])
        ps_s = ps("d_ps_s", [P, 2, HALF])
        ps_o = ps("d_ps_o", [P, HALF])
        ps_st = ps("d_ps_st", [P, P])
        ps_t = ps("d_ps_t", [P, HALF])

        loaded = sem("d_loaded")
        const = sem("d_const")
        step = sem("d_step")
        passed = sem("d_passed")
        set_up = sem("d_set_up")
        moved = sem("d_moved")
        norm_ready = sem("d_norm_ready")
        norm_done = sem("d_norm_done")
        exps_done = sem("d_exps_done")
        stats_done = [sem(f"d_stats_done{k}") for k in range(2)]
        mv_done = [sem(f"d_mv_done{k}") for k in range(2)]
        rstd_done = [sem(f"d_rstd_done{k}") for k in range(2)]
        xn_done = [sem(f"d_xn_done{k}") for k in range(2)]
        xn_used = [sem(f"d_xn_used{k}") for k in range(2)]
        x_ready = sem("d_x_ready")
        x_free = sem("d_x_free")
        p_ready = sem("d_p_ready")
        p_copied = sem("d_p_copied")
        tables_used = sem("d_tables_used")
        k_ready = sem("d_k_ready")
        k_done = sem("d_k_done")
        v_done = sem("d_v_done")
        s_ready = sem("d_s_ready")
        inner_done = sem("d_inner_done")
        chunk_done = sem("d_chunk_done")
        st_ready = sem("d_st_ready")
        st_done = sem("d_st_done")
        o_copied = sem("d_o_copied")
        o_turned = sem("d_o_turned")
        t_added = sem("d_t_added")
        xT_sent = sem("d_xT_sent")
        g_step = sem("d_g_step")
        gap_exp = sem("d_gap_exp")
        N_LOADS = 20

        def positive(eng, s, value):
            if not (isinstance(value, int) and value <= 0):
                eng.wait_ge(s, value)

        def parts_of(n):
            if not isinstance(n, int):
                return True, True, True
            return n >= 1, n < IMAGES - 1, 0 <= n < IMAGES

        def uses(n):
            finish, prepare, _ = parts_of(n)
            fills = (FIN3 if finish else {}) | (PREP3 if prepare else {})
            if isinstance(n, int) and n < 1:
                first = 0 if n < 0 else len(PREP3)
            elif isinstance(n, int) and n == IMAGES:
                first = (n - 2) * USES3 + 2 * len(PREP3) + len(FIN3)
            else:
                first = (n - 1) * USES3 + 2 * len(PREP3)
            return first, fills

        def use(n, name):
            first, fills = uses(n)
            return first + sorted(fills, key=fills.get).index(name)

        def filled_at(n, a, c):
            return [name for name, at in uses(n)[1].items() if at == (a, c)]

        def images(eng, body):
            body(-1)
            body(0)
            with eng.Fori(1, IMAGES - 1) as n:
                body(n)
            body(IMAGES - 1)
            body(IMAGES)

        def slots(n):
            steps = parts_of(n)[2]
            for a in range(4):
                for c in range(CHUNKS):
                    nxt = steps and not (isinstance(n, int) and n == IMAGES - 1 and a == 3)
                    if isinstance(n, int) and n < 0:
                        nxt = a == 3
                    yield a, c, steps, nxt

        def state_index(n, a, c):
            if a >= 2 and c == CHUNKS - 1:
                return None
            return n * STATES + (a * 4 + c if a < 3 else 11 + c)

        block = ctx.enter_context(nc.Block())

        @block.sync
        def _(sp):
            for k, name in enumerate(("wq", "wk", "wv")):
                sp.dma_start(w_in[k][:], dram[f"L3_attn_{name}_w"]).then_inc(loaded, 16)
            with nc.allow_non_contiguous_dma("one number to a partition"):
                for k, name in enumerate(("phazor_re", "phazor_im")):
                    sp.dma_start(cols[:, k:k + 1], dram[f"L3_attn_{name}"].rearrange("h (d a) -> (h d) a", a=1)
                                 ).then_inc(loaded, 16)
                for k, name in enumerate(("wq_b", "wk_b", "wv_b")):
                    sp.dma_start(cols[:, 3 + k:4 + k], dram[f"L3_attn_{name}"].rearrange("(p a) -> p a", a=1)
                                 ).then_inc(loaded, 16)
                amp = dram["L3_attn_amplitude"].rearrange("(h a) -> h a", a=1)
                for h in range(HD):
                    sp.dma_start(cols[DH * h:DH * (h + 1), 2:3], amp[h:h + 1].broadcast_to([DH, 1])
                                 ).then_inc(loaded, 16)
                sp.dma_start(amp_all[:], amp.rearrange("h a -> a h").broadcast_to([P, HD])).then_inc(loaded, 16)
            for k, name in enumerate(("re", "im")):
                sp.dma_start(conv[:, k], dram[f"L3_attn_last_conv_{name}"].rearrange("h d e -> (h d) e")
                             ).then_inc(loaded, 16)
            sp.dma_start(wg[:], dram["L3_ffn_Wg"]).then_inc(loaded, 16)
            sp.dma_start(bg[:], dram["L3_ffn_bg"].rearrange("(a e) -> a e", a=1).broadcast_to([P, E])
                         ).then_inc(loaded, 16)
            assert 3 + 2 + 3 + HD + 1 + 2 + 2 == N_LOADS + 1

            def body(n):
                if parts_of(n)[0]:
                    sp.wait_ge(x_free, use(n, "x21") + 1)
                    sp.dma_start(xT_dram[:, ds((n - 1) * PX, PX)], xT[1][:]).then_inc(xT_sent, 16)

            images(sp, body)
            sp.wait_ge(xT_sent, 16 * IMAGES)

        @block.gpsimd
        def _(pool):
            count = [0]

            def made(ins):
                count[0] += 1
                ins.then_inc(const, 1)
                pool.wait_ge(const, count[0])

            made(pool.memset(ones[:], 1.0))
            made(pool.memset(mhalf[:], -0.5))
            made(pool.memset(eps[:], EPS_T))
            made(pool.memset(zero[:], 0.0))
            made(pool.memset(ones3[:], 1.0))
            made(pool.memset(v_tok[:], 0.0))
            made(pool.iota(iota[:], [[1, E]], base=0, channel_multiplier=0,
                           allow_small_or_imprecise_dtypes=True))
            made(pool.iota(lag[:], [[1, P]], base=0, channel_multiplier=-1))
            for g in range(2):
                made(pool.affine_select(
                    out=spread_m[:, g].rearrange("p (j s d) -> p j s d", s=2, d=DH),
                    in_=ones[:].rearrange("p (j s d) -> p j s d", s=2, d=DH), compare_op=ALU.is_equal, fill=0.0,
                    base=-g * GH * DH, pattern=[[-DH, GH], [0, 2], [-1, DH]], channel_multiplier=1))
            made(pool.affine_select(out=own[:], in_=ones[:, 0:2 * GH], compare_op=ALU.is_ge, fill=0.0, base=0,
                                    pattern=[[-DH, 2 * GH]], channel_multiplier=1))
            made(pool.affine_select(out=own[:], in_=own[:], compare_op=ALU.is_ge, fill=0.0, base=DH - 1,
                                    pattern=[[DH, 2 * GH]], channel_multiplier=-1))
            made(pool.affine_select(out=mirror[:], in_=ones[:], compare_op=ALU.is_equal, fill=0.0, base=1 - P,
                                    pattern=[[1, P]], channel_multiplier=1))
            for k, off in enumerate((DH, -DH)):
                made(pool.affine_select(out=swap[:, k], in_=ones[:], compare_op=ALU.is_equal, fill=0.0, base=off,
                                        pattern=[[-1, P]], channel_multiplier=1))
            pool.wait_ge(norm_ready, 1)
            nc.gpsimd.tensor_tensor(norm2b[:].rearrange("p a b -> p (a b)"), norm2[:].rearrange("p a b -> p (a b)"),
                                    mhalf[:, 0:2], ALU.pow).then_inc(norm_done, 1)

            def scales(m, k):
                wait_apart(pool, mv_done[k], m + 1, passed)
                positive(pool, xn_done[k], TILES * m)
                nc.gpsimd.tensor_tensor(rstd[k][:], mv[k][:, :, 1], eps[:], ALU.add).then_inc(rstd_done[k], 1)
                pool.wait_ge(rstd_done[k], 4 * m + 1)
                nc.gpsimd.tensor_tensor(rstd[k][:], rstd[k][:], mhalf[:], ALU.pow).then_inc(rstd_done[k], 1)
                pool.wait_ge(rstd_done[k], 4 * m + 2)
                nc.gpsimd.tensor_tensor(shift[k][:], mv[k][:, :, 0], rstd[k][:], ALU.mult).then_inc(rstd_done[k], 1)
                pool.wait_ge(rstd_done[k], 4 * m + 3)
                nc.gpsimd.tensor_tensor(shift[k][:], zero[:], shift[k][:], ALU.subtract).then_inc(rstd_done[k], 1)

            def with_tables(w, g, k):
                pool.wait_ge(p_copied, 2 * w + 1)
                positive(pool, chunk_done, 4 * (w - 1))
                for c in range(CHUNKS):
                    nc.gpsimd.tensor_tensor(
                        q_wide[:, k, c].rearrange("p (j l) -> p j l", j=GH),
                        raw[:, 0:1, c * P:(c + 1) * P].broadcast_to([P, GH, P]), tab_q[:, g], ALU.mult
                    ).then_inc(tables_used, 1)
                nc.gpsimd.tensor_tensor(
                    q_state[:, k].rearrange("p (c l) -> p c l", c=CHUNKS),
                    raw[:, 0].rearrange("p (c l) -> p c l", c=CHUNKS),
                    tab_s[:, g:g + 1].broadcast_to([P, CHUNKS, P]), ALU.mult).then_inc(tables_used, 1)
                pool.wait_ge(p_copied, 2 * w + 2)
                nc.gpsimd.tensor_tensor(
                    k_chan[:, k].rearrange("p (c l) -> p c l", c=CHUNKS),
                    raw[:, 1].rearrange("p (c l) -> p c l", c=CHUNKS),
                    tab_k[:, g:g + 1].broadcast_to([P, CHUNKS, P]), ALU.mult).then_inc(tables_used, 1)

            def body(n):
                finish, prepare, _ = parts_of(n)
                if isinstance(n, int) and n < 0:
                    scales(0, 0)
                for a, c, steps, nxt in slots(n):
                    if (a, c) == (0, 2) and finish:
                        scales(n - 1, 1)
                    if (a, c) == (1, 2) and prepare and not (isinstance(n, int) and n < 0):
                        scales(n + 1, 0)
                    if c == 0 and nxt:
                        with_tables(4 * n + a + 1, (a + 1) % 2, (a + 1) % 2)

            pool.wait_ge(step, TABLE_STEPS)
            images(pool, body)

        @block.vector
        def _(dve):
            count = [0]

            def link(ins):
                count[0] += 1
                ins.then_inc(step, 1)
                dve.wait_ge(step, count[0])

            def by_row(x, n):
                return x.rearrange("p (a b) -> p a b", b=1).broadcast_to([P, x.shape[1], n])

            tt, tsc, stt = nc.vector.tensor_tensor, nc.vector.tensor_scalar, nc.vector.scalar_tensor_tensor
            dve.wait_ge(loaded, 16 * (N_LOADS + 1))
            dve.wait_ge(const, 15)
            own_v = own[:].rearrange("p (j s) -> p j s", s=2)
            link(nc.vector.tensor_reduce(is_part[:], own[:].rearrange("p (j s) -> p s j", s=2), AX.X, ALU.add))
            link(nc.vector.tensor_reduce(is_head[:], own_v, AX.X, ALU.add))
            link(nc.vector.tensor_copy(block_mask[:].rearrange("p (j x) -> p j x", j=GH), by_row(is_head[:], 2 * DH)))
            link(tsc(signs[:], swap[:, 0], is_part[:, 0:1], None, ALU.mult))
            link(tsc(swap[:, 1], swap[:, 1], is_part[:, 1:2], None, ALU.mult))
            link(tt(signs[:], signs[:], swap[:, 1], ALU.subtract))
            dve.wait_ge(set_up, 1)
            link(nc.vector.tensor_copy(wq[:].rearrange("p g r -> p (g r)"), ps_q[:, 0:2 * P]))
            link(nc.vector.tensor_copy(wkv[:], ps_k[:, 0:MIX_COLS]))
            link(nc.vector.tensor_copy(row[:], ps_o[:, 0:10].rearrange("p (g k) -> p g k", g=2)))
            link(nc.vector.tensor_copy(bias_in[:], ps_s[0:3, 0, 0:MIX_COLS]))
            lc = ps_s[:, 1, 0:4 * DH].rearrange("p (g s e) -> p g s e", g=2, s=2)
            link(nc.vector.tensor_copy(pt[:, 0, :, 0:2 * DH].rearrange("p g (s e) -> p g s e", s=2), lc))
            for g in range(2):
                link(tsc(pt[:, 1, g, 0:DH], pt[:, 0, g, 0:DH], is_part[:, 0:1], None, ALU.mult))
                link(stt(pt[:, 1, g, 0:DH], pt[:, 0, g, DH:2 * DH], is_part[:, 1:2], pt[:, 1, g, 0:DH],
                         ALU.mult, ALU.add))
                link(nc.vector.memset(start[:, g], 0.0))
                link(tt(start[:, g].rearrange("p (j x) -> p j x", j=GH)[:, :, 0:DH],
                        pt[:, 1, g:g + 1, 0:DH].broadcast_to([P, GH, DH]), by_row(is_head[:], DH), ALU.mult))
            left = bias_in
            for k in range(3):
                link(nc.vector.tensor_copy(bias_part[k][:], left[:]))
                if k < 2:
                    link(tt(bias_rest[k][:], left[:], bias_part[k][:], ALU.subtract))
                    left = bias_rest[k]
            link(tsc(bias_rows[:], bias_part[0][:], ident[0:3, 0:1], None, ALU.mult))
            for k in (1, 2):
                link(stt(bias_rows[:], bias_part[k][:], ident[0:3, k:k + 1], bias_rows[:], ALU.mult, ALU.add))
            link(tt(pt[:, 0, :, 0:1], row[:, :, 0:1], row[:, :, 0:1], ALU.mult))
            link(tt(pt[:, 1, :, 0:1], row[:, :, 1:2], row[:, :, 1:2], ALU.mult))
            tt(norm2[:], pt[:, 0, :, 0:1], pt[:, 1, :, 0:1], ALU.add).then_inc(norm_ready, 1)
            dve.wait_ge(norm_done, 1)
            link(nc.vector.memset(pw[:, 0, :, 0:1], 1.0))
            link(nc.vector.memset(pw[:, 1, :, 0:1], 0.0))
            link(nc.vector.memset(pw[:, 2, :, 0:1], 1.0))
            link(tt(pw[:, 0, :, 1:2], row[:, :, 0:1], norm2b[:], ALU.mult))
            link(tt(pw[:, 1, :, 1:2], row[:, :, 1:2], norm2b[:], ALU.mult))
            dve.wait_ge(exps_done, 2)
            link(tsc(row_exp[:], row_exp[:], 1.0, None, ALU.add))
            link(nc.vector.reciprocal(pw[:, 2, :, 1], row_exp[:]))
            link(tsc(amp_exp[:], amp_exp[:], 1.0, None, ALU.add))
            link(nc.vector.reciprocal(amp_pow[:, 0], amp_exp[:]))
            n = 1
            while n < P:
                def at_n(k):
                    return pw[:, k, :, n:n + 1].broadcast_to([P, 2, n])

                def low(k):
                    return pw[:, k, :, 1:n + 1]

                tt(pt[:, 0, :, 0:n], low(0), at_n(0), ALU.mult)
                tt(pt[:, 1, :, 0:n], low(1), at_n(1), ALU.mult)
                tt(pt[:, 2, :, 0:n], low(0), at_n(1), ALU.mult)
                link(tt(pt[:, 3, :, 0:n], low(1), at_n(0), ALU.mult))
                tt(pw[:, 2, :, n + 1:2 * n + 1], low(2), at_n(2), ALU.mult)
                tt(pw[:, 0, :, n + 1:2 * n + 1], pt[:, 0, :, 0:n], pt[:, 1, :, 0:n], ALU.subtract)
                link(tt(pw[:, 1, :, n + 1:2 * n + 1], pt[:, 2, :, 0:n], pt[:, 3, :, 0:n], ALU.add))
                n *= 2
            for k in range(2):
                link(tt(z[:, k], pw[:, k], pw[:, 2], ALU.mult))
            for g in range(2):
                link(tsc(tab_k[:, g], pw[:, 0, g, 0:P], is_part[:, 0:1], None, ALU.mult))
                link(stt(tab_k[:, g], pw[:, 1, g, 0:P], is_part[:, 1:2], tab_k[:, g], ALU.mult, ALU.add))
                link(tt(tab_q[:, g], tab_k[:, g:g + 1].broadcast_to([P, GH, P]), by_row(is_head[:], P), ALU.mult))
                link(tsc(pt[:, 0, g], z[:, 1, g, 1:P + 1], is_part[:, 1:2], None, ALU.mult))
                link(stt(tab_s[:, g], z[:, 0, g, 1:P + 1], is_part[:, 0:1], pt[:, 0, g], ALU.mult, ALU.subtract))
                link(tsc(ta[:, g], z[:, 0, g, 0:P], is_part[:, 0:1], None, ALU.mult))
                link(stt(ta[:, g], z[:, 1, g, 0:P], is_part[:, 1:2], ta[:, g], ALU.mult, ALU.add))
                link(tsc(turn_m[:, g], ident[:], z[:, 0, g, P:P + 1], None, ALU.mult))
                link(stt(turn_m[:, g], signs[:], z[:, 1, g, P:P + 1], turn_m[:, g], ALU.mult, ALU.add))
            nc.vector.memset(pt[:, 3, 0, 0:1], 0.0).then_inc(moved, 1)
            dve.wait_ge(set_up, 2)
            nc.vector.tensor_copy(ta_t[:].rearrange("p g r -> p (g r)"), ps_q[:, 0:2 * P]).then_inc(moved, 1)
            dve.wait_ge(set_up, 3)
            link(nc.vector.tensor_copy(tab_end[:].rearrange("p g r -> p (g r)"), ps_k[:, 0:2 * P]))
            for k in range(1, 7):
                link(tt(amp_pow[:, k], amp_pow[:, k - 1], amp_pow[:, k - 1], ALU.mult))
            link(tsc(bit[:], lag[:], 0.0, None, ALU.is_ge))
            link(nc.vector.tensor_copy(decay[:], bit[:].rearrange("p (a l) -> p a l", a=1).broadcast_to([P, HD, P])))
            for k in range(7):
                link(tsc(bit_i[:], lag[:], k, 1, ALU.logical_shift_right, ALU.bitwise_and))
                link(nc.vector.tensor_copy(bit[:], bit_i[:]))
                link(tsc(no_bit[:], bit[:], -1.0, 1.0, ALU.mult, ALU.add))
                link(tt(factor[:], bit[:].rearrange("p (a l) -> p a l", a=1).broadcast_to([P, HD, P]),
                        by_row(amp_pow[:, k], P), ALU.mult))
                link(tt(factor[:], factor[:],
                        no_bit[:].rearrange("p (a l) -> p a l", a=1).broadcast_to([P, HD, P]), ALU.add))
                link(tt(decay[:], decay[:], factor[:], ALU.mult))
            assert count[0] == TABLE_STEPS, count[0]

            def statistics(m, k):
                for j in range(TILES):
                    last = nc.vector.bn_stats(stats[k][:, j, :], T[:, ds(m * PX + j * P, P)])
                last.then_inc(stats_done[k], 1)
                positive(dve, xn_done[k], TILES * m)
                wait_apart(dve, stats_done[k], m + 1, passed)
                for j in range(TILES):
                    last = nc.vector.bn_aggr(mv[k][:, j, :], stats[k][:, j, :])
                last.then_inc(mv_done[k], 1)

            def masked(w, c, g):
                at = 4 * w + c
                dve.wait_ge(s_ready, at + 1)
                positive(dve, chunk_done, at - 1)
                tt(inner[:, c % 2].rearrange("p (j l) -> p j l", j=GH), ps_s[:, c % 2].rearrange(
                    "p (j l) -> p j l", j=GH), decay[:, g * GH:(g + 1) * GH], ALU.mult).then_inc(inner_done, 1)

            def end_keys(n, half, c):
                at = 8 * n + 4 * half + c
                dve.wait_ge(k_ready, at + 1)
                positive(dve, chunk_done, 4 * (4 * (n - 1) + 2 * half + 2))
                tt(k_tok[:, half, c], ps_k[:, 0:2 * P], tab_end[:].rearrange("p g r -> p (g r)"), ALU.mult
                   ).then_inc(k_done, 1)

            def new_state(n, a, c):
                at = state_index(n, a, c)
                g, cc = a % 2, 4 * (a // 2) + c
                dve.wait_ge(st_ready, at + 1)
                tt(state[:, g, (cc + 1) % 2], ps_st[:], block_mask[:], ALU.mult
                   ).then_inc(st_done, 1)

            def add_item(w, image, a):
                g, half = a % 2, a // 2
                dve.wait_ge(o_turned, w + 1)
                t_v = T[:, ds(image * PX + half * HALF, HALF)].rearrange(
                    "p (c h e) -> p c h e", c=CHUNKS, e=DH)[:, :, g * GH:(g + 1) * GH]
                tt(t_v, t_v, ps_t[:].rearrange("p (c j x) -> p c j x", c=CHUNKS, j=GH)[:, :, :, 0:DH], ALU.add
                   ).then_inc(t_added, 1)

            def gate(n):
                m = n - 1
                g0 = 9 * m
                dve.wait_ge(x_ready, use(n, "logits") + 1)
                nc.vector.tensor_tensor(
                    logits[:], ps_x[:, 0:TILES * E].rearrange("p (t e) -> p t e", e=E),
                    bg[:].rearrange("p (a e) -> p a e", a=1).broadcast_to([P, TILES, E]),
                    ALU.add).then_inc(g_step, 1)
                dve.wait_ge(g_step, g0 + 1)
                dve.sem_inc(x_free, 1)
                for j in range(TILES):
                    last = nc.vector.max(top[:, j, :], logits[:, j, :])
                last.then_inc(g_step, 1)
                dve.wait_ge(g_step, g0 + 2)
                nc.vector.tensor_tensor(gap[:], top[:, :, 1], top[:, :, 0], ALU.subtract).then_inc(g_step, 1)
                for j in range(TILES):
                    last = nc.vector.max_index(top_at[:, j, :], top[:, j, :], logits[:, j, :])
                last.then_inc(g_step, 1)
                dve.wait_ge(g_step, g0 + 4)
                nc.vector.tensor_copy(top_atf[:], top_at[:, :, 0:2]).then_inc(g_step, 1)
                dve.wait_ge(gap_exp, m + 1)
                nc.vector.tensor_scalar(gsum[:], expo[:], 1.0, None, ALU.add).then_inc(g_step, 1)
                dve.wait_ge(g_step, g0 + 6)
                nc.vector.reciprocal(w1[:], gsum[:]).then_inc(g_step, 1)
                for k in range(2):
                    nc.vector.tensor_tensor(
                        hit[:, k], iota[:].rearrange("p (a e) -> p a e", a=1).broadcast_to([P, TILES, E]),
                        top_atf[:, :, k:k + 1].broadcast_to([P, TILES, E]), ALU.is_equal)
                dve.wait_ge(g_step, g0 + 7)
                nc.vector.tensor_tensor(w2[:], w1[:], expo[:], ALU.mult).then_inc(g_step, 1)
                dve.wait_ge(g_step, g0 + 8)
                for k, w in ((0, w1), (1, w2)):
                    last = nc.vector.tensor_tensor(
                        hit[:, k], hit[:, k],
                        w[:].rearrange("p (t a) -> p t a", a=1).broadcast_to([P, TILES, E]), ALU.mult)
                last.then_inc(g_step, 1)
                dve.wait_ge(g_step, g0 + 9)
                nc.vector.tensor_tensor(
                    gates[:, ds(m * TILES * E, TILES * E)],
                    hit[:, 0].rearrange("p t e -> p (t e)"), hit[:, 1].rearrange("p t e -> p (t e)"), ALU.add)

            def body(n):
                finish, prepare, _ = parts_of(n)
                if isinstance(n, int) and n < 0:
                    statistics(0, 0)
                for a, c, steps, nxt in slots(n):
                    w = 4 * n + a
                    if steps and c < CHUNKS - 1:
                        masked(w, c + 1, a % 2)
                    elif c == CHUNKS - 1 and nxt:
                        masked(w + 1, 0, (a + 1) % 2)
                    if nxt and a % 2:
                        if a == 1:
                            end_keys(n, 1, c)
                        else:
                            end_keys(n + 1, 0, c)
                    if c == 1 and (finish if a == 0 else steps):
                        image, item = (n - 1, 3) if a == 0 else (n, a - 1)
                        add_item(w - 1, image, item)
                    if steps and state_index(0, a, c) is not None:
                        new_state(n, a, c)
                    if (a, c) == (0, 2) and finish:
                        dve.wait_ge(t_added, 4 * n)
                        statistics(n - 1, 1)
                    if (a, c) == (1, 0) and prepare and not (isinstance(n, int) and n < 0):
                        statistics(n + 1, 0)
                    if (a, c) == FIN3["logits"] and finish:
                        gate(n)

            images(dve, body)

        @block.scalar
        def _(act):
            act.wait_ge(loaded, 16 * (N_LOADS + 1))
            act.wait_ge(step, ROW_STEPS)
            nc.scalar.activation(row_exp[:], row[:, :, 2], ACT.Exp, scale=-1.0).then_inc(exps_done, 1)
            nc.scalar.activation(amp_exp[:], amp_all[:], ACT.Exp, scale=-1.0).then_inc(exps_done, 1)

            def normalise(m, k):
                act.wait_ge(rstd_done[k], 4 * m + 4)
                positive(act, xn_used[k], m)
                for j in range(TILES):
                    nc.scalar.activation(xn[k][:, j * P:(j + 1) * P], T[:, ds(m * PX + j * P, P)], ACT.Identity,
                                         scale=rstd[k][:, j:j + 1], bias=shift[k][:, j:j + 1],
                                         ).then_inc(xn_done[k], 1)

            def read_out(n, name):
                half = int(name[2])
                k = 0 if name[:2] == "xt" else 1
                act.wait_ge(x_ready, use(n, name) + 1)
                if k and half == 0:
                    positive(act, xT_sent, 16 * (n - 1))
                nc.scalar.activation(xT[k][:, half * HALF:half * HALF + HALF], ps_x[:], ACT.Copy).then_inc(x_free, 1)

            def copy_projection(w, g, kind):
                act.wait_ge(p_ready, 2 * w + kind + 1)
                positive(act, tables_used, 6 * w - 1 + kind)
                nc.scalar.activation(raw[:, kind], ps_q[:], ACT.Identity, bias=row[:, g, 3 + kind:4 + kind]
                                     ).then_inc(p_copied, 1)

            def values(n, half, c):
                at = 8 * n + 4 * half + c
                act.wait_ge(k_done, at + 1)
                positive(act, chunk_done, 4 * (4 * (n - 1) + 2 * half + 2))
                nc.scalar.activation(v_tok[:, half, c, :, 0:DH],
                                     ps_k[:, 2 * P:3 * P].rearrange("p (h e) -> p h e", h=HD), ACT.Copy
                                     ).then_inc(v_done, 1)

            def body(n):
                finish, prepare, _ = parts_of(n)
                first = isinstance(n, int) and n < 0
                if first:
                    normalise(0, 0)
                for a, c, steps, nxt in slots(n):
                    w = 4 * n + a
                    if (a, c) == (1, 1) and finish:
                        normalise(n - 1, 1)
                    if (a, c) == (2, 0) and prepare and not first:
                        normalise(n + 1, 0)
                    if nxt and c < 2:
                        copy_projection(w + 1, (a + 1) % 2, c)
                    if nxt and a % 2:
                        if a == 1:
                            values(n, 1, c)
                        else:
                            values(n + 1, 0, c)
                    for name in filled_at(n, a, c):
                        if name != "logits":
                            read_out(n, name)
                    if (a, c) == FIN3["logits"] and finish:
                        act.wait_ge(g_step, 9 * (n - 1) + 3)
                        nc.scalar.activation(expo[:], gap[:], ACT.Exp).then_inc(gap_exp, 1)
                    if steps and c == CHUNKS - 1:
                        act.wait_ge(chunk_done, 4 * w + 4)
                        positive(act, o_turned, w - 1)
                        nc.scalar.activation(o_chan[:, a % 2], ps_o[:], ACT.Copy).then_inc(o_copied, 1)

            images(act, body)

        @block.tensor
        def _(pe):
            pe.wait_ge(loaded, 16 * (N_LOADS + 1))
            pe.wait_ge(const, 15)
            mm = nc.tensor.matmul
            for g in range(2):
                mm(ps_q[:, g * P:(g + 1) * P], w_in[0][:], spread_m[:, g], start=True, stop=True)
                mm(ps_k[:, g * P:(g + 1) * P], w_in[1][:], spread_m[:, g], start=True, stop=True)
                mm(ps_o[:, g * 5:g * 5 + 5], spread_m[:, g], cols[:, 0:5], start=True, stop=True)
                mm(ps_s[0:3, 0, g * P:(g + 1) * P], cols[:, 4:5].broadcast_to([P, 3]), spread_m[:, g],
                   start=True, stop=True)
                mm(ps_s[:, 1, g * 2 * DH:(g + 1) * 2 * DH], spread_m[:, g], conv[:].rearrange("p s e -> p (s e)"),
                   start=True, stop=True)
            mm(ps_k[:, 2 * P:3 * P], w_in[2][:], ident[:], start=True, stop=True)
            mm(ps_s[0:3, 0, 2 * P:3 * P], cols[:, 5:6].broadcast_to([P, 3]), ident[:], start=True, stop=True
               ).then_inc(set_up, 1)
            pe.wait_ge(moved, 1)
            for g in range(2):
                last = nc.tensor.transpose(ps_q[:, g * P:(g + 1) * P], ta[:, g], ident[:])
            last.then_inc(set_up, 1)
            pe.wait_ge(moved, 2)
            mm(ps_k[:, 0:2 * P], mirror[:], ta_t[:].rearrange("p g r -> p (g r)"), start=True, stop=True
               ).then_inc(set_up, 1)
            pe.wait_ge(step, TABLE_STEPS)

            def use_x(n, name):
                positive(pe, x_free, use(n, name))
                if name == "logits":
                    for j in range(TILES):
                        last = mm(ps_x[:, j * E:(j + 1) * E], xT[1][:, j * P:(j + 1) * P], wg[:],
                                  start=True, stop=True)
                    last.then_inc(x_ready, 1)
                    return
                half = int(name[2])
                k, m = (0, n + 1) if name[:2] == "xt" else (1, n - 1)
                pe.wait_ge(xn_done[k], TILES * m + 4 * (half + 1))
                for j in range(4):
                    c = half * HALF + j * P
                    last = nc.tensor.transpose(ps_x[:, j * P:(j + 1) * P], xn[k][:, c:c + P], ident[:])
                last.then_inc(x_ready, 1)
                if half:
                    pe.wait_ge(x_ready, use(n, name) + 1)
                    pe.sem_inc(xn_used[k], 1)

            def project(w, a, kind):
                g, half = a % 2, a // 2
                positive(pe, p_copied, 2 * w + kind)
                weights = wq[:, g] if kind == 0 else wkv[:, g * P:(g + 1) * P]
                mm(ps_q[:], weights, xT[0][:, half * HALF:half * HALF + HALF], start=True, stop=True
                   ).then_inc(p_ready, 1)

            def mix(n, half, c):
                at = 8 * n + 4 * half + c
                positive(pe, k_done, at)
                positive(pe, v_done, at)
                t = half * HALF + c * P
                mm(ps_k[:, 0:MIX_COLS], xT[0][:, t:t + P], wkv[:], start=True, stop=False)
                mm(ps_k[:, 0:MIX_COLS], ones3[:], bias_rows[:], start=False, stop=True).then_inc(k_ready, 1)

            def score(w, a, c):
                positive(pe, inner_done, 4 * w + c - 1)
                if c == 0:
                    pe.wait_ge(tables_used, 6 * w + 6)
                mm(ps_s[:, c % 2], k_chan[:, a % 2, c * P:(c + 1) * P], q_wide[:, a % 2, c], start=True, stop=True
                   ).then_inc(s_ready, 1)

            def chunk(n, a, c):
                w = 4 * n + a
                g, half, cc = a % 2, a // 2, 4 * (a // 2) + c
                s_now = start[:, g] if cc == 0 else state[:, g, cc % 2]
                at = state_index(n, a, c)
                if cc:
                    before = state_index(n, a, c - 1) if c else state_index(n, a - 2, CHUNKS - 1)
                    pe.wait_ge(st_done, before + 1)
                if c == 0:
                    pe.wait_ge(v_done, 8 * n + 4 * half + 4)
                    pe.wait_ge(k_done, 8 * n + 4 * half + 4)
                if at is not None:
                    positive(pe, st_done, at)
                    mm(ps_st[:], turn_m[:, g], s_now, start=True, stop=False)
                    mm(ps_st[:], k_tok[:, half, c, g * P:(g + 1) * P],
                       v_tok[:, half, c, g * GH:(g + 1) * GH].rearrange("p h x -> p (h x)"),
                       start=False, stop=True).then_inc(st_ready, 1)
                if c == 0:
                    positive(pe, o_copied, w)
                o = ps_o[:, c * P:(c + 1) * P]
                mm(o, s_now, q_state[:, a % 2, c * P:(c + 1) * P], start=True, stop=False, skip_group_check=True)
                pe.wait_ge(inner_done, 4 * w + c + 1)
                for j in range(GH):
                    last = mm(ps_o[32 * j:32 * j + 32, c * P:(c + 1) * P], v_tok[:, half, c, g * GH + j],
                              inner[:, c % 2, j * P:(j + 1) * P], start=False, stop=True, skip_group_check=True)
                last.then_inc(chunk_done, 1)

            def turn_item(w, a):
                pe.wait_ge(o_copied, w + 1)
                positive(pe, t_added, w)
                for c in range(CHUNKS):
                    last = nc.tensor.transpose(ps_t[:, c * P:(c + 1) * P], o_chan[:, a % 2, c * P:(c + 1) * P],
                                               ident[:])
                last.then_inc(o_turned, 1)

            def body(n):
                finish, prepare, _ = parts_of(n)
                if isinstance(n, int) and n < 0:
                    use_x(n, "xt0")
                    use_x(n, "xt1")
                for a, c, steps, nxt in slots(n):
                    w = 4 * n + a
                    if steps and c < CHUNKS - 1:
                        score(w, a, c + 1)
                    elif c == CHUNKS - 1 and nxt:
                        score(w + 1, (a + 1) % 4, 0)
                    if nxt and (a, c) == (3, 0):
                        pe.wait_ge(x_free, use(n, "xt1") + 1)
                    if nxt and c < 2:
                        project(w + 1, (a + 1) % 4, c)
                    if nxt and a % 2:
                        if a == 1:
                            mix(n, 1, c)
                        else:
                            mix(n + 1, 0, c)
                    if c == 1 and (finish if a == 0 else steps):
                        turn_item(w - 1, (a - 1) % 4)
                    for name in filled_at(n, a, c):
                        if not (isinstance(n, int) and n < 0):
                            use_x(n, name)
                    if steps:
                        chunk(n, a, c)

            images(pe, body)


def conv_attention_mixtures(nc, dram, out):
    with ExitStack() as ctx:
        sb, _, sem = allocator(nc, ctx)
        T = sb("tokens", [P, TOK])
        gates = sb("gates", [P, TILES * IMAGES * E])
        ident = sb("ident", [P, P])
        xT_dram = nc.dram_tensor("normalised_t", (P, TOK), F32, kind="Internal").ap()
        ident_zero = sem("ident_zero")

        with nc.Block() as block:
            @block.gpsimd
            def _(pool):
                nc.gpsimd.memset(ident[:], 0.0).then_inc(ident_zero, 1)
                pool.wait_ge(ident_zero, 1)
                nc.gpsimd.affine_select(out=ident[:], in_=ident[:], compare_op=ALU.not_equal, fill=1.0, base=0,
                                        pattern=[[-1, P]], channel_multiplier=1).then_inc(ident_zero, 1)
                pool.wait_ge(ident_zero, 2)

        convolution_stage(nc, T, ident, dram)
        attention_stage(nc, T, xT_dram, gates, ident, dram)
        mixture_stage(nc, T, xT_dram, gates, ident, dram["L2_ffn_W1"], dram["L2_ffn_b1"], dram["L2_ffn_W2"],
                      dram["L2_ffn_b2"], gated=True)
        decay_stage(nc, T, xT_dram, gates, ident, dram)
        mixture_stage(nc, T, xT_dram, gates, ident, dram["L3_ffn_W1"], dram["L3_ffn_b1"], dram["L3_ffn_W2"],
                      dram["L3_ffn_b2"], gated=False, out=out)


_INS = ["x", "L0_conv_w_channel", "L0_conv_w_spatial", "L0_conv_w_temporal", "L1_conv_w1", "L1_conv_w2",
        "L1_conv_fc1_w", "L1_conv_fc2_w", "L2_attn_Wq", "L2_attn_Wk", "L2_attn_Wv", "L2_attn_Wo", "L2_ffn_Wg",
        "L2_ffn_bg", "L2_ffn_W1", "L2_ffn_b1", "L2_ffn_W2", "L2_ffn_b2", "L3_attn_wq_w", "L3_attn_wq_b",
        "L3_attn_wk_w", "L3_attn_wk_b", "L3_attn_wv_w", "L3_attn_wv_b", "L3_attn_phazor_re",
        "L3_attn_phazor_im", "L3_attn_amplitude", "L3_attn_last_conv_re", "L3_attn_last_conv_im", "L3_ffn_Wg",
        "L3_ffn_bg", "L3_ffn_W1", "L3_ffn_b1", "L3_ffn_W2", "L3_ffn_b2"]
_OUTS = [((IMAGES, C, SIDE, SIDE), "float32")]


def kernel(**inputs):
    import numpy as _np
    import concourse.bacc as _bacc
    from concourse import mybir as _mybir
    from concourse.bass_utils import run_bass_kernel_spmd as _run

    nc = _bacc.Bacc("TRN2", target_bir_lowering=False, num_devices=1)
    arrays, dram, outs = {}, {}, []
    for name in _INS:
        a = _np.ascontiguousarray(inputs[name])
        arrays[f"in_{name}_dram"] = a
        dram[name] = nc.dram_tensor(f"in_{name}_dram", a.shape, _mybir.dt.from_np(a.dtype), kind="ExternalInput").ap()
    for i, (shape, dtype) in enumerate(_OUTS):
        dt = _mybir.dt.from_np(_np.dtype(dtype))
        outs.append(nc.dram_tensor(f"out_{i}_dram", shape, dt, kind="ExternalOutput").ap())
    conv_attention_mixtures(nc, dram, outs[0])
    r = _run(nc, [arrays], core_ids=[0])
    got = tuple(r.results[0][f"out_{i}_dram"] for i in range(len(_OUTS)))
    return got[0]
```

```python
from contextlib import ExitStack

import concourse.bass as bass
from concourse import mybir

F32 = mybir.dt.float32
BF16 = mybir.dt.bfloat16
U32 = mybir.dt.uint32
ALU = mybir.AluOpType
ACT = mybir.ActivationFunctionType
AX = mybir.AxisListType

P = 128
IMAGES = 16
C = 128
SIDE = 32
PX = SIDE * SIDE
TOK = IMAGES * PX
TILES = PX // P
HALF = 512
EPS_T = 1e-5
E = 8


def ds(at, n):
    return bass.ds(at, n)


def allocator(nc, ctx):
    semaphores = []

    def sb(name, shape, dt=F32):
        return ctx.enter_context(nc.sbuf_tensor(name, shape, dt))

    def ps(name, shape, dt=F32):
        return ctx.enter_context(nc.psum_tensor(name, shape, dt))

    def sem(name):
        semaphores.append(nc.alloc_semaphore(name))
        return semaphores[-1]

    def set_back():
        nc.clear_and_free_semaphores(semaphores)
        nc.all_engine_barrier()

    ctx.callback(set_back)

    return sb, ps, sem


def wait_apart(eng, s, value, passed):
    eng.wait_ge(s, value)
    eng.sem_inc(passed, 1)


TIME = 8
PER_STEP = IMAGES // TIME
TAPS = 5
EPS_G = 1e-5
CH_GROUP = 4
SQUEEZED = 8


def convolution_stage(nc, T, ident, dram):
    with ExitStack() as ctx:
        sb, ps, sem = allocator(nc, ctx)
        X = sb("a_x", [P, IMAGES * PX])
        spikes = sb("a_spikes", [P, IMAGES * PX], BF16)
        u = sb("a_u", [P, PER_STEP * PX])
        xh = T[:, 0:2 * PER_STEP * PX].rearrange("p (k x) -> p k x", k=2)
        strips = T[:, 2 * PER_STEP * PX:2 * PER_STEP * PX + IMAGES * SIDE * 4]
        wide = T[:, TOK // 2:TOK // 2 + P * TAPS].rearrange("p (o k) -> p o k", k=TAPS)
        stats = sb("a_stats", [P, IMAGES, 2, 6])
        mv = sb("a_mv", [P, IMAGES, 2])
        both = sb("a_both", [P, 2, IMAGES])
        group = sb("a_group", [P, P])
        tmp = sb("a_tmp", [P, IMAGES])
        scale = sb("a_scale", [P, IMAGES])
        shift = sb("a_shift", [P, IMAGES])
        mhalf = sb("a_mhalf", [P, IMAGES])
        eps = sb("a_eps", [P, IMAGES])
        zero = sb("a_zero", [P, IMAGES])
        counts = sb("a_counts", [P, IMAGES])
        average = sb("a_average", [P, IMAGES])
        picks = sb("a_picks", [P, 63], BF16)
        maps = sb("a_maps", [2 * IMAGES, 2, HALF])
        rows = sb("a_rows", [2 * SIDE, IMAGES, SIDE + TAPS - 1])
        ones = sb("a_ones", [P, TAPS, P])
        near = sb("a_near", [P, TAPS, P])
        near_y = sb("a_near_y", [2 * SIDE, TAPS, SIDE])
        w_ch = sb("a_w_ch", [P, TAPS])
        w_t = sb("a_w_t", [P, TAPS])
        w_sp = sb("a_w_sp", [2 * SIDE, TAPS * TAPS])
        wide_y = sb("a_wide_y", [2 * SIDE, TAPS, SIDE, TAPS])
        band_ch = sb("a_band_ch", [P, P])
        band_sp = sb("a_band_sp", [2 * SIDE, TAPS, SIDE])
        mean_all = sb("a_mean_all", [P, P])
        times = sb("a_times", [P, TIME + TAPS - 1, PER_STEP])
        temporal = sb("a_temporal", [P, IMAGES])
        factor = sb("a_factor", [P, IMAGES])
        sp_att = sb("a_sp_att", [SIDE, HALF])
        product = sb("a_product", [P, 2, HALF])
        kept = sb("a_kept", [P, 2, HALF])
        y4s = sb("a_y4s", [P, IMAGES, 16])
        pyr = sb("a_pyr", [P, 3, 16, IMAGES])
        y2h = sb("a_y2h", [P, 4, 2, IMAGES])
        y2 = sb("a_y2", [P, 2, 2, IMAGES])
        y1h = sb("a_y1h", [P, 2, IMAGES])
        w1 = sb("a_w1", [P, 27])
        w2 = sb("a_w2", [P, 9])
        z1 = sb("a_z1", [P, 4, IMAGES])
        z2 = sb("a_z2", [P, IMAGES])
        fc1 = sb("a_fc1", [P, SQUEEZED])
        fc2 = sb("a_fc2", [SQUEEZED, P])
        squeezed = sb("a_squeezed", [SQUEEZED, IMAGES])
        expo = sb("a_expo", [P, IMAGES])
        gate = sb("a_gate", [P, IMAGES])

        ps_small = ps("a_ps_small", [P, HALF])
        ps_maps = ps("a_ps_maps", [2 * IMAGES, HALF])
        ps_rows = ps("a_ps_rows", [SIDE, HALF])
        ps_big = ps("a_ps_big", [P, 2, HALF])
        map_dram = nc.dram_tensor("a_map", [2, IMAGES, PX], F32, kind="Internal").ap()

        x_in = [sem(f"a_x_in{t}") for t in range(TIME)]
        weights_in = sem("a_weights_in")
        const = sem("a_const")
        step = sem("a_step")
        moments = sem("a_moments")
        grouped = sem("a_grouped")
        variance = sem("a_variance")
        scale_step = sem("a_scale_step")
        xh_done = sem("a_xh_done")
        u_added = sem("a_u_added")
        spiked = sem("a_spiked")
        averaged = sem("a_averaged")
        att_sums = sem("a_att_sums")
        summed = sem("a_summed")
        maps_done = sem("a_maps_done")
        map_out = sem("a_map_out")
        rows_in = sem("a_rows_in")
        bands = sem("a_bands")
        rows_conv = sem("a_rows_conv")
        sp_done = sem("a_sp_done")
        spread = sem("a_spread")
        spread_used = sem("a_spread_used")
        kept_done = sem("a_kept_done")
        x_added = sem("a_x_added")
        pooled = sem("a_pooled")
        fc1_done = sem("a_fc1_done")
        relu_done = sem("a_relu_done")
        fc2_done = sem("a_fc2_done")
        exp_done = sem("a_exp_done")
        gated = sem("a_gated")
        flipped = sem("a_flipped")
        flip_used = sem("a_flip_used")
        passed = sem("a_passed")

        WEIGHTS = 7
        block = ctx.enter_context(nc.Block())

        @block.sync
        def _(sp):
            x_v = dram["x"].rearrange("(t i) c h w -> t c i (h w)", i=PER_STEP)
            for t in range(TIME):
                sp.dma_start(X[:, t * PER_STEP * PX:(t + 1) * PER_STEP * PX]
                             .rearrange("c (i p) -> c i p", p=PX), x_v[t]).then_inc(x_in[t], 16)
            sp.dma_start(w_ch[:], dram["L0_conv_w_channel"][0].broadcast_to([P, TAPS])).then_inc(weights_in, 16)
            sp.dma_start(w_t[:], dram["L0_conv_w_temporal"][0].broadcast_to([P, TAPS])).then_inc(weights_in, 16)
            w_sp_v = dram["L0_conv_w_spatial"].rearrange("a c h w -> a c (h w)")
            for c in range(2):
                sp.dma_start(w_sp[c * SIDE:(c + 1) * SIDE, :],
                             w_sp_v[:, c].broadcast_to([SIDE, TAPS * TAPS])).then_inc(weights_in, 16)
            sp.dma_start(w1[:], dram["L1_conv_w1"].rearrange("a c h w -> a (c h w)").broadcast_to([P, 27])
                         ).then_inc(weights_in, 16)
            sp.dma_start(w2[:], dram["L1_conv_w2"].rearrange("a c h w -> a (c h w)").broadcast_to([P, 9])
                         ).then_inc(weights_in, 16)
            with nc.allow_non_contiguous_dma("two small matrices, turned"):
                sp.dma_start(fc1[:], dram["L1_conv_fc1_w"].rearrange("r c -> c r")).then_inc(weights_in, 16)
                sp.dma_start(fc2[:], dram["L1_conv_fc2_w"].rearrange("c r -> r c")).then_inc(weights_in, 16)
            sp.wait_ge(maps_done, 2)
            sp.dma_start(map_dram.rearrange("m i (h p) -> (i h) m p", h=2), maps[:]).then_inc(map_out, 16)
            sp.wait_ge(map_out, 16)
            sp.wait_ge(const, 11)
            for m in range(2):
                sp.dma_start(rows[m * SIDE:(m + 1) * SIDE, :, 2:2 + SIDE],
                             map_dram[m].rearrange("i (y x) -> y i x", x=SIDE)).then_inc(rows_in, 16)

        @block.gpsimd
        def _(pool):
            steps = [0]

            def made(ins):
                steps[0] += 1
                ins.then_inc(const, 1)
                pool.wait_ge(const, steps[0])

            made(pool.memset(mhalf[:], -0.5))
            made(pool.memset(eps[:], EPS_G))
            made(pool.memset(zero[:], 0.0))
            made(pool.memset(ones[:], 1.0))
            made(pool.affine_select(out=near[:], in_=ones[:], compare_op=ALU.is_equal, fill=0.0, base=2,
                                    pattern=[[-1, TAPS], [-1, P]], channel_multiplier=1))
            for c in range(2):
                made(pool.affine_select(out=near_y[c * SIDE:(c + 1) * SIDE], in_=ones[c * SIDE:(c + 1) * SIDE, :, 0:SIDE],
                                        compare_op=ALU.is_equal, fill=0.0, base=2,
                                        pattern=[[-1, TAPS], [-1, SIDE]], channel_multiplier=1))
            made(pool.memset(group[:], 1.0 / CH_GROUP))
            gv = group[:].rearrange("p (g k) -> p g k", k=CH_GROUP)
            made(pool.affine_select(out=gv, in_=gv, compare_op=ALU.is_ge, fill=0.0, base=0,
                                    pattern=[[-CH_GROUP, P // CH_GROUP], [0, CH_GROUP]], channel_multiplier=1))
            made(pool.affine_select(out=gv, in_=gv, compare_op=ALU.is_ge, fill=0.0, base=CH_GROUP - 1,
                                    pattern=[[CH_GROUP, P // CH_GROUP], [0, CH_GROUP]], channel_multiplier=-1))
            made(pool.memset(rows[:], 0.0))
            made(pool.memset(times[:], 0.0))
            made(pool.memset(picks[:], 0.0))
            made(pool.memset(picks[:, 31:32], 1.0))
            made(pool.memset(mean_all[:], 1.0 / C))
            for norm in range(2):
                pool.wait_ge(variance, norm + 1)
                nc.gpsimd.tensor_tensor(tmp[:], tmp[:], eps[:], ALU.add).then_inc(scale_step, 1)
                pool.wait_ge(scale_step, 2 * norm + 1)
                nc.gpsimd.tensor_tensor(scale[:], tmp[:], mhalf[:], ALU.pow).then_inc(scale_step, 1)
                if norm == 0:
                    x_v = X[:].rearrange("c (i y x) -> c i (y x)", i=IMAGES, x=SIDE)
                    with pool.Fori(0, SIDE // 2) as pair:
                        for k in range(2):
                            y = 2 * pair + k
                            pool.wait_ge(kept_done, y + 1)
                            xs = x_v[:, :, ds(y * SIDE, SIDE)]
                            nc.gpsimd.tensor_tensor(xs, xs, kept[:, k].rearrange("c (i x) -> c i x", x=SIDE),
                                                    ALU.add).then_inc(x_added, 1)

        @block.vector
        def _(dve):
            count = [0]

            def link(ins):
                count[0] += 1
                ins.then_inc(step, 1)
                dve.wait_ge(step, count[0])

            def norm_scales(norm):
                link(nc.vector.tensor_copy(both[:, 0], mv[:, :, 0]))
                link(nc.vector.tensor_tensor(both[:, 1], mv[:, :, 0], mv[:, :, 0], ALU.mult))
                nc.vector.tensor_tensor(both[:, 1], both[:, 1], mv[:, :, 1], ALU.add).then_inc(moments, 1)
                dve.wait_ge(grouped, norm + 1)
                link(nc.vector.tensor_copy(shift[:], ps_small[:, 0:IMAGES]))
                link(nc.vector.tensor_tensor(tmp[:], shift[:], shift[:], ALU.mult))
                nc.vector.tensor_tensor(tmp[:], ps_small[:, IMAGES:2 * IMAGES], tmp[:], ALU.subtract
                                        ).then_inc(variance, 1)
                dve.wait_ge(scale_step, 2 * norm + 2)
                link(nc.vector.scalar_tensor_tensor(shift[:], shift[:], -1.0, scale[:], ALU.mult, ALU.mult))

            dve.wait_ge(weights_in, 16 * (WEIGHTS + 1))
            dve.wait_ge(const, 15)
            link(nc.vector.tensor_tensor(
                wide, near[:].rearrange("p k o -> p o k"),
                w_ch[:].rearrange("p (a k) -> p a k", a=1).broadcast_to([P, P, TAPS]), ALU.mult))
            link(nc.vector.tensor_reduce(band_ch[:], wide, AX.X, ALU.add))
            w_v = w_sp[:].rearrange("p (dy dx) -> p dx dy", dx=TAPS)
            for dx in range(TAPS):
                last = nc.vector.tensor_tensor(
                    wide_y[:, dx], near_y[:].rearrange("p k o -> p o k"),
                    w_v[:, dx:dx + 1, :].broadcast_to([2 * SIDE, SIDE, TAPS]), ALU.mult)
            link(last)
            nc.vector.tensor_reduce(band_sp[:], wide_y[:], AX.X, ALU.add).then_inc(bands, 1)

            for t in range(TIME):
                dve.wait_ge(x_in[t], 16)
                for i in range(t * PER_STEP, (t + 1) * PER_STEP):
                    for h in range(2):
                        last = nc.vector.bn_stats(stats[:, i, h], X[:, i * PX + h * HALF:i * PX + (h + 1) * HALF])
            link(last)
            for i in range(IMAGES):
                last = nc.vector.bn_aggr(mv[:, i], stats[:, i])
            link(last)
            norm_scales(0)
            nc.vector.tensor_copy(gate[:], scale[:]).then_inc(gated, 1)

            for t in range(TIME):
                dve.wait_ge(xh_done, PER_STEP * (t + 1))
                if t == 0:
                    nc.vector.tensor_copy(u[:], xh[:, 0]).then_inc(u_added, 1)
                else:
                    nc.vector.scalar_tensor_tensor(u[:], u[:], 0.5, xh[:, t % 2], ALU.mult, ALU.add
                                                   ).then_inc(u_added, 1)
                dve.wait_ge(u_added, t + 1)
                for k in range(PER_STEP):
                    i = t * PER_STEP + k
                    last = nc.vector.tensor_scalar(spikes[:, i * PX:(i + 1) * PX], u[:, k * PX:(k + 1) * PX],
                                                   1.0, 0.0, ALU.is_gt, ALU.add, accum_out=counts[:, i:i + 1])
                last.then_inc(spiked, 1)
                dve.wait_ge(spiked, t + 1)
                if t < TIME - 1:
                    link(nc.vector.tensor_tensor(
                        u[:], u[:], spikes[:, t * PER_STEP * PX:(t + 1) * PER_STEP * PX], ALU.subtract))

            nc.vector.tensor_scalar(average[:], counts[:], 1.0 / PX, None, ALU.mult).then_inc(averaged, 1)
            dve.wait_ge(summed, 1)
            nc.vector.tensor_scalar(maps[:, 0], ps_maps[:], 1.0 / C, None, ALU.mult).then_inc(maps_done, 1)
            nc.vector.tensor_scalar(maps[:, 1], ps_maps[:], 0.5, None, ALU.is_gt).then_inc(maps_done, 1)
            dve.wait_ge(att_sums, 1)
            link(nc.vector.tensor_copy(times[:, 2:2 + TIME, :],
                                       ps_small[:, 64:64 + IMAGES].rearrange("c (t b) -> c t b", b=PER_STEP)))
            for k in range(TAPS):
                window = times[:, k:k + TIME, :].rearrange("c t b -> c (t b)")
                if k == 0:
                    link(nc.vector.tensor_scalar(temporal[:], window, w_t[:, 0:1], None, ALU.mult))
                else:
                    link(nc.vector.scalar_tensor_tensor(temporal[:], window, w_t[:, k:k + 1], temporal[:],
                                                        ALU.mult, ALU.add))
            link(nc.vector.tensor_tensor(factor[:], temporal[:], ps_small[:, 96:96 + IMAGES], ALU.mult))
            dve.wait_ge(rows_conv, 1)
            nc.vector.tensor_copy(sp_att[:], ps_rows[:]).then_inc(sp_done, 1)

            s_v = spikes[:].rearrange("c (i p) -> c i p", i=IMAGES)
            f_v = factor[:].rearrange("c (i a) -> c i a", a=1).broadcast_to([P, IMAGES, SIDE])

            def keep_row(y, k, first):
                if not first:
                    dve.wait_ge(kept_done, y - 1)
                dve.wait_ge(spread, y + 1)
                nc.vector.tensor_tensor(product[:, k].rearrange("c (i x) -> c i x", x=SIDE),
                                        ps_big[:, k].rearrange("c (i x) -> c i x", x=SIDE), f_v,
                                        ALU.mult).then_inc(spread_used, 1)
                if not first:
                    dve.wait_ge(x_added, y - 1)
                dve.wait_ge(spread_used, y + 1)
                nc.vector.scalar_tensor_tensor(kept[:, k].rearrange("c (i x) -> c i x", x=SIDE),
                                               product[:, k].rearrange("c (i x) -> c i x", x=SIDE), 0.0,
                                               s_v[:, :, ds(y * SIDE, SIDE)], ALU.is_ge, ALU.mult
                                               ).then_inc(kept_done, 1)

            for y in range(2):
                keep_row(y, y, True)
            with dve.Fori(1, SIDE // 2) as pair:
                for k in range(2):
                    keep_row(2 * pair + k, k, False)
            dve.wait_ge(x_added, SIDE)

            with dve.Fori(0, IMAGES) as i:
                for h in range(2):
                    nc.vector.bn_stats(stats[:, ds(i, 1), h].rearrange("c a s -> c (a s)"),
                                       X[:, ds(i * PX + h * HALF, HALF)])
            link(nc.vector.tensor_reduce(strips, X[:].rearrange("c (s e) -> c s e", e=8), AX.X, ALU.add))
            for i in range(IMAGES):
                last = nc.vector.bn_aggr(mv[:, i], stats[:, i])
            link(last)
            sv = strips.rearrange("c (i b y x) -> c (i b) x y", b=4, y=8, x=4)
            link(nc.vector.tensor_reduce(y4s[:].rearrange("c i (b x) -> c (i b) x", x=4), sv, AX.X, ALU.add))
            norm_scales(1)
            sc = scale[:].rearrange("c (a i) -> c a i", a=1).broadcast_to([P, 16, IMAGES])
            sh = shift[:].rearrange("c (a i) -> c a i", a=1).broadcast_to([P, 16, IMAGES])
            link(nc.vector.scalar_tensor_tensor(pyr[:, 2], y4s[:].rearrange("c i q -> c q i"), 1.0 / 64, sc,
                                                ALU.mult, ALU.mult))
            link(nc.vector.tensor_tensor(pyr[:, 2], pyr[:, 2], sh, ALU.add))
            cells = pyr[:, 2].rearrange("c (y x) i -> c y x i", x=4)
            for x in range(2):
                last = nc.vector.tensor_tensor(y2h[:, :, x], cells[:, :, 2 * x], cells[:, :, 2 * x + 1], ALU.add)
            link(last)
            for y in range(2):
                last = nc.vector.tensor_tensor(y2[:, y], y2h[:, 2 * y], y2h[:, 2 * y + 1], ALU.add)
            link(last)
            link(nc.vector.tensor_tensor(y1h[:], y2[:, 0], y2[:, 1], ALU.add))
            link(nc.vector.tensor_tensor(tmp[:], y1h[:, 0], y1h[:, 1], ALU.add))
            link(nc.vector.tensor_scalar(pyr[:, 0], tmp[:].rearrange("c (a i) -> c a i", a=1)
                                         .broadcast_to([P, 16, IMAGES]), 1.0 / 16, None, ALU.mult))
            twos = pyr[:, 1].rearrange("c (y x) i -> c y x i", x=4)
            for y in range(4):
                for x in range(2):
                    last = nc.vector.tensor_scalar(
                        twos[:, y, 2 * x:2 * x + 2],
                        y2[:, y // 2, x:x + 1].broadcast_to([P, 2, IMAGES]), 0.25, None, ALU.mult)
            link(last)
            z_v = z1[:].rearrange("c (y x) i -> c y (x i)", x=2)
            for n in range(27):
                m, a, b = n // 9, n // 3 % 3, n % 3
                window = (pyr[:, m].rearrange("c (y x) i -> c y (x i)", x=4)
                          [:, a:a + 2, b * IMAGES:(b + 2) * IMAGES])
                if n == 0:
                    link(nc.vector.tensor_scalar(z_v, window, w1[:, 0:1], None, ALU.mult))
                else:
                    link(nc.vector.scalar_tensor_tensor(z_v, window, w1[:, n:n + 1], z_v, ALU.mult, ALU.add))
            for n in range(4):
                w = w2[:, 3 * (1 + n // 2) + 1 + n % 2:][:, 0:1]
                if n == 0:
                    ins = nc.vector.tensor_scalar(z2[:], z1[:, 0], w, None, ALU.mult)
                else:
                    ins = nc.vector.scalar_tensor_tensor(z2[:], z1[:, n], w, z2[:], ALU.mult, ALU.add)
                if n < 3:
                    link(ins)
            ins.then_inc(pooled, 1)
            dve.wait_ge(fc1_done, 1)
            nc.vector.tensor_scalar(squeezed[:], ps_small[0:SQUEEZED, 128:128 + IMAGES], 0.0, None, ALU.max
                                    ).then_inc(relu_done, 1)
            dve.wait_ge(exp_done, 1)
            link(nc.vector.tensor_scalar(expo[:], expo[:], 1.0, None, ALU.add))
            link(nc.vector.reciprocal(gate[:], expo[:]))
            link(nc.vector.tensor_tensor(scale[:], scale[:], gate[:], ALU.mult))
            link(nc.vector.tensor_scalar(scale[:], scale[:], 1.0, None, ALU.add))
            nc.vector.tensor_tensor(shift[:], shift[:], gate[:], ALU.mult).then_inc(gated, 1)
            dve.wait_ge(gated, 2)
            with dve.Fori(0, IMAGES) as i:
                xs = X[:, ds(i * PX, PX)]
                nc.vector.tensor_scalar(xs, xs, scale[:, ds(i, 1)], shift[:, ds(i, 1)], ALU.mult, ALU.add
                                        ).then_inc(kept_done, 1)

        @block.scalar
        def _(act):
            act.wait_ge(gated, 1)
            for t in range(TIME):
                if t >= 2:
                    act.wait_ge(u_added, t - 1)
                for k in range(PER_STEP):
                    i = t * PER_STEP + k
                    nc.scalar.activation(xh[:, t % 2, k * PX:(k + 1) * PX], X[:, i * PX:(i + 1) * PX], ACT.Identity,
                                         scale=scale[:, i:i + 1], bias=shift[:, i:i + 1]).then_inc(xh_done, 1)
            act.wait_ge(fc2_done, 1)
            nc.scalar.activation(expo[:], ps_small[:, 160:160 + IMAGES], ACT.Exp, scale=-1.0).then_inc(exp_done, 1)
            with act.Fori(0, IMAGES) as i:
                for h in range(2):
                    act.wait_ge(flipped, 2 * i + h + 1)
                    nc.scalar.activation(T[:, ds(i * PX + h * HALF, HALF)], ps_big[:, h], ACT.Copy
                                         ).then_inc(flip_used, 1)

        @block.tensor
        def _(pe):
            pe.wait_ge(const, 15)
            pe.wait_ge(moments, 1)
            nc.tensor.matmul(ps_small[:, 0:2 * IMAGES], group[:], both[:].rearrange("p a i -> p (a i)"),
                             start=True, stop=True).then_inc(grouped, 1)
            for n in range(2 * IMAGES):
                if n % (2 * PER_STEP) == 0:
                    pe.wait_ge(spiked, n // (2 * PER_STEP) + 1)
                last = nc.tensor.matmul(ps_maps[:], picks[:, 31 - n:63 - n],
                                        spikes[:, n * HALF:(n + 1) * HALF],
                                        start=(n == 0), stop=(n == 2 * IMAGES - 1))
            last.then_inc(summed, 1)
            pe.wait_ge(averaged, 1)
            pe.wait_ge(bands, 1)
            nc.tensor.matmul(ps_small[:, 64:64 + IMAGES], mean_all[:], average[:], start=True, stop=True)
            nc.tensor.matmul(ps_small[:, 96:96 + IMAGES], band_ch[:], average[:], start=True, stop=True
                             ).then_inc(att_sums, 1)
            pe.wait_ge(rows_in, 32)
            for dx in range(TAPS):
                last = nc.tensor.matmul(ps_rows[:], band_sp[:, dx], rows[:, :, dx:dx + SIDE],
                                        start=(dx == 0), stop=(dx == TAPS - 1))
            last.then_inc(rows_conv, 1)
            pe.wait_ge(sp_done, 1)

            def spread_row(y):
                nc.tensor.matmul(ps_big[:, y % 2], ident[0:SIDE, y:y + 1].broadcast_to([SIDE, P]), sp_att[:],
                                 start=True, stop=True).then_inc(spread, 1)

            for y in range(SIDE):
                if y >= 2:
                    pe.wait_ge(spread_used, y - 1)
                spread_row(y)
            pe.wait_ge(moments, 2)
            nc.tensor.matmul(ps_small[:, 0:2 * IMAGES], group[:], both[:].rearrange("p a i -> p (a i)"),
                             start=True, stop=True).then_inc(grouped, 1)
            pe.wait_ge(pooled, 1)
            nc.tensor.matmul(ps_small[0:SQUEEZED, 128:128 + IMAGES], fc1[:], z2[:], start=True, stop=True
                             ).then_inc(fc1_done, 1)
            pe.wait_ge(relu_done, 1)
            nc.tensor.matmul(ps_small[:, 160:160 + IMAGES], fc2[:], squeezed[:], start=True, stop=True
                             ).then_inc(fc2_done, 1)

            for i in range(IMAGES):
                pe.wait_ge(kept_done, SIDE + i + 1)
                for h in range(2):
                    if i:
                        pe.wait_ge(flip_used, 2 * i + h - 1)
                    for j in range(4):
                        c = i * PX + h * HALF + j * P
                        last = nc.tensor.transpose(ps_big[:, h, j * P:(j + 1) * P], X[:, c:c + P], ident[:])
                    last.then_inc(flipped, 1)


HEADS = 8
KV = 2
GROUP = HEADS // KV
DK = 16
STACK = 6 * DK
SPLIT_Q = (0, 0, 1, 0, 1, 2)
SPLIT_K = (0, 1, 0, 2, 1, 0)
STEPS = KV * 2 * TILES
MAXES = GROUP * TILES
MAX_FROM = 12
MAX_HALF = 16
MAX_PER_STEP = 2 * MAXES // MAX_HALF
STATS_AT, NORM_AT = 26, 29
STATS2_AT, NORM2_AT = 10, 13
GATE_AT = 20
FINISH_FILLS = {"wo0": 7, "wo1": 8, "x20": 15, "x21": 16, "logits": 17}
PREPARE_FILLS = {"xt0": 0, "xt1": 1, "q0": 2, "q1": 3, "k0": 4, "k1": 5, "v": 6, "mt0": MAX_FROM + MAX_HALF}
OWN_FILLS = {"mt1": MAX_FROM}
USES = len(FINISH_FILLS) + len(PREPARE_FILLS) + len(OWN_FILLS)


def attention_stage(nc, T, xT_dram, gates, ident, dram):
    with ExitStack() as ctx:
        sb, ps, sem = allocator(nc, ctx)
        wq = sb("b_wq", [P, C])
        wk = sb("b_wk", [P, KV * DK])
        wv = sb("b_wv", [P, KV * DK])
        wo = sb("b_wo", [P, KV, C])
        wg = sb("b_wg", [P, E])
        bg = sb("b_bg", [P, E])
        iota = sb("b_iota", [P, E])
        eps = sb("b_eps", [P, TILES])
        zero = sb("b_zero", [P, TILES])
        mhalf = sb("b_mhalf", [P, TILES])
        stats = [sb(f"b_stats{k}", [P, TILES, 6]) for k in range(2)]
        mv = [sb(f"b_mv{k}", [P, TILES, 2]) for k in range(2)]
        shift = [sb(f"b_shift{k}", [P, TILES]) for k in range(2)]
        rstd = [sb(f"b_rstd{k}", [P, TILES]) for k in range(2)]
        xn = [sb(f"b_xn{k}", [P, PX]) for k in range(2)]
        xT = [sb(f"b_xT{k}", [P, PX]) for k in range(2)]
        q_parts = sb("b_qparts", [P, 3, PX], BF16)
        k_parts = sb("b_kparts", [KV * DK, 3, PX], BF16)
        rest = sb("b_rest", [P, 2, HALF])
        qs = sb("b_qs", [P, 2, HEADS * PX], BF16)
        ks = sb("b_ks", [P, 2, KV * PX], BF16)
        vs = sb("b_vs", [P, 2, TILES, KV, 2 * DK])
        half_max = sb("b_halfmax", [P, KV, MAXES, 2])
        maxes = sb("b_maxes", [P, MAXES])
        m_parts = sb("b_mparts", [MAXES, 3, P], BF16)
        m_rest = sb("b_mrest", [MAXES, P])
        m_rest2 = sb("b_mrest2", [MAXES, P])
        probs = sb("b_probs", [P, 2, 2 * 2 * HALF])
        o_flip = sb("b_oflip", [P, HALF])
        o_scale = sb("b_oscale", [P, HALF // (2 * DK)])
        o_norm = sb("b_onorm", [P, KV, PX])
        logits = sb("b_logits", [P, TILES, E])
        top = sb("b_top", [P, TILES, 8])
        top_at = sb("b_topat", [P, TILES, 8], U32)
        top_atf = sb("b_topatf", [P, TILES, 2])
        gap = sb("b_gap", [P, TILES])
        expo = sb("b_expo", [P, TILES])
        gsum = sb("b_gsum", [P, TILES])
        w1 = sb("b_w1", [P, TILES])
        w2 = sb("b_w2", [P, TILES])
        hit = sb("b_hit", [P, 2, TILES, E])

        ps_s = ps("b_ps_s", [P, 2, 2 * HALF])
        ps_m = ps("b_ps_m", [P, 2, HALF])
        ps_o = ps("b_ps_o", [P, HALF])
        ps_x = ps("b_ps_x", [P, HALF])

        q_dram = nc.dram_tensor("b_q_parts", [2, 3, P, PX], BF16, kind="Internal").ap()
        k_dram = nc.dram_tensor("b_k_parts", [2, 3, KV * DK, PX], BF16, kind="Internal").ap()
        m_dram = nc.dram_tensor("b_m_parts", [2, 3, HEADS * PX], BF16, kind="Internal").ap()

        loaded = sem("b_loaded")
        wo_loaded = sem("b_wo_loaded")
        const = sem("b_const")
        passed = sem("b_passed")
        wo_zero = sem("b_wo_zero")
        stats_done = [sem(f"b_stats_done{k}") for k in range(2)]
        mv_done = [sem(f"b_mv_done{k}") for k in range(2)]
        rstd_done = [sem(f"b_rstd_done{k}") for k in range(2)]
        xn_done = [sem(f"b_xn_done{k}") for k in range(2)]
        xn_used = [sem(f"b_xn_used{k}") for k in range(2)]
        x_ready = sem("b_x_ready")
        x_free = sem("b_x_free")
        part1_done = sem("b_part1")
        rest_done = sem("b_rest_done")
        part2_done = sem("b_part2")
        part3_done = sem("b_part3")
        stacked = sem("b_stacked")
        spilled = sem("b_spilled")
        m_spilled = sem("b_m_spilled")
        v_done = sem("b_v_done")
        m_ready = sem("b_m_ready")
        m_free = sem("b_m_free")
        maxes_done = sem("b_maxes_done")
        mp_step = sem("b_mp_step")
        m_rows = sem("b_m_rows")
        s_ready = sem("b_s_ready")
        exp_done = sem("b_exp_done")
        pv_done = sem("b_pv_done")
        o_free = sem("b_o_free")
        o_done = sem("b_o_done")
        o_step = sem("b_o_step")
        t_added = sem("b_t_added")
        xT_copied = sem("b_xT_copied")
        g_step = sem("b_g_step")
        gap_exp = sem("b_gap_exp")

        def uses(n):
            finish, prepare, steps = parts_of(n)
            fills = FINISH_FILLS if finish else {}
            fills = fills | (PREPARE_FILLS if prepare else {}) | (OWN_FILLS if steps else {})
            ahead = len(PREPARE_FILLS)
            if isinstance(n, int) and n < 0:
                start = 0
            elif isinstance(n, int) and n == 0:
                start = ahead
            elif isinstance(n, int) and n == IMAGES:
                start = (n - 1) * USES + ahead + len(OWN_FILLS)
            else:
                start = (n - 1) * USES + 2 * ahead + len(OWN_FILLS)
            return start, fills

        def use(n, name):
            start, fills = uses(n)
            return start + sorted(fills, key=fills.get).index(name)

        def filled_at(n, s):
            return [name for name, step in uses(n)[1].items() if step == s]

        def positive(eng, s, value):
            if not (isinstance(value, int) and value <= 0):
                eng.wait_ge(s, value)

        def images(eng, body):
            body(-1, 1)
            body(0, 0)
            body(1, 1)
            body(2, 0)
            with eng.Fori(1, IMAGES // 2 - 2) as pair:
                body(2 * pair + 1, 1)
                body(2 * pair + 2, 0)
            body(IMAGES - 3, 1)
            body(IMAGES - 2, 0)
            body(IMAGES - 1, 1)
            body(IMAGES, 0)

        def parts_of(n):
            finish, prepare, steps = True, True, True
            if isinstance(n, int):
                finish, prepare, steps = n >= 1, n < IMAGES - 1, 0 <= n < IMAGES
            return finish, prepare, steps

        def max_units(n, s):
            prepare, steps = parts_of(n)[1:]
            if s >= MAX_FROM:
                if not prepare:
                    return []
                image, first, last = n + 1, s - MAX_FROM, s - MAX_FROM
                if not steps and s == MAX_FROM:
                    last = MAX_HALF - 1
                elif not steps and s < MAX_FROM + MAX_HALF:
                    return []
            elif not steps:
                return []
            else:
                image, first, last = n, STEPS + s - MAX_FROM, STEPS + s - MAX_FROM
            return [(image, i // (2 * MAXES), i % (2 * MAXES))
                    for i in range(first * MAX_PER_STEP, (last + 1) * MAX_PER_STEP)]

        def norm_ahead(n):
            return not (isinstance(n, int) and n + 2 >= IMAGES)

        block = ctx.enter_context(nc.Block())

        @block.sync
        def _(sp):
            sp.dma_start(wq[:], dram["L2_attn_Wq"]).then_inc(loaded, 16)
            sp.dma_start(wk[:], dram["L2_attn_Wk"]).then_inc(loaded, 16)
            sp.dma_start(wv[:], dram["L2_attn_Wv"]).then_inc(loaded, 16)
            sp.dma_start(wg[:], dram["L2_ffn_Wg"]).then_inc(loaded, 16)
            sp.dma_start(bg[:], dram["L2_ffn_bg"].rearrange("(a e) -> a e", a=1)
                         .broadcast_to([P, E])).then_inc(loaded, 16)
            sp.wait_ge(wo_zero, 1)
            wo_rows = dram["L2_attn_Wo"].rearrange("(h e) n -> h e n", e=DK)
            for h in range(HEADS):
                j = h % GROUP
                sp.dma_start(wo[32 * j:32 * j + DK, h // GROUP, :], wo_rows[h]).then_inc(wo_loaded, 16)

            def place_maxima(m, kv, buffer):
                n = 2 * m + kv
                cols = slice(kv * GROUP * PX, (kv + 1) * GROUP * PX)
                sp.wait_ge(mp_step, 5 * n + 5)
                sp.dma_start(m_dram[buffer, :, cols].rearrange("s (r q) -> r s q", q=P), m_parts[:]
                             ).then_inc(m_spilled, 16)
                sp.wait_ge(m_spilled, 16 * n + 16)
                sp.dma_start(qs[STACK:STACK + 3, buffer, cols], m_dram[buffer, :, cols]).then_inc(m_rows, 16)

            def body(n, parity):
                finish, prepare, steps = parts_of(n)
                m = n + 1
                other = 1 - parity
                if prepare:
                    sp.wait_ge(part3_done, 4 * m + 2)
                    sp.dma_start(q_dram[other].rearrange("s p t -> p s t"), q_parts[:]).then_inc(spilled, 16)
                    sp.wait_ge(part3_done, 4 * m + 4)
                    sp.dma_start(k_dram[other].rearrange("s p t -> p s t"), k_parts[:]).then_inc(spilled, 16)
                    sp.wait_ge(spilled, 32 * m + 32)
                    for g, part in enumerate(SPLIT_Q):
                        sp.dma_start(
                            qs[DK * g:DK * g + DK, other, :].rearrange("d (h t) -> d h t", h=HEADS),
                            q_dram[other, part].rearrange("(h d) t -> d h t", d=DK),
                        ).then_inc(stacked, 16)
                    for g, part in enumerate(SPLIT_K):
                        sp.dma_start(
                            ks[DK * g:DK * g + DK, other, :].rearrange("d (h t) -> d h t", h=KV),
                            k_dram[other, part].rearrange("(h d) t -> d h t", d=DK),
                        ).then_inc(stacked, 16)
                if steps:
                    place_maxima(n, 1, parity)
                if finish:
                    sp.wait_ge(x_free, use(n, "x21") + 1)
                    sp.dma_start(xT_dram[:, ds((n - 1) * PX, PX)], xT[1][:]).then_inc(xT_copied, 16)
                if prepare:
                    place_maxima(m, 0, other)

            images(sp, body)
            sp.wait_ge(xT_copied, 16 * IMAGES)

        @block.gpsimd
        def _(pool):
            pool.memset(wo[:], 0.0).then_inc(wo_zero, 1)
            pool.memset(mhalf[:], -0.5).then_inc(const, 1)
            pool.memset(eps[:], EPS_T).then_inc(const, 1)
            pool.memset(zero[:], 0.0).then_inc(const, 1)
            pool.memset(vs[:], 1.0).then_inc(const, 1)
            pool.wait_ge(const, 4)
            pool.memset(ks[STACK:P, :, :], 1.0).then_inc(const, 1)
            pool.wait_ge(const, 5)
            pool.iota(iota[:], [[1, E]], base=0, channel_multiplier=0,
                      allow_small_or_imprecise_dtypes=True).then_inc(const, 1)

            def scales(m, k):
                wait_apart(pool, mv_done[k], m + 1, passed)
                positive(pool, xn_done[k], TILES * m)
                nc.gpsimd.tensor_tensor(rstd[k][:], mv[k][:, :, 1], eps[:], ALU.add).then_inc(rstd_done[k], 1)
                pool.wait_ge(rstd_done[k], 4 * m + 1)
                nc.gpsimd.tensor_tensor(rstd[k][:], rstd[k][:], mhalf[:], ALU.pow).then_inc(rstd_done[k], 1)
                pool.wait_ge(rstd_done[k], 4 * m + 2)
                nc.gpsimd.tensor_tensor(shift[k][:], mv[k][:, :, 0], rstd[k][:], ALU.mult).then_inc(rstd_done[k], 1)
                pool.wait_ge(rstd_done[k], 4 * m + 3)
                nc.gpsimd.tensor_tensor(shift[k][:], zero[:], shift[k][:], ALU.subtract).then_inc(rstd_done[k], 1)

            def part_three(dst, rows, m, k, half):
                n = 4 * m + 2 * k + half
                cols = slice(half * HALF, half * HALF + HALF)
                wait_apart(pool, part2_done, n + 1, passed)
                nc.gpsimd.tensor_tensor(dst[:, 2, cols], rest[0:rows, half, :], dst[:, 1, cols],
                                        ALU.subtract).then_inc(part3_done, 1)

            def body(n, parity):
                finish, prepare, steps = parts_of(n)
                if isinstance(n, int) and n < 0:
                    scales(0, 0)
                if prepare:
                    for k, dst, rows in ((0, q_parts, P), (1, k_parts, KV * DK)):
                        for half in range(2):
                            part_three(dst, rows, n + 1, k, half)
                if finish:
                    scales(n - 1, 1)
                if norm_ahead(n):
                    scales(n + 2, 0)

            pool.wait_ge(const, 6)
            images(pool, body)

        @block.vector
        def _(dve):
            def statistics(m, k, half):
                for j in range(half * TILES // 2, (half + 1) * TILES // 2):
                    last = nc.vector.bn_stats(stats[k][:, j, :], T[:, ds(m * PX + j * P, P)])
                if half == 0:
                    return
                last.then_inc(stats_done[k], 1)
                positive(dve, xn_done[k], TILES * m)
                wait_apart(dve, stats_done[k], m + 1, passed)
                for j in range(TILES):
                    last = nc.vector.bn_aggr(mv[k][:, j, :], stats[k][:, j, :])
                last.then_inc(mv_done[k], 1)

            def left_over(dst, rows, m, k, half, n, name, scale):
                at = 4 * m + 2 * k + half
                dve.wait_ge(part1_done, at + 1)
                positive(dve, part3_done, at - 1)
                nc.vector.scalar_tensor_tensor(
                    rest[0:rows, half, :], ps_x[0:rows, :], scale,
                    dst[:, 0, half * HALF:half * HALF + HALF], ALU.mult, ALU.subtract,
                ).then_inc(rest_done, 1)
                dve.wait_ge(rest_done, at + 1)
                dve.sem_inc(x_free, 1)
                nc.vector.tensor_copy(dst[:, 1, half * HALF:half * HALF + HALF], rest[0:rows, half, :]
                                      ).then_inc(part2_done, 1)

            def reduce_unit(m, kv, u):
                wait_at = m * (4 * MAXES) + kv * 2 * MAXES + u
                dve.wait_ge(m_ready, wait_at + 1)
                nc.vector.tensor_reduce(half_max[:, kv, u // 2, u % 2:u % 2 + 1], ps_m[:, u % 2, :], AX.X,
                                        ALU.max).then_inc(m_free, 1)

            def out_of(n, g):
                kv, half = g // 2, g % 2
                dve.wait_ge(pv_done, STEPS * n + TILES * (g + 1))
                positive(dve, o_done, 4 * n + g)
                nc.vector.transpose(o_flip[:], ps_o[:]).then_inc(o_free, 1)

            def scale_out(n, g):
                kv, half = g // 2, g % 2
                dve.wait_ge(o_free, 4 * n + g + 1)
                block = o_flip[:].rearrange("p (b r) -> p b r", r=2 * DK)
                nc.vector.reciprocal(o_scale[:], block[:, :, DK]).then_inc(o_step, 1)
                dve.wait_ge(o_step, 8 * n + 2 * g + 1)
                nc.vector.tensor_tensor(
                    block, block, o_scale[:].rearrange("p (b a) -> p b a", a=1)
                    .broadcast_to([P, HALF // (2 * DK), 2 * DK]), ALU.mult).then_inc(o_step, 1)
                dve.wait_ge(o_step, 8 * n + 2 * g + 2)
                nc.vector.transpose(o_norm[:, kv, half * HALF:half * HALF + HALF], o_flip[:]).then_inc(o_done, 1)

            def add_out(n, half):
                dve.wait_ge(x_ready, use(n, f"wo{half}") + 1)
                tt = T[:, ds((n - 1) * PX + half * HALF, HALF)]
                nc.vector.tensor_tensor(tt, tt, ps_x[:], ALU.add).then_inc(t_added, 1)
                dve.wait_ge(t_added, 2 * (n - 1) + half + 1)
                dve.sem_inc(x_free, 1)

            def gate(n):
                m = n - 1
                g0 = 9 * m
                dve.wait_ge(x_ready, use(n, "logits") + 1)
                nc.vector.tensor_tensor(
                    logits[:], ps_x[:, 0:TILES * E].rearrange("p (t e) -> p t e", e=E),
                    bg[:].rearrange("p (a e) -> p a e", a=1).broadcast_to([P, TILES, E]),
                    ALU.add).then_inc(g_step, 1)
                dve.wait_ge(g_step, g0 + 1)
                dve.sem_inc(x_free, 1)
                for j in range(TILES):
                    last = nc.vector.max(top[:, j, :], logits[:, j, :])
                last.then_inc(g_step, 1)
                dve.wait_ge(g_step, g0 + 2)
                nc.vector.tensor_tensor(gap[:], top[:, :, 1], top[:, :, 0], ALU.subtract).then_inc(g_step, 1)
                for j in range(TILES):
                    last = nc.vector.max_index(top_at[:, j, :], top[:, j, :], logits[:, j, :])
                last.then_inc(g_step, 1)
                dve.wait_ge(g_step, g0 + 4)
                nc.vector.tensor_copy(top_atf[:], top_at[:, :, 0:2]).then_inc(g_step, 1)

            def gate_weights(n):
                m = n - 1
                g0 = 9 * m
                dve.wait_ge(gap_exp, m + 1)
                nc.vector.tensor_scalar(gsum[:], expo[:], 1.0, None, ALU.add).then_inc(g_step, 1)
                dve.wait_ge(g_step, g0 + 6)
                nc.vector.reciprocal(w1[:], gsum[:]).then_inc(g_step, 1)
                for k in range(2):
                    nc.vector.tensor_tensor(
                        hit[:, k], iota[:].rearrange("p (a e) -> p a e", a=1).broadcast_to([P, TILES, E]),
                        top_atf[:, :, k:k + 1].broadcast_to([P, TILES, E]), ALU.is_equal)
                dve.wait_ge(g_step, g0 + 7)
                nc.vector.tensor_tensor(w2[:], w1[:], expo[:], ALU.mult).then_inc(g_step, 1)
                dve.wait_ge(g_step, g0 + 8)
                for k, w in ((0, w1), (1, w2)):
                    last = nc.vector.tensor_tensor(
                        hit[:, k], hit[:, k],
                        w[:].rearrange("p (t a) -> p t a", a=1).broadcast_to([P, TILES, E]), ALU.mult)
                last.then_inc(g_step, 1)
                dve.wait_ge(g_step, g0 + 9)
                nc.vector.tensor_tensor(
                    gates[:, ds(m * TILES * E, TILES * E)],
                    hit[:, 0].rearrange("p t e -> p (t e)"), hit[:, 1].rearrange("p t e -> p (t e)"), ALU.add)

            def minus_maxima(n, m, kv):
                g0 = 5 * (2 * m + kv)
                dve.wait_ge(x_ready, use(n, f"mt{kv}") + 1)
                positive(dve, m_rows, 16 * (2 * m + kv))
                nc.vector.tensor_scalar(m_parts[:, 0, :], ps_x[0:MAXES, 0:P], -1.0, None,
                                        ALU.mult).then_inc(mp_step, 1)
                dve.wait_ge(mp_step, g0 + 1)
                nc.vector.scalar_tensor_tensor(m_rest[:], ps_x[0:MAXES, 0:P], -1.0, m_parts[:, 0, :],
                                               ALU.mult, ALU.subtract).then_inc(mp_step, 1)
                dve.wait_ge(mp_step, g0 + 2)
                dve.sem_inc(x_free, 1)
                nc.vector.tensor_copy(m_parts[:, 1, :], m_rest[:]).then_inc(mp_step, 1)
                dve.wait_ge(mp_step, g0 + 3)
                nc.vector.tensor_tensor(m_rest2[:], m_rest[:], m_parts[:, 1, :], ALU.subtract).then_inc(mp_step, 1)
                dve.wait_ge(mp_step, g0 + 4)
                nc.vector.tensor_copy(m_parts[:, 2, :], m_rest2[:]).then_inc(mp_step, 1)

            def whole_maxima(m, kv):
                dve.wait_ge(m_free, m * (4 * MAXES) + (kv + 1) * 2 * MAXES)
                nc.vector.tensor_tensor(maxes[:], half_max[:, kv, :, 0], half_max[:, kv, :, 1],
                                        ALU.max).then_inc(maxes_done, 1)

            def read_out(n, name):
                m = n + 1
                if name[:2] == "wo":
                    add_out(n, int(name[2]))
                elif name[0] == "q":
                    left_over(q_parts, P, m, 0, int(name[1]), n, name, DK ** -0.5)
                elif name[0] == "k":
                    left_over(k_parts, KV * DK, m, 1, int(name[1]), n, name, 1.0)
                elif name == "logits":
                    gate(n)
                elif name == "mt1":
                    minus_maxima(n, n, 1)
                elif name == "mt0":
                    minus_maxima(n, m, 0)

            def body(n, parity):
                finish, prepare, steps = parts_of(n)
                m = n + 1
                if isinstance(n, int) and n < 0:
                    statistics(0, 0, 0)
                    statistics(0, 0, 1)
                for s in range(STEPS):
                    units = max_units(n, s)
                    for unit in units[:2]:
                        reduce_unit(*unit)
                    for name in filled_at(n, s - 1):
                        read_out(n, name)
                    for unit in units[2:]:
                        reduce_unit(*unit)
                    if s in (STATS2_AT, STATS2_AT + 1) and finish:
                        statistics(n - 1, 1, s - STATS2_AT)
                    if s in (STATS_AT, STATS_AT + 1) and norm_ahead(n):
                        statistics(n + 2, 0, s - STATS_AT)
                    if s == GATE_AT and finish:
                        gate_weights(n)
                    if s == MAX_FROM - 1 and steps:
                        whole_maxima(n, 1)
                    if s == MAX_FROM + MAX_HALF - 1 and prepare:
                        whole_maxima(m, 0)
                    if steps and s and s % TILES == 0:
                        out_of(n, s // TILES - 1)
                    if (s - 1) % TILES == 0 and (s > 1 and steps or s == 1 and finish):
                        scale_out(*((n, s // TILES - 1) if s > 1 else (n - 1, STEPS // TILES - 1)))
                if steps:
                    out_of(n, STEPS // TILES - 1)

            dve.wait_ge(loaded, 16 * 5)
            dve.wait_ge(const, 6)
            images(dve, body)

        @block.scalar
        def _(act):
            def evacuate(n, name, dst):
                u = use(n, name)
                act.wait_ge(x_ready, u + 1)
                nc.scalar.activation(dst, ps_x[:], ACT.Copy).then_inc(x_free, 1)

            def normalise(m, k, half):
                if half == 0:
                    act.wait_ge(rstd_done[k], 4 * m + 4)
                    positive(act, xn_used[k], m)
                for j in range(half * TILES // 2, (half + 1) * TILES // 2):
                    nc.scalar.activation(xn[k][:, j * P:(j + 1) * P], T[:, ds(m * PX + j * P, P)], ACT.Identity,
                                         scale=rstd[k][:, j:j + 1], bias=shift[k][:, j:j + 1],
                                         ).then_inc(xn_done[k], 1)

            def part_one(dst, rows, m, k, half, n, name, scale):
                act.wait_ge(x_ready, use(n, name) + 1)
                positive(act, stacked, 192 * m)
                nc.scalar.activation(dst[:, 0, half * HALF:half * HALF + HALF], ps_x[0:rows, :], ACT.Copy,
                                     scale=scale).then_inc(part1_done, 1)

            def read_out(n, name, other):
                m = n + 1
                if name[:2] == "xt":
                    half = int(name[2])
                    evacuate(n, name, xT[0][:, half * HALF:half * HALF + HALF])
                elif name[:2] == "x2":
                    half = int(name[2])
                    if half == 0:
                        positive(act, xT_copied, 16 * (n - 1))
                    evacuate(n, name, xT[1][:, half * HALF:half * HALF + HALF])
                elif name[0] == "q":
                    part_one(q_parts, P, m, 0, int(name[1]), n, name, DK ** -0.5)
                elif name[0] == "k":
                    part_one(k_parts, KV * DK, m, 1, int(name[1]), n, name, 1.0)
                elif name == "v":
                    act.wait_ge(x_ready, use(n, "v") + 1)
                    nc.scalar.activation(
                        vs[:, other, :, :, 0:DK],
                        ps_x[:, 0:TILES * KV * DK].rearrange("p (t k d) -> p t k d", k=KV, d=DK),
                        ACT.Copy).then_inc(v_done, 1)
                    act.wait_ge(v_done, m + 1)
                    act.sem_inc(x_free, 1)

            def body(n, parity):
                finish, prepare, steps = parts_of(n)
                m = n + 1
                if isinstance(n, int) and n < 0:
                    normalise(0, 0, 0)
                    normalise(0, 0, 1)
                for s in range(STEPS):
                    for name in filled_at(n, s - 1):
                        read_out(n, name, 1 - parity)
                    for at, there, image, k in ((NORM_AT, norm_ahead(n), n + 2, 0), (NORM2_AT, finish, n - 1, 1)):
                        if there and s in (at, at + 1):
                            normalise(image, k, s - at)
                    if s == FINISH_FILLS["logits"] + 2 and finish:
                        act.wait_ge(g_step, 9 * (n - 1) + 3)
                        nc.scalar.activation(expo[:], gap[:], ACT.Exp).then_inc(gap_exp, 1)
                    if steps:
                        for pair in range(2):
                            v = 2 * s + pair
                            act.wait_ge(s_ready, 2 * STEPS * n + v + 1)
                            positive(act, pv_done, STEPS * n + s - 1)
                            nc.scalar.activation(
                                probs[:, s % 2, pair * 2 * HALF:(pair + 1) * 2 * HALF], ps_s[:, pair, :],
                                ACT.Exp).then_inc(exp_done, 1)

            act.wait_ge(const, 6)
            images(act, body)

        @block.tensor
        def _(pe):
            def fill(n, name):
                positive(pe, x_free, use(n, name))

            def transposes(n, m, k, name, half):
                pe.wait_ge(xn_done[k], TILES * m + 4 * (half + 1))
                fill(n, name)
                for j in range(4):
                    c = half * HALF + j * P
                    last = nc.tensor.transpose(ps_x[:, j * P:(j + 1) * P], xn[k][:, c:c + P], ident[:])
                last.then_inc(x_ready, 1)
                if half:
                    pe.wait_ge(x_ready, use(n, name) + 1)
                    pe.sem_inc(xn_used[k], 1)

            def project(n, w, rows, name, half):
                fill(n, name)
                nc.tensor.matmul(ps_x[0:rows, :], w[:], xT[0][:, half * HALF:half * HALF + HALF],
                                 start=True, stop=True).then_inc(x_ready, 1)

            def max_unit(m, kv, u, buffer):
                h, qt, half = kv * GROUP + u // 2 // TILES, u // 2 % TILES, u % 2
                positive(pe, m_free, m * (4 * MAXES) + kv * 2 * MAXES + u - 1)
                nc.tensor.matmul(
                    ps_m[:, u % 2, :], qs[0:STACK, buffer, h * PX + qt * P:h * PX + qt * P + P],
                    ks[0:STACK, buffer, kv * PX + half * HALF:kv * PX + half * HALF + HALF],
                    start=True, stop=True).then_inc(m_ready, 1)

            def scores(n, s, parity, pair):
                g, tt = s // TILES, s % TILES
                kv, half = g // 2, g % 2
                rows = STACK + 3
                positive(pe, exp_done, 2 * STEPS * n + 2 * s + pair - 1)
                for j in range(2):
                    h = kv * GROUP + 2 * pair + j
                    last = nc.tensor.matmul(
                        ps_s[:, pair, j * HALF:(j + 1) * HALF],
                        ks[0:rows, parity, kv * PX + tt * P:kv * PX + tt * P + P],
                        qs[0:rows, parity, h * PX + half * HALF:h * PX + half * HALF + HALF],
                        start=True, stop=True)
                last.then_inc(s_ready, 1)

            def products(n, s, parity, part):
                cols = slice(part * HALF // 2, (part + 1) * HALF // 2)
                g, tt = s // TILES, s % TILES
                pe.wait_ge(exp_done, 2 * STEPS * n + 2 * s + 2)
                if tt == 0 and part == 0:
                    positive(pe, o_free, 4 * n + g)
                for j in range(GROUP):
                    last = nc.tensor.matmul(
                        ps_o[32 * j:32 * j + 32, cols], vs[:, parity, tt, g // 2, :],
                        probs[:, s % 2, j * HALF:(j + 1) * HALF][:, cols],
                        start=(tt == 0 and part == 0), stop=(tt == TILES - 1), skip_group_check=True)
                if part:
                    last.then_inc(pv_done, 1)

            def use_x(n, name):
                m = n + 1
                half = int(name[-1]) if name[-1] in "01" else 0
                if name[:2] == "wo":
                    pe.wait_ge(o_done, 4 * n)
                    fill(n, name)
                    for j in range(4):
                        c = half * HALF + j * P
                        for kv in range(KV):
                            last = nc.tensor.matmul(
                                ps_x[:, j * P:(j + 1) * P], o_norm[:, kv, c:c + P], wo[:, kv, :],
                                start=(kv == 0), stop=(kv == KV - 1))
                    last.then_inc(x_ready, 1)
                elif name[:2] == "xt":
                    transposes(n, m, 0, name, half)
                elif name[:2] == "x2":
                    transposes(n, n - 1, 1, name, half)
                elif name[0] == "q":
                    project(n, wq, P, name, half)
                elif name[0] == "k":
                    project(n, wk, KV * DK, name, half)
                elif name == "v":
                    fill(n, "v")
                    w = KV * DK
                    for j in range(TILES):
                        last = nc.tensor.matmul(ps_x[:, j * w:(j + 1) * w], xT[0][:, j * P:(j + 1) * P],
                                                wv[:], start=True, stop=True)
                    last.then_inc(x_ready, 1)
                elif name == "logits":
                    fill(n, "logits")
                    for j in range(TILES):
                        last = nc.tensor.matmul(ps_x[:, j * E:(j + 1) * E], xT[1][:, j * P:(j + 1) * P],
                                                wg[:], start=True, stop=True)
                    last.then_inc(x_ready, 1)
                else:
                    fill(n, name)
                    wait_apart(pe, maxes_done, 2 * n + 2 if name == "mt1" else 2 * m + 1, passed)
                    nc.tensor.transpose(ps_x[0:MAXES, 0:P], maxes[:], ident[:]).then_inc(x_ready, 1)

            def body(n, parity):
                finish, prepare, steps = parts_of(n)
                if steps:
                    pe.wait_ge(m_rows, 16 * (2 * n + 1))
                    pe.wait_ge(v_done, n + 1)
                for s in range(STEPS + 1):
                    if steps and s == STEPS // 2:
                        pe.wait_ge(m_rows, 16 * (2 * n + 2))
                    if prepare and s == MAX_FROM:
                        pe.wait_ge(stacked, 192 * (n + 2))
                    buffer = 1 - parity if s >= MAX_FROM else parity
                    between = [unit + (buffer,) for unit in max_units(n, s)] if s < STEPS else []
                    for pair in range(2 if steps and s < STEPS else 0):
                        for unit in between[:1]:
                            max_unit(*unit)
                        del between[:1]
                        scores(n, s, parity, pair)
                    for part in range(2 if steps and s else 0):
                        for unit in between[:1]:
                            max_unit(*unit)
                        del between[:1]
                        products(n, s - 1, parity, part)
                    if s == STEPS:
                        break
                    for unit in between:
                        max_unit(*unit)
                    for name in filled_at(n, s):
                        use_x(n, name)

            pe.wait_ge(const, 6)
            pe.wait_ge(loaded, 16 * 5)
            pe.wait_ge(wo_loaded, 16 * HEADS)
            images(pe, body)


BT = HALF // P
F32R = mybir.dt.float32r
SET_UP = {True: 3 + E + 4, False: 3 + 2 * E + 4}
G_ROWS = 3 * E


def mixture_stage(nc, T, xT_dram, gates, ident, W1, b1, W2, b2, gated, out=None):
    hidden = W2.shape[1]
    rest = hidden - P
    if gated:
        sets, set_units, per_unit, units_of_gate = E, 2, 2, 2
        ring_h, ring_a, lag = 2, 8, 4
    else:
        sets, set_units, per_unit, units_of_gate = E // 2, 3, 1, 1
        ring_h, ring_a, lag = 4, 6, 4
    n_units = sets * set_units
    n_bias = n_units * per_unit
    n_gates = n_units // units_of_gate
    TURN_AT, GATES_AT, NEXT_X_AT = lag + 1, lag + 2, n_units - 3
    HIGH_DELAY = 2 if gated else 1
    pre = "c" if gated else "e"
    RING, STAGING = 4, 2

    with ExitStack() as ctx:
        sb, ps, sem = allocator(nc, ctx)
        w1_in = sb(pre + "_w1_in", [P, STAGING, set_units, per_unit, P])
        w2_in = sb(pre + "_w2_in", [P, STAGING, set_units, C])
        w1_hi, w1_lo = [sb(f"{pre}_w1_{part}", [P, n_units, per_unit, P], F32R) for part in ("hi", "lo")]
        w2_hi, w2_lo = [sb(f"{pre}_w2_{part}", [P, n_units, C], F32R) for part in ("hi", "lo")]
        bias_in = sb(pre + "_bias_in", [n_bias, P])
        bias = sb(pre + "_bias", [P, n_bias])
        b2_in = sb(pre + "_b2_in", [G_ROWS, C])
        b2_hi = sb(pre + "_b2_hi", [G_ROWS, C], F32R)
        b2_lo = sb(pre + "_b2_lo", [G_ROWS, C], F32R)
        b2_own = sb(pre + "_b2_own", [G_ROWS, C], F32R)
        b2_rows = sb(pre + "_b2_rows", [G_ROWS, C], F32R)
        is_rows = sb(pre + "_is_rows", [G_ROWS, 3])
        not_rows = sb(pre + "_not_rows", [G_ROWS, 3])
        own_expert = sb(pre + "_own_expert", [G_ROWS, E])
        spread = sb(pre + "_spread", [G_ROWS, n_gates, P], F32R)
        xb = sb(pre + "_xb", [P, 2, HALF])
        x_hi = sb(pre + "_x_hi", [P, 2, HALF], F32R)
        x_lo = sb(pre + "_x_lo", [P, 2, HALF], F32R)
        g_laid = sb(pre + "_g_laid", [P, BT, 3, E])
        g_hi = sb(pre + "_g_hi", [G_ROWS, HALF], F32R)
        g_lo = sb(pre + "_g_lo", [G_ROWS, HALF], F32R)
        g_own = sb(pre + "_g_own", [G_ROWS, HALF], F32R)
        g_rows = sb(pre + "_g_rows", [G_ROWS, 2, HALF], F32R)
        half_way = sb(pre + "_half_way", [P, 2, HALF]) if gated else None
        act_buf = sb(pre + "_act", [P, RING, HALF])
        act_hi = sb(pre + "_act_hi", [P, ring_a, HALF], F32R)
        act_lo = sb(pre + "_act_lo", [P, ring_a, HALF], F32R)
        total = sb(pre + "_total", [P, 2, HALF])
        t_copy = sb(pre + "_t_copy", [P, 2, HALF]) if out is not None else None
        ps_h = ps(pre + "_ps_h", [P, ring_h, per_unit, HALF])
        ps_g = ps(pre + "_ps_g", [P, 2, HALF])
        ps_y = ps(pre + "_ps_y", [P, 2, HALF])

        w_in = [sem(f"{pre}_w_in{k}") for k in range(STAGING)]
        w_hi_done = sem(pre + "_w_hi_done")
        w_lo_done = sem(pre + "_w_lo_done")
        bias_loaded = sem(pre + "_bias_loaded")
        bias_turned = sem(pre + "_bias_turned")
        bias_ready = sem(pre + "_bias_ready")
        b2_loaded = sem(pre + "_b2_loaded")
        set_up = sem(pre + "_set_up")
        x_in = [sem(f"{pre}_x_in{k}") for k in range(2)]
        x_hi_done = sem(pre + "_x_hi_done")
        x_lo_done = sem(pre + "_x_lo_done")
        g_laid_done = sem(pre + "_g_laid_done")
        g_turned = sem(pre + "_g_turned")
        g_step = sem(pre + "_g_step")
        g_ready = sem(pre + "_g_ready")
        h_ready = sem(pre + "_h_ready")
        half_done = sem(pre + "_half_done")
        a_ready = sem(pre + "_a_ready")
        weighed = sem(pre + "_weighed")
        hi_done = sem(pre + "_hi_done")
        lo_done = sem(pre + "_lo_done")
        y_used = sem(pre + "_y_used")
        y_ready = sem(pre + "_y_ready")
        y_copied = sem(pre + "_y_copied")
        y_turned = sem(pre + "_y_turned")
        t_added = sem(pre + "_t_added")
        t_copied = sem(pre + "_t_copied")
        out_sent = [sem(f"{pre}_out_sent{k}") for k in range(2)]

        def positive(eng, s, value):
            if not (isinstance(value, int) and value <= 0):
                eng.wait_ge(s, value)

        def blocks(eng, body):
            for k in range(2):
                body(0, k)
            for k in range(2):
                body(1, k)
            with eng.Fori(2, IMAGES - 1) as image:
                for k in range(2):
                    body(image, k)
            for k in range(2):
                body(IMAGES - 1, k)

        def number(image, k):
            return 2 * image + k

        def before(image, k):
            if k:
                return image, 0
            return None if isinstance(image, int) and image == 0 else (image - 1, 1)

        def after(image, k):
            if k == 0:
                return image, 1
            return None if isinstance(image, int) and image == IMAGES - 1 else (image + 1, 0)

        def late(image, k, u, delay, step):
            if u >= delay:
                step(image, k, u - delay)
            elif before(image, k):
                step(*before(image, k), n_units + u - delay)

        def tail(delay, step):
            for u in range(n_units - delay, n_units):
                step(IMAGES - 1, 1, u)

        def bias_column(u, t):
            at = 4 * (u // 2) + 2 * t + u % 2 if gated else u
            return slice(at, at + 1)

        def high_part(eng, copy, image, k, u):
            at = number(image, k) * n_units + u
            positive(eng, y_used, at - ring_a + 1)
            eng.wait_ge(weighed, at + 1)
            copy(act_hi[:, u % ring_a], act_buf[:, u % RING]).then_inc(hi_done, 1)

        block = ctx.enter_context(nc.Block())
        loads = 3 if gated else 5
        bias_loads = 1 if gated else E

        @block.sync
        def _(sp):
            def load_x(image, k):
                b = number(image, k)
                positive(sp, x_lo_done, b - 1)
                sp.dma_start(xb[:, k], xT_dram[:, ds(b * HALF, HALF)]).then_inc(x_in[k], 16)

            def load_set(s):
                k = s % STAGING
                positive(sp, w_lo_done, s - STAGING + 1)
                if gated:
                    for t in range(2):
                        sp.dma_start(w1_in[:, k, :, t], W1[s][:, t * hidden:(t + 1) * hidden].rearrange(
                            "p (u m) -> p u m", u=2)).then_inc(w_in[k], 16)
                    sp.dma_start(w2_in[:, k], W2[s].rearrange("(u p) c -> p u c", p=P)).then_inc(w_in[k], 16)
                    return
                e = 2 * s
                sp.dma_start(w1_in[:, k, 0:2, 0], W1[e:e + 2, :, 0:P].rearrange("k p m -> p k m")
                             ).then_inc(w_in[k], 16)
                sp.dma_start(w1_in[:, k, 2, 0].rearrange("p (k m) -> p k m", k=2),
                             W1[e:e + 2, :, P:hidden].rearrange("k p m -> p k m")).then_inc(w_in[k], 16)
                sp.dma_start(w2_in[:, k, 0:2], W2[e:e + 2, 0:P].rearrange("k p c -> p k c")).then_inc(w_in[k], 16)
                for i in range(2):
                    sp.dma_start(w2_in[i * rest:(i + 1) * rest, k, 2], W2[e + i, P:hidden]).then_inc(w_in[k], 16)

            def send(image, k):
                sp.wait_ge(y_copied, number(image, k) + 1)
                sp.dma_start(out.rearrange("i c y x -> c i (y x)")[:, ds(image, 1), k * HALF:(k + 1) * HALF],
                             total[:, k].rearrange("c (a p) -> c a p", a=1)).then_inc(out_sent[k], 16)

            def body(image, k):
                if not (isinstance(image, int) and image == 0):
                    load_x(image, k)
                if out is not None and before(image, k):
                    send(*before(image, k))

            load_set(0)
            load_x(0, 0)
            if gated:
                sp.dma_start(bias_in[:], b1.rearrange("e (t m) -> (e t) m", m=P)).then_inc(bias_loaded, 16)
            else:
                for pair in range(sets):
                    e, at = 2 * pair, 3 * pair
                    sp.dma_start(bias_in[at:at + 2], b1[e:e + 2, 0:P]).then_inc(bias_loaded, 16)
                    sp.dma_start(bias_in[at + 2:at + 3].rearrange("a (k h) -> a k h", k=2),
                                 b1[e:e + 2, P:hidden].rearrange("(a k) h -> a k h", a=1)).then_inc(bias_loaded, 16)
            for third in range(3):
                sp.dma_start(b2_in[third * E:(third + 1) * E], b2).then_inc(b2_loaded, 16)
            load_set(1)
            load_x(0, 1)
            for s in range(2, sets):
                load_set(s)
            blocks(sp, body)
            if out is not None:
                send(IMAGES - 1, 1)
                for k in range(2):
                    sp.wait_ge(out_sent[k], 16 * IMAGES)

        @block.gpsimd
        def _(pool):
            def body(image, k):
                b = number(image, k)
                for u in range(n_units):
                    pool.wait_ge(hi_done, b * n_units + u + 1)
                    nc.gpsimd.tensor_tensor(act_lo[:, u % ring_a], act_buf[:, u % RING], act_hi[:, u % ring_a],
                                            ALU.subtract).then_inc(lo_done, 1)

            blocks(pool, body)

        @block.vector
        def _(dve):
            steps = [0]

            def link(ins):
                steps[0] += 1
                ins.then_inc(set_up, 1)
                dve.wait_ge(set_up, steps[0])

            def set_rest(s):
                units = slice(s * set_units, (s + 1) * set_units)
                dve.wait_ge(w_hi_done, s + 1)
                nc.vector.tensor_tensor(w2_lo[:, units], w2_in[:, s % STAGING], w2_hi[:, units], ALU.subtract)
                nc.vector.tensor_tensor(
                    w1_lo[:, units].rearrange("p u t m -> p (u t m)"),
                    w1_in[:, s % STAGING].rearrange("p u t m -> p (u t m)"),
                    w1_hi[:, units].rearrange("p u t m -> p (u t m)"), ALU.subtract).then_inc(w_lo_done, 1)

            def make_rows():
                link(nc.vector.tensor_reduce(is_rows[:], ident[0:G_ROWS, 0:G_ROWS].rearrange(
                    "p (k e) -> p k e", e=E), AX.X, ALU.add))
                link(nc.vector.tensor_scalar(not_rows[:], is_rows[:], -1.0, 1.0, ALU.mult, ALU.add))
                link(nc.vector.tensor_tensor(own_expert[:], ident[0:G_ROWS, 0:E], ident[0:G_ROWS, E:2 * E], ALU.add))
                def wide(e, n):
                    return own_expert[:, e:e + 1].broadcast_to([G_ROWS, n])

                if gated:
                    for e in range(E):
                        link(nc.vector.tensor_copy(spread[:, e], wide(e, P)))
                else:
                    for u in range(n_units):
                        pair, i = u // 3, u % 3
                        if i < 2:
                            link(nc.vector.tensor_copy(spread[:, u], wide(2 * pair + i, P)))
                        else:
                            for part in range(2):
                                link(nc.vector.tensor_copy(spread[:, u, part * rest:(part + 1) * rest],
                                                           wide(2 * pair + part, rest)))
                dve.wait_ge(b2_loaded, 48)
                link(nc.vector.tensor_copy(b2_hi[:], b2_in[:]))
                link(nc.vector.tensor_tensor(b2_lo[:], b2_in[:], b2_hi[:], ALU.subtract))
                link(nc.vector.tensor_scalar(b2_own[:], b2_hi[:], not_rows[:, 2:3], None, ALU.mult))
                link(nc.vector.scalar_tensor_tensor(b2_rows[:], b2_lo[:], is_rows[:, 2:3], b2_own[:],
                                                    ALU.mult, ALU.add))

            def lay_gates(image, k):
                b = number(image, k)
                positive(dve, g_turned, b)
                nc.vector.tensor_copy(
                    g_laid[:], gates[:, ds(b * BT * E, BT * E)].rearrange("p (j a e) -> p j a e", j=BT, a=1
                                                                          ).broadcast_to([P, BT, 3, E])
                ).then_inc(g_laid_done, 1)

            def split_gates(image, k, part):
                b = number(image, k)
                if part == 0:
                    dve.wait_ge(g_turned, b + 1)
                    nc.vector.tensor_copy(g_hi[:], ps_y[0:G_ROWS, k]).then_inc(g_step, 1)
                if part == 1:
                    dve.wait_ge(g_step, 4 * b + 1)
                    nc.vector.tensor_tensor(g_lo[:], ps_y[0:G_ROWS, k], g_hi[:], ALU.subtract).then_inc(g_step, 1)
                    nc.vector.tensor_scalar(g_own[:], g_hi[:], not_rows[:, 1:2], None, ALU.mult).then_inc(g_step, 1)
                if part == 2:
                    dve.wait_ge(g_step, 4 * b + 3)
                    positive(dve, y_ready, b - 1)
                    nc.vector.scalar_tensor_tensor(g_rows[:, k], g_lo[:], is_rows[:, 1:2], g_own[:],
                                                   ALU.mult, ALU.add).then_inc(g_step, 1)

            def split_x(image, k):
                dve.wait_ge(x_hi_done, number(image, k) + 1)
                nc.vector.tensor_tensor(x_lo[:, k], xb[:, k], x_hi[:, k], ALU.subtract).then_inc(x_lo_done, 1)

            def multiply(image, k, u):
                at = number(image, k) * n_units + u
                dve.wait_ge(half_done, at + 1)
                positive(dve, lo_done, at - RING + 1)
                nc.vector.scalar_tensor_tensor(
                    act_buf[:, u % RING], ps_h[:, u % ring_h, 1], bias[:, bias_column(u, 1)],
                    half_way[:, u % 2], ALU.add, ALU.mult).then_inc(a_ready, 1)

            def weigh(image, k, u):
                b = number(image, k)
                dve.wait_ge(a_ready, b * n_units + u + 1)
                dve.wait_ge(g_ready, b * n_gates + u // units_of_gate + 1)
                nc.vector.tensor_tensor(act_buf[:, u % RING], act_buf[:, u % RING],
                                        ps_g[:, (u // units_of_gate) % 2], ALU.mult).then_inc(weighed, 1)

            def add_block(image, k):
                b = number(image, k)
                dve.wait_ge(y_turned, b + 1)
                t = T[:, ds(b * HALF, HALF)]
                nc.vector.tensor_tensor(t, t, ps_y[:, k], ALU.add).then_inc(t_added, 1)

            def high(image, k, u):
                high_part(dve, nc.vector.tensor_copy, image, k, u)

            def body(image, k):
                first = isinstance(image, int) and image == 0 and k == 0
                for u in range(n_units):
                    if first and u % set_units == 0 and u // set_units + 2 < sets:
                        set_rest(u // set_units + 2)
                    if gated:
                        multiply(image, k, u)
                        late(image, k, u, 1, weigh)
                    else:
                        weigh(image, k, u)
                        late(image, k, u, HIGH_DELAY, high)
                    if u == NEXT_X_AT + 1 and after(image, k):
                        split_x(*after(image, k))
                    if u == TURN_AT and out is None and before(image, k):
                        add_block(*before(image, k))
                    if u == GATES_AT - 1 and after(image, k):
                        lay_gates(*after(image, k))
                    if GATES_AT <= u < GATES_AT + 3 and after(image, k):
                        split_gates(*after(image, k), u - GATES_AT)

            lay_gates(0, 0)
            make_rows()
            set_rest(0)
            assert steps[0] == SET_UP[gated], steps
            split_x(0, 0)
            for part in range(3):
                split_gates(0, 0, part)
            set_rest(1)
            dve.wait_ge(bias_ready, 1)
            blocks(dve, body)
            if gated:
                tail(1, weigh)
            else:
                tail(HIGH_DELAY, high)
            if out is None:
                add_block(IMAGES - 1, 1)

        @block.scalar
        def _(act):
            def set_high(s):
                units = slice(s * set_units, (s + 1) * set_units)
                act.wait_ge(w_in[s % STAGING], 16 * loads * (s // STAGING + 1))
                nc.scalar.activation(w2_hi[:, units], w2_in[:, s % STAGING], ACT.Copy)
                nc.scalar.activation(w1_hi[:, units].rearrange("p u t m -> p (u t m)"),
                                     w1_in[:, s % STAGING].rearrange("p u t m -> p (u t m)"), ACT.Copy
                                     ).then_inc(w_hi_done, 1)

            def high_x(image, k):
                b = number(image, k)
                act.wait_ge(x_in[k], 16 * (image + 1))
                positive(act, h_ready, (b - 1) * n_units)
                nc.scalar.activation(x_hi[:, k], xb[:, k], ACT.Copy).then_inc(x_hi_done, 1)

            def copy_tokens(image, k):
                b = number(image, k)
                positive(act, y_ready, b - 1)
                nc.scalar.activation(t_copy[:, k], T[:, ds(b * HALF, HALF)], ACT.Copy).then_inc(t_copied, 1)

            def copy_sums(image, k):
                act.wait_ge(y_ready, number(image, k) + 1)
                if out is not None:
                    positive(act, out_sent[k], 16 * image)
                else:
                    positive(act, y_turned, number(image, k) - 1)
                nc.scalar.activation(total[:, k], ps_y[:, k], ACT.Copy).then_inc(y_copied, 1)

            def high(image, k, u):
                high_part(act, nc.scalar.copy, image, k, u)

            def body(image, k):
                b = number(image, k)
                first = isinstance(image, int) and image == 0 and k == 0
                for u in range(n_units):
                    at = b * n_units + u
                    if first and u % set_units == 0 and u // set_units + 2 < sets:
                        set_high(u // set_units + 2)
                    act.wait_ge(h_ready, at + 1)
                    if gated:
                        positive(act, a_ready, at - 1)
                        nc.scalar.activation(half_way[:, u % 2], ps_h[:, u % ring_h, 0], ACT.Silu,
                                             bias=bias[:, bias_column(u, 0)]).then_inc(half_done, 1)
                        late(image, k, u, HIGH_DELAY, high)
                    else:
                        positive(act, lo_done, at - RING + 1)
                        nc.scalar.activation(act_buf[:, u % RING], ps_h[:, u % ring_h, 0], ACT.Gelu,
                                             bias=bias[:, bias_column(u, 0)]).then_inc(a_ready, 1)
                        if u == lag + 1:
                            copy_tokens(image, k)
                    if u == NEXT_X_AT and after(image, k):
                        high_x(*after(image, k))
                    if u == lag and before(image, k):
                        copy_sums(*before(image, k))

            set_high(0)
            high_x(0, 0)
            set_high(1)
            act.wait_ge(bias_turned, 1)
            nc.scalar.activation(bias[:], ps_y[:, 1, 0:n_bias], ACT.Copy).then_inc(bias_ready, 1)
            act.wait_ge(bias_ready, 1)
            blocks(act, body)
            if gated:
                tail(HIGH_DELAY, high)
            copy_sums(IMAGES - 1, 1)

        @block.tensor
        def _(pe):
            mm = nc.tensor.matmul

            def turn_gates(image, k):
                b = number(image, k)
                pe.wait_ge(g_laid_done, b + 1)
                if out is None:
                    positive(pe, t_added, b - 1)
                else:
                    positive(pe, y_copied, b - 1)
                for j in range(BT):
                    last = nc.tensor.transpose(ps_y[0:G_ROWS, k, j * P:(j + 1) * P],
                                               g_laid[:, j].rearrange("p a e -> p (a e)"), ident[:])
                last.then_inc(g_turned, 1)

            def spread_gates(image, k, g):
                at = number(image, k) * n_gates + g
                if g == 0:
                    pe.wait_ge(g_step, 4 * number(image, k) + 4)
                positive(pe, weighed, (at - 1) * units_of_gate)
                mm(ps_g[:, g % 2], spread[:, g], g_rows[:, k], start=True, stop=True).then_inc(g_ready, 1)

            def unit(image, k, u):
                at = number(image, k) * n_units + u
                positive(pe, a_ready, at - ring_h + 1)
                h = ps_h[:, u % ring_h]
                for t in range(per_unit):
                    mm(h[:, t], w1_hi[:, u, t], x_hi[:, k], start=True, stop=False)
                    mm(h[:, t], w1_hi[:, u, t], x_lo[:, k], start=False, stop=False)
                    last = mm(h[:, t], w1_lo[:, u, t], x_hi[:, k], start=False, stop=True)
                last.then_inc(h_ready, 1)

            def second(image, k, u):
                b = number(image, k)
                pe.wait_ge(lo_done, b * n_units + u + 1)
                y, s = ps_y[:, k], u % ring_a
                if u == 0:
                    pe.wait_ge(g_step, 4 * b + 4)
                mm(y, w2_hi[:, u], act_hi[:, s], start=(u == 0), stop=False, skip_group_check=True)
                mm(y, w2_hi[:, u], act_lo[:, s], start=False, stop=False, skip_group_check=True)
                mm(y, w2_lo[:, u], act_hi[:, s], start=False, stop=False, skip_group_check=True
                   ).then_inc(y_used, 1)
                if u == n_units - 1:
                    if out is not None:
                        pe.wait_ge(t_copied, b + 1)
                        for j in range(BT):
                            mm(y[:, j * P:(j + 1) * P], t_copy[:, k, j * P:(j + 1) * P], ident[:],
                               start=False, stop=False, skip_group_check=True)
                    mm(y, b2_rows[:], g_rows[:, k], start=False, stop=True, skip_group_check=True
                       ).then_inc(y_ready, 1)

            def turn(image, k):
                pe.wait_ge(y_copied, number(image, k) + 1)
                for j in range(BT):
                    last = nc.tensor.transpose(ps_y[:, k, j * P:(j + 1) * P], total[:, k, j * P:(j + 1) * P], ident[:])
                last.then_inc(y_turned, 1)

            def body(image, k):
                first = isinstance(image, int) and image == 0 and k == 0
                pe.wait_ge(x_lo_done, number(image, k) + 1)
                for u in range(n_units):
                    if first and u % set_units == 0:
                        pe.wait_ge(w_lo_done, u // set_units + 1)
                    unit(image, k, u)
                    if gated and u % 2 == 0:
                        spread_gates(image, k, u // 2)
                    if not gated:
                        spread_gates(image, k, u)
                    late(image, k, u, lag, second)
                    if u == TURN_AT and out is None and before(image, k):
                        turn(*before(image, k))
                    if u == GATES_AT and after(image, k):
                        turn_gates(*after(image, k))

            turn_gates(0, 0)
            pe.wait_ge(bias_loaded, 16 * bias_loads)
            nc.tensor.transpose(ps_y[:, 1, 0:n_bias], bias_in[:], ident[0:n_bias, 0:n_bias]).then_inc(bias_turned, 1)
            pe.wait_ge(bias_ready, 1)
            pe.wait_ge(set_up, SET_UP[gated])
            blocks(pe, body)
            tail(lag, second)
            if out is None:
                turn(IMAGES - 1, 1)


HD = 8
DH = 16
GH = 4
CHUNKS = 4
TABLE_STEPS = 123
ROW_STEPS = 9
FIN3 = {"x20": (1, 2), "x21": (1, 3), "logits": (2, 1)}
PREP3 = {"xt0": (2, 2), "xt1": (2, 3)}
USES3 = len(FIN3) + len(PREP3)
STATES = 14
MIX_COLS = 3 * P


def decay_stage(nc, T, xT_dram, gates, ident, dram):
    with ExitStack() as ctx:
        sb, ps, sem = allocator(nc, ctx)
        w_in = [sb(f"d_w_in{k}", [P, C]) for k in range(3)]
        cols = sb("d_cols", [P, 6])
        conv = sb("d_conv", [P, 2, DH])
        spread_m = sb("d_spread", [P, 2, P])
        ones = sb("d_ones", [P, P])
        own = sb("d_own", [P, 2 * GH])
        is_part = sb("d_is_part", [P, 2])
        is_head = sb("d_is_head", [P, GH])
        mirror = sb("d_mirror", [P, P])
        swap = sb("d_swap", [P, 2, P])
        signs = sb("d_signs", [P, P])
        row = sb("d_row", [P, 2, 5])
        norm2 = sb("d_norm2", [P, 2, 1])
        norm2b = sb("d_norm2b", [P, 2, 1])
        mhalf = sb("d_mhalf", [P, TILES])
        eps = sb("d_eps", [P, TILES])
        zero = sb("d_zero", [P, TILES])
        pw = sb("d_pw", [P, 3, 2, P + 1])
        pt = sb("d_pt", [P, 4, 2, P])
        z = sb("d_z", [P, 2, 2, P + 1])
        amp_all = sb("d_amp_all", [P, HD])
        amp_exp = sb("d_amp_exp", [P, HD])
        row_exp = sb("d_row_exp", [P, 2])
        amp_pow = sb("d_amp_pow", [P, 7, HD])
        lag = sb("d_lag", [P, P], mybir.dt.int32)
        bit_i = sb("d_bit_i", [P, P], mybir.dt.int32)
        bit = sb("d_bit", [P, P])
        no_bit = sb("d_no_bit", [P, P])
        factor = sb("d_factor", [P, HD, P])
        ta = sb("d_ta", [P, 2, P])
        ta_t = sb("d_ta_t", [P, 2, P])
        wq = sb("d_wq", [P, 2, P])
        wkv = sb("d_wkv", [P, MIX_COLS])
        bias_in = sb("d_bias_in", [3, MIX_COLS])
        bias_part = [sb(f"d_bias_part{k}", [3, MIX_COLS], BF16) for k in range(3)]
        bias_rest = [sb(f"d_bias_rest{k}", [3, MIX_COLS]) for k in range(2)]
        bias_rows = sb("d_bias_rows", [3, MIX_COLS], BF16)
        ones3 = sb("d_ones3", [3, P], BF16)
        tab_k = sb("d_tab_k", [P, 2, P])
        tab_q = sb("d_tab_q", [P, 2, GH, P])
        tab_s = sb("d_tab_s", [P, 2, P])
        tab_end = sb("d_tab_end", [P, 2, P])
        decay = sb("d_decay", [P, HD, P])
        turn_m = sb("d_turn", [P, 2, P])
        start = sb("d_start", [P, 2, P])
        state = sb("d_state", [P, 2, 2, P])
        block_mask = sb("d_block_mask", [P, P])
        wg = sb("d_wg", [P, E])
        bg = sb("d_bg", [P, E])
        iota = sb("d_iota", [P, E])
        stats = [sb(f"d_stats{k}", [P, TILES, 6]) for k in range(2)]
        mv = [sb(f"d_mv{k}", [P, TILES, 2]) for k in range(2)]
        rstd = [sb(f"d_rstd{k}", [P, TILES]) for k in range(2)]
        shift = [sb(f"d_shift{k}", [P, TILES]) for k in range(2)]
        xn = [sb(f"d_xn{k}", [P, PX]) for k in range(2)]
        xT = [sb(f"d_xT{k}", [P, PX]) for k in range(2)]
        raw = sb("d_raw", [P, 2, HALF])
        q_wide = sb("d_q_wide", [P, 2, CHUNKS, GH * P])
        q_state = sb("d_q_state", [P, 2, HALF])
        k_chan = sb("d_k_chan", [P, 2, HALF])
        k_tok = sb("d_k_tok", [P, 2, CHUNKS, 2 * P])
        v_tok = sb("d_v_tok", [P, 2, CHUNKS, HD, 2 * DH])
        inner = sb("d_inner", [P, 2, HALF])
        o_chan = sb("d_o_chan", [P, 2, HALF])
        logits = sb("d_logits", [P, TILES, E])
        top = sb("d_top", [P, TILES, 8])
        top_at = sb("d_topat", [P, TILES, 8], U32)
        top_atf = sb("d_topatf", [P, TILES, 2])
        gap = sb("d_gap", [P, TILES])
        expo = sb("d_expo", [P, TILES])
        gsum = sb("d_gsum", [P, TILES])
        w1 = sb("d_w1", [P, TILES])
        w2 = sb("d_w2", [P, TILES])
        hit = sb("d_hit", [P, 2, TILES, E])

        ps_x = ps("d_ps_x", [P, HALF])
        ps_q = ps("d_ps_q", [P, HALF])
        ps_k = ps("d_ps_k", [P, HALF])
        ps_s = ps("d_ps_s", [P, 2, HALF])
        ps_o = ps("d_ps_o", [P, HALF])
        ps_st = ps("d_ps_st", [P, P])
        ps_t = ps("d_ps_t", [P, HALF])

        loaded = sem("d_loaded")
        const = sem("d_const")
        step = sem("d_step")
        passed = sem("d_passed")
        set_up = sem("d_set_up")
        moved = sem("d_moved")
        norm_ready = sem("d_norm_ready")
        norm_done = sem("d_norm_done")
        exps_done = sem("d_exps_done")
        stats_done = [sem(f"d_stats_done{k}") for k in range(2)]
        mv_done = [sem(f"d_mv_done{k}") for k in range(2)]
        rstd_done = [sem(f"d_rstd_done{k}") for k in range(2)]
        xn_done = [sem(f"d_xn_done{k}") for k in range(2)]
        xn_used = [sem(f"d_xn_used{k}") for k in range(2)]
        x_ready = sem("d_x_ready")
        x_free = sem("d_x_free")
        p_ready = sem("d_p_ready")
        p_copied = sem("d_p_copied")
        tables_used = sem("d_tables_used")
        k_ready = sem("d_k_ready")
        k_done = sem("d_k_done")
        v_done = sem("d_v_done")
        s_ready = sem("d_s_ready")
        inner_done = sem("d_inner_done")
        chunk_done = sem("d_chunk_done")
        st_ready = sem("d_st_ready")
        st_done = sem("d_st_done")
        o_copied = sem("d_o_copied")
        o_turned = sem("d_o_turned")
        t_added = sem("d_t_added")
        xT_sent = sem("d_xT_sent")
        g_step = sem("d_g_step")
        gap_exp = sem("d_gap_exp")
        N_LOADS = 20

        def positive(eng, s, value):
            if not (isinstance(value, int) and value <= 0):
                eng.wait_ge(s, value)

        def parts_of(n):
            if not isinstance(n, int):
                return True, True, True
            return n >= 1, n < IMAGES - 1, 0 <= n < IMAGES

        def uses(n):
            finish, prepare, _ = parts_of(n)
            fills = (FIN3 if finish else {}) | (PREP3 if prepare else {})
            if isinstance(n, int) and n < 1:
                first = 0 if n < 0 else len(PREP3)
            elif isinstance(n, int) and n == IMAGES:
                first = (n - 2) * USES3 + 2 * len(PREP3) + len(FIN3)
            else:
                first = (n - 1) * USES3 + 2 * len(PREP3)
            return first, fills

        def use(n, name):
            first, fills = uses(n)
            return first + sorted(fills, key=fills.get).index(name)

        def filled_at(n, a, c):
            return [name for name, at in uses(n)[1].items() if at == (a, c)]

        def images(eng, body):
            body(-1)
            body(0)
            body(1)
            with eng.Fori(2, IMAGES - 1) as n:
                body(n)
            body(IMAGES - 1)
            body(IMAGES)

        def slots(n):
            steps = parts_of(n)[2]
            for a in range(4):
                for c in range(CHUNKS):
                    nxt = steps and not (isinstance(n, int) and n == IMAGES - 1 and a == 3)
                    if isinstance(n, int) and n < 0:
                        nxt = a == 3
                    yield a, c, steps, nxt

        def state_index(n, a, c):
            if a >= 2 and c == CHUNKS - 1:
                return None
            return n * STATES + (a * 4 + c if a < 3 else 11 + c)

        block = ctx.enter_context(nc.Block())

        @block.sync
        def _(sp):
            for k, name in enumerate(("wq", "wk", "wv")):
                sp.dma_start(w_in[k][:], dram[f"L3_attn_{name}_w"]).then_inc(loaded, 16)
            with nc.allow_non_contiguous_dma("one number to a partition"):
                for k, name in enumerate(("phazor_re", "phazor_im")):
                    sp.dma_start(cols[:, k:k + 1], dram[f"L3_attn_{name}"].rearrange("h (d a) -> (h d) a", a=1)
                                 ).then_inc(loaded, 16)
                for k, name in enumerate(("wq_b", "wk_b", "wv_b")):
                    sp.dma_start(cols[:, 3 + k:4 + k], dram[f"L3_attn_{name}"].rearrange("(p a) -> p a", a=1)
                                 ).then_inc(loaded, 16)
                amp = dram["L3_attn_amplitude"].rearrange("(h a) -> h a", a=1)
                for h in range(HD):
                    sp.dma_start(cols[DH * h:DH * (h + 1), 2:3], amp[h:h + 1].broadcast_to([DH, 1])
                                 ).then_inc(loaded, 16)
                sp.dma_start(amp_all[:], amp.rearrange("h a -> a h").broadcast_to([P, HD])).then_inc(loaded, 16)
            assert 3 + 2 + 3 + HD + 1 + 2 + 2 == N_LOADS + 1

            def body(n):
                if parts_of(n)[0]:
                    sp.wait_ge(x_free, use(n, "x21") + 1)
                    sp.dma_start(xT_dram[:, ds((n - 1) * PX, PX)], xT[1][:]).then_inc(xT_sent, 16)

            images(sp, body)
            sp.wait_ge(xT_sent, 16 * IMAGES)

        @block.gpsimd
        def _(pool):
            count = [0]

            def made(ins):
                count[0] += 1
                ins.then_inc(const, 1)
                pool.wait_ge(const, count[0])

            made(pool.memset(ones[:], 1.0))
            made(pool.memset(mhalf[:], -0.5))
            made(pool.memset(eps[:], EPS_T))
            made(pool.memset(zero[:], 0.0))
            made(pool.memset(ones3[:], 1.0))
            made(pool.memset(v_tok[:], 0.0))
            made(pool.iota(iota[:], [[1, E]], base=0, channel_multiplier=0,
                           allow_small_or_imprecise_dtypes=True))
            made(pool.iota(lag[:], [[1, P]], base=0, channel_multiplier=-1))
            for g in range(2):
                made(pool.affine_select(
                    out=spread_m[:, g].rearrange("p (j s d) -> p j s d", s=2, d=DH),
                    in_=ones[:].rearrange("p (j s d) -> p j s d", s=2, d=DH), compare_op=ALU.is_equal, fill=0.0,
                    base=-g * GH * DH, pattern=[[-DH, GH], [0, 2], [-1, DH]], channel_multiplier=1))
            made(pool.affine_select(out=own[:], in_=ones[:, 0:2 * GH], compare_op=ALU.is_ge, fill=0.0, base=0,
                                    pattern=[[-DH, 2 * GH]], channel_multiplier=1))
            made(pool.affine_select(out=own[:], in_=own[:], compare_op=ALU.is_ge, fill=0.0, base=DH - 1,
                                    pattern=[[DH, 2 * GH]], channel_multiplier=-1))
            made(pool.affine_select(out=mirror[:], in_=ones[:], compare_op=ALU.is_equal, fill=0.0, base=1 - P,
                                    pattern=[[1, P]], channel_multiplier=1))
            for k, off in enumerate((DH, -DH)):
                made(pool.affine_select(out=swap[:, k], in_=ones[:], compare_op=ALU.is_equal, fill=0.0, base=off,
                                        pattern=[[-1, P]], channel_multiplier=1))
            pool.wait_ge(norm_ready, 1)
            nc.gpsimd.tensor_tensor(norm2b[:].rearrange("p a b -> p (a b)"), norm2[:].rearrange("p a b -> p (a b)"),
                                    mhalf[:, 0:2], ALU.pow).then_inc(norm_done, 1)

            def scales(m, k):
                wait_apart(pool, mv_done[k], m + 1, passed)
                positive(pool, xn_done[k], TILES * m)
                nc.gpsimd.tensor_tensor(rstd[k][:], mv[k][:, :, 1], eps[:], ALU.add).then_inc(rstd_done[k], 1)
                pool.wait_ge(rstd_done[k], 4 * m + 1)
                nc.gpsimd.tensor_tensor(rstd[k][:], rstd[k][:], mhalf[:], ALU.pow).then_inc(rstd_done[k], 1)
                pool.wait_ge(rstd_done[k], 4 * m + 2)
                nc.gpsimd.tensor_tensor(shift[k][:], mv[k][:, :, 0], rstd[k][:], ALU.mult).then_inc(rstd_done[k], 1)
                pool.wait_ge(rstd_done[k], 4 * m + 3)
                nc.gpsimd.tensor_tensor(shift[k][:], zero[:], shift[k][:], ALU.subtract).then_inc(rstd_done[k], 1)

            def with_tables(w, g, k):
                pool.wait_ge(p_copied, 2 * w + 1)
                positive(pool, chunk_done, 4 * (w - 1))
                nc.gpsimd.tensor_tensor(
                    k_chan[:, k].rearrange("p (c l) -> p c l", c=CHUNKS),
                    raw[:, 0].rearrange("p (c l) -> p c l", c=CHUNKS),
                    tab_k[:, g:g + 1].broadcast_to([P, CHUNKS, P]), ALU.mult).then_inc(tables_used, 1)
                pool.wait_ge(p_copied, 2 * w + 2)
                for c in range(CHUNKS):
                    nc.gpsimd.tensor_tensor(
                        q_wide[:, k, c].rearrange("p (j l) -> p j l", j=GH),
                        raw[:, 1:2, c * P:(c + 1) * P].broadcast_to([P, GH, P]), tab_q[:, g], ALU.mult
                    ).then_inc(tables_used, 1)
                    if c == 0:
                        nc.gpsimd.tensor_tensor(
                            q_state[:, k].rearrange("p (c l) -> p c l", c=CHUNKS),
                            raw[:, 1].rearrange("p (c l) -> p c l", c=CHUNKS),
                            tab_s[:, g:g + 1].broadcast_to([P, CHUNKS, P]), ALU.mult).then_inc(tables_used, 1)

            def body(n):
                finish, prepare, _ = parts_of(n)
                if isinstance(n, int) and n < 0:
                    scales(0, 0)
                for a, c, steps, nxt in slots(n):
                    if (a, c) == (0, 3) and finish:
                        scales(n - 1, 1)
                    if (a, c) == (1, 3) and prepare and not (isinstance(n, int) and n < 0):
                        scales(n + 1, 0)
                    if c == 0 and nxt:
                        with_tables(4 * n + a + 1, (a + 1) % 2, (a + 1) % 2)

            pool.wait_ge(step, TABLE_STEPS)
            images(pool, body)

        @block.vector
        def _(dve):
            count = [0]

            def link(ins):
                count[0] += 1
                ins.then_inc(step, 1)
                dve.wait_ge(step, count[0])

            def by_row(x, n):
                return x.rearrange("p (a b) -> p a b", b=1).broadcast_to([P, x.shape[1], n])

            tt, tsc, stt = nc.vector.tensor_tensor, nc.vector.tensor_scalar, nc.vector.scalar_tensor_tensor
            dve.wait_ge(loaded, 16 * (N_LOADS + 1))
            dve.wait_ge(const, 15)
            own_v = own[:].rearrange("p (j s) -> p j s", s=2)
            link(nc.vector.tensor_reduce(is_part[:], own[:].rearrange("p (j s) -> p s j", s=2), AX.X, ALU.add))
            link(nc.vector.tensor_reduce(is_head[:], own_v, AX.X, ALU.add))
            link(nc.vector.tensor_copy(block_mask[:].rearrange("p (j x) -> p j x", j=GH), by_row(is_head[:], 2 * DH)))
            link(tsc(signs[:], swap[:, 0], is_part[:, 0:1], None, ALU.mult))
            link(tsc(swap[:, 1], swap[:, 1], is_part[:, 1:2], None, ALU.mult))
            link(tt(signs[:], signs[:], swap[:, 1], ALU.subtract))
            dve.wait_ge(set_up, 1)
            link(nc.vector.tensor_copy(wq[:].rearrange("p g r -> p (g r)"), ps_q[:, 0:2 * P]))
            link(nc.vector.tensor_copy(wkv[:], ps_k[:, 0:MIX_COLS]))
            link(nc.vector.tensor_copy(row[:], ps_o[:, 0:10].rearrange("p (g k) -> p g k", g=2)))
            link(nc.vector.tensor_copy(bias_in[:], ps_s[0:3, 0, 0:MIX_COLS]))
            lc = ps_s[:, 1, 0:4 * DH].rearrange("p (g s e) -> p g s e", g=2, s=2)
            link(nc.vector.tensor_copy(pt[:, 0, :, 0:2 * DH].rearrange("p g (s e) -> p g s e", s=2), lc))
            for g in range(2):
                link(tsc(pt[:, 1, g, 0:DH], pt[:, 0, g, 0:DH], is_part[:, 0:1], None, ALU.mult))
                link(stt(pt[:, 1, g, 0:DH], pt[:, 0, g, DH:2 * DH], is_part[:, 1:2], pt[:, 1, g, 0:DH],
                         ALU.mult, ALU.add))
                link(nc.vector.memset(start[:, g], 0.0))
                link(tt(start[:, g].rearrange("p (j x) -> p j x", j=GH)[:, :, 0:DH],
                        pt[:, 1, g:g + 1, 0:DH].broadcast_to([P, GH, DH]), by_row(is_head[:], DH), ALU.mult))
            left = bias_in
            for k in range(3):
                link(nc.vector.tensor_copy(bias_part[k][:], left[:]))
                if k < 2:
                    link(tt(bias_rest[k][:], left[:], bias_part[k][:], ALU.subtract))
                    left = bias_rest[k]
            link(tsc(bias_rows[:], bias_part[0][:], ident[0:3, 0:1], None, ALU.mult))
            for k in (1, 2):
                link(stt(bias_rows[:], bias_part[k][:], ident[0:3, k:k + 1], bias_rows[:], ALU.mult, ALU.add))
            link(tt(pt[:, 0, :, 0:1], row[:, :, 0:1], row[:, :, 0:1], ALU.mult))
            link(tt(pt[:, 1, :, 0:1], row[:, :, 1:2], row[:, :, 1:2], ALU.mult))
            tt(norm2[:], pt[:, 0, :, 0:1], pt[:, 1, :, 0:1], ALU.add).then_inc(norm_ready, 1)
            dve.wait_ge(norm_done, 1)
            link(nc.vector.memset(pw[:, 0, :, 0:1], 1.0))
            link(nc.vector.memset(pw[:, 1, :, 0:1], 0.0))
            link(nc.vector.memset(pw[:, 2, :, 0:1], 1.0))
            link(tt(pw[:, 0, :, 1:2], row[:, :, 0:1], norm2b[:], ALU.mult))
            link(tt(pw[:, 1, :, 1:2], row[:, :, 1:2], norm2b[:], ALU.mult))
            dve.wait_ge(exps_done, 2)
            link(tsc(row_exp[:], row_exp[:], 1.0, None, ALU.add))
            link(nc.vector.reciprocal(pw[:, 2, :, 1], row_exp[:]))
            link(tsc(amp_exp[:], amp_exp[:], 1.0, None, ALU.add))
            link(nc.vector.reciprocal(amp_pow[:, 0], amp_exp[:]))
            n = 1
            while n < P:
                def at_n(k):
                    return pw[:, k, :, n:n + 1].broadcast_to([P, 2, n])

                def low(k):
                    return pw[:, k, :, 1:n + 1]

                tt(pt[:, 0, :, 0:n], low(0), at_n(0), ALU.mult)
                tt(pt[:, 1, :, 0:n], low(1), at_n(1), ALU.mult)
                tt(pt[:, 2, :, 0:n], low(0), at_n(1), ALU.mult)
                link(tt(pt[:, 3, :, 0:n], low(1), at_n(0), ALU.mult))
                tt(pw[:, 2, :, n + 1:2 * n + 1], low(2), at_n(2), ALU.mult)
                tt(pw[:, 0, :, n + 1:2 * n + 1], pt[:, 0, :, 0:n], pt[:, 1, :, 0:n], ALU.subtract)
                link(tt(pw[:, 1, :, n + 1:2 * n + 1], pt[:, 2, :, 0:n], pt[:, 3, :, 0:n], ALU.add))
                n *= 2
            for k in range(2):
                link(tt(z[:, k], pw[:, k], pw[:, 2], ALU.mult))
            for g in range(2):
                link(tsc(tab_k[:, g], pw[:, 0, g, 0:P], is_part[:, 0:1], None, ALU.mult))
                link(stt(tab_k[:, g], pw[:, 1, g, 0:P], is_part[:, 1:2], tab_k[:, g], ALU.mult, ALU.add))
                link(tt(tab_q[:, g], tab_k[:, g:g + 1].broadcast_to([P, GH, P]), by_row(is_head[:], P), ALU.mult))
                link(tsc(pt[:, 0, g], z[:, 1, g, 1:P + 1], is_part[:, 1:2], None, ALU.mult))
                link(stt(tab_s[:, g], z[:, 0, g, 1:P + 1], is_part[:, 0:1], pt[:, 0, g], ALU.mult, ALU.subtract))
                link(tsc(ta[:, g], z[:, 0, g, 0:P], is_part[:, 0:1], None, ALU.mult))
                link(stt(ta[:, g], z[:, 1, g, 0:P], is_part[:, 1:2], ta[:, g], ALU.mult, ALU.add))
                link(tsc(turn_m[:, g], ident[:], z[:, 0, g, P:P + 1], None, ALU.mult))
                link(stt(turn_m[:, g], signs[:], z[:, 1, g, P:P + 1], turn_m[:, g], ALU.mult, ALU.add))
            nc.vector.memset(pt[:, 3, 0, 0:1], 0.0).then_inc(moved, 1)
            dve.wait_ge(set_up, 2)
            nc.vector.tensor_copy(ta_t[:].rearrange("p g r -> p (g r)"), ps_q[:, 0:2 * P]).then_inc(moved, 1)
            dve.wait_ge(set_up, 3)
            link(nc.vector.tensor_copy(tab_end[:].rearrange("p g r -> p (g r)"), ps_k[:, 0:2 * P]))
            for k in range(1, 7):
                link(tt(amp_pow[:, k], amp_pow[:, k - 1], amp_pow[:, k - 1], ALU.mult))
            link(tsc(bit[:], lag[:], 0.0, None, ALU.is_ge))
            link(nc.vector.tensor_copy(decay[:], bit[:].rearrange("p (a l) -> p a l", a=1).broadcast_to([P, HD, P])))
            for k in range(7):
                link(tsc(bit_i[:], lag[:], k, 1, ALU.logical_shift_right, ALU.bitwise_and))
                link(nc.vector.tensor_copy(bit[:], bit_i[:]))
                link(tsc(no_bit[:], bit[:], -1.0, 1.0, ALU.mult, ALU.add))
                link(tt(factor[:], bit[:].rearrange("p (a l) -> p a l", a=1).broadcast_to([P, HD, P]),
                        by_row(amp_pow[:, k], P), ALU.mult))
                link(tt(factor[:], factor[:],
                        no_bit[:].rearrange("p (a l) -> p a l", a=1).broadcast_to([P, HD, P]), ALU.add))
                link(tt(decay[:], decay[:], factor[:], ALU.mult))
            assert count[0] == TABLE_STEPS, count[0]

            def statistics(m, k, half):
                for j in range(half * TILES // 2, (half + 1) * TILES // 2):
                    last = nc.vector.bn_stats(stats[k][:, j, :], T[:, ds(m * PX + j * P, P)])
                if half == 0:
                    return
                last.then_inc(stats_done[k], 1)
                positive(dve, xn_done[k], TILES * m)
                wait_apart(dve, stats_done[k], m + 1, passed)
                for j in range(TILES):
                    last = nc.vector.bn_aggr(mv[k][:, j, :], stats[k][:, j, :])
                last.then_inc(mv_done[k], 1)

            def masked(w, c, g):
                at = 4 * w + c
                dve.wait_ge(s_ready, at + 1)
                positive(dve, chunk_done, at - 1)
                tt(inner[:, c % 2].rearrange("p (j l) -> p j l", j=GH), ps_s[:, c % 2].rearrange(
                    "p (j l) -> p j l", j=GH), decay[:, g * GH:(g + 1) * GH], ALU.mult).then_inc(inner_done, 1)

            def end_keys(n, half, c):
                at = 8 * n + 4 * half + c
                dve.wait_ge(k_ready, at + 1)
                positive(dve, chunk_done, 4 * (4 * (n - 1) + 2 * half + 2))
                tt(k_tok[:, half, c], ps_k[:, 0:2 * P], tab_end[:].rearrange("p g r -> p (g r)"), ALU.mult
                   ).then_inc(k_done, 1)

            def new_state(n, a, c):
                at = state_index(n, a, c)
                g, cc = a % 2, 4 * (a // 2) + c
                dve.wait_ge(st_ready, at + 1)
                tt(state[:, g, (cc + 1) % 2], ps_st[:], block_mask[:], ALU.mult
                   ).then_inc(st_done, 1)

            def add_item(w, image, a):
                g, half = a % 2, a // 2
                dve.wait_ge(o_turned, w + 1)
                t_v = T[:, ds(image * PX + half * HALF, HALF)].rearrange(
                    "p (c h e) -> p c h e", c=CHUNKS, e=DH)[:, :, g * GH:(g + 1) * GH]
                tt(t_v, t_v, ps_t[:].rearrange("p (c j x) -> p c j x", c=CHUNKS, j=GH)[:, :, :, 0:DH], ALU.add
                   ).then_inc(t_added, 1)

            def gate(n):
                m = n - 1
                g0 = 9 * m
                dve.wait_ge(x_ready, use(n, "logits") + 1)
                nc.vector.tensor_tensor(
                    logits[:], ps_x[:, 0:TILES * E].rearrange("p (t e) -> p t e", e=E),
                    bg[:].rearrange("p (a e) -> p a e", a=1).broadcast_to([P, TILES, E]),
                    ALU.add).then_inc(g_step, 1)
                dve.wait_ge(g_step, g0 + 1)
                dve.sem_inc(x_free, 1)
                for j in range(TILES):
                    last = nc.vector.max(top[:, j, :], logits[:, j, :])
                last.then_inc(g_step, 1)
                dve.wait_ge(g_step, g0 + 2)
                nc.vector.tensor_tensor(gap[:], top[:, :, 1], top[:, :, 0], ALU.subtract).then_inc(g_step, 1)
                for j in range(TILES):
                    last = nc.vector.max_index(top_at[:, j, :], top[:, j, :], logits[:, j, :])
                last.then_inc(g_step, 1)
                dve.wait_ge(g_step, g0 + 4)
                nc.vector.tensor_copy(top_atf[:], top_at[:, :, 0:2]).then_inc(g_step, 1)

            def gate_weights(n):
                m = n - 1
                g0 = 9 * m
                dve.wait_ge(gap_exp, m + 1)
                nc.vector.tensor_scalar(gsum[:], expo[:], 1.0, None, ALU.add).then_inc(g_step, 1)
                dve.wait_ge(g_step, g0 + 6)
                nc.vector.reciprocal(w1[:], gsum[:]).then_inc(g_step, 1)
                for k in range(2):
                    nc.vector.tensor_tensor(
                        hit[:, k], iota[:].rearrange("p (a e) -> p a e", a=1).broadcast_to([P, TILES, E]),
                        top_atf[:, :, k:k + 1].broadcast_to([P, TILES, E]), ALU.is_equal)
                dve.wait_ge(g_step, g0 + 7)
                nc.vector.tensor_tensor(w2[:], w1[:], expo[:], ALU.mult).then_inc(g_step, 1)
                dve.wait_ge(g_step, g0 + 8)
                for k, w in ((0, w1), (1, w2)):
                    last = nc.vector.tensor_tensor(
                        hit[:, k], hit[:, k],
                        w[:].rearrange("p (t a) -> p t a", a=1).broadcast_to([P, TILES, E]), ALU.mult)
                last.then_inc(g_step, 1)
                dve.wait_ge(g_step, g0 + 9)
                nc.vector.tensor_tensor(
                    gates[:, ds(m * TILES * E, TILES * E)],
                    hit[:, 0].rearrange("p t e -> p (t e)"), hit[:, 1].rearrange("p t e -> p (t e)"), ALU.add)

            def body(n):
                finish, prepare, _ = parts_of(n)
                if isinstance(n, int) and n < 0:
                    statistics(0, 0, 0)
                    statistics(0, 0, 1)
                for a, c, steps, nxt in slots(n):
                    w = 4 * n + a
                    if steps and c < CHUNKS - 1:
                        masked(w, c + 1, a % 2)
                    elif c == CHUNKS - 1 and nxt:
                        masked(w + 1, 0, (a + 1) % 2)
                    if nxt and a % 2:
                        if a == 1:
                            end_keys(n, 1, c)
                        else:
                            end_keys(n + 1, 0, c)
                    if c == 1 and (finish if a == 0 else steps):
                        image, item = (n - 1, 3) if a == 0 else (n, a - 1)
                        add_item(w - 1, image, item)
                    if steps and state_index(0, a, c) is not None:
                        new_state(n, a, c)
                    if (a, c) in ((0, 2), (0, 3)) and finish:
                        dve.wait_ge(t_added, 4 * n)
                        statistics(n - 1, 1, c - 2)
                    if (a, c) in ((1, 0), (1, 1)) and prepare and not (isinstance(n, int) and n < 0):
                        statistics(n + 1, 0, c)
                    if (a, c) == FIN3["logits"] and finish:
                        gate(n)
                    if (a, c) == (2, 3) and finish:
                        gate_weights(n)

            images(dve, body)

        @block.scalar
        def _(act):
            for k, name in enumerate(("re", "im")):
                act.dma_start(conv[:, k], dram[f"L3_attn_last_conv_{name}"].rearrange("h d e -> (h d) e")
                             ).then_inc(loaded, 16)
            act.dma_start(wg[:], dram["L3_ffn_Wg"]).then_inc(loaded, 16)
            act.dma_start(bg[:], dram["L3_ffn_bg"].rearrange("(a e) -> a e", a=1).broadcast_to([P, E])
                         ).then_inc(loaded, 16)
            act.wait_ge(loaded, 16 * (N_LOADS + 1))
            act.wait_ge(step, ROW_STEPS)
            nc.scalar.activation(row_exp[:], row[:, :, 2], ACT.Exp, scale=-1.0).then_inc(exps_done, 1)
            nc.scalar.activation(amp_exp[:], amp_all[:], ACT.Exp, scale=-1.0).then_inc(exps_done, 1)

            def normalise(m, k, half):
                if half == 0:
                    act.wait_ge(rstd_done[k], 4 * m + 4)
                    positive(act, xn_used[k], m)
                for j in range(half * TILES // 2, (half + 1) * TILES // 2):
                    nc.scalar.activation(xn[k][:, j * P:(j + 1) * P], T[:, ds(m * PX + j * P, P)], ACT.Identity,
                                         scale=rstd[k][:, j:j + 1], bias=shift[k][:, j:j + 1],
                                         ).then_inc(xn_done[k], 1)

            def read_out(n, name):
                half = int(name[2])
                k = 0 if name[:2] == "xt" else 1
                act.wait_ge(x_ready, use(n, name) + 1)
                if k and half == 0:
                    positive(act, xT_sent, 16 * (n - 1))
                nc.scalar.activation(xT[k][:, half * HALF:half * HALF + HALF], ps_x[:], ACT.Copy).then_inc(x_free, 1)

            def copy_projection(w, g, kind):
                act.wait_ge(p_ready, 2 * w + kind + 1)
                positive(act, tables_used, 6 * (w - 1) + (6 if kind else 1))
                nc.scalar.activation(raw[:, kind], ps_q[:], ACT.Identity, bias=row[:, g, 4 - kind:5 - kind]
                                     ).then_inc(p_copied, 1)

            def values(n, half, c):
                at = 8 * n + 4 * half + c
                act.wait_ge(k_done, at + 1)
                positive(act, chunk_done, 4 * (4 * (n - 1) + 2 * half + 2))
                nc.scalar.activation(v_tok[:, half, c, :, 0:DH],
                                     ps_k[:, 2 * P:3 * P].rearrange("p (h e) -> p h e", h=HD), ACT.Copy
                                     ).then_inc(v_done, 1)

            def body(n):
                finish, prepare, _ = parts_of(n)
                first = isinstance(n, int) and n < 0
                if first:
                    normalise(0, 0, 0)
                    normalise(0, 0, 1)
                for a, c, steps, nxt in slots(n):
                    w = 4 * n + a
                    if nxt and c < 2:
                        copy_projection(w + 1, (a + 1) % 2, c)
                    if nxt and a % 2:
                        if a == 1:
                            values(n, 1, c)
                        else:
                            values(n + 1, 0, c)
                    for name in filled_at(n, a, c):
                        if name != "logits":
                            read_out(n, name)
                    if (a, c) == FIN3["logits"] and finish:
                        act.wait_ge(g_step, 9 * (n - 1) + 3)
                        nc.scalar.activation(expo[:], gap[:], ACT.Exp).then_inc(gap_exp, 1)
                    if steps and c == CHUNKS - 1:
                        act.wait_ge(chunk_done, 4 * w + 4)
                        positive(act, o_turned, w - 1)
                        nc.scalar.activation(o_chan[:, a % 2], ps_o[:], ACT.Copy).then_inc(o_copied, 1)
                    if (a, c) in ((1, 0), (1, 1)) and finish:
                        normalise(n - 1, 1, c)
                    if (a, c) in ((2, 0), (2, 1)) and prepare and not first:
                        normalise(n + 1, 0, c)

            images(act, body)

        @block.tensor
        def _(pe):
            pe.wait_ge(loaded, 16 * (N_LOADS + 1))
            pe.wait_ge(const, 15)
            mm = nc.tensor.matmul
            for g in range(2):
                mm(ps_q[:, g * P:(g + 1) * P], w_in[0][:], spread_m[:, g], start=True, stop=True)
                mm(ps_k[:, g * P:(g + 1) * P], w_in[1][:], spread_m[:, g], start=True, stop=True)
                mm(ps_o[:, g * 5:g * 5 + 5], spread_m[:, g], cols[:, 0:5], start=True, stop=True)
                mm(ps_s[0:3, 0, g * P:(g + 1) * P], cols[:, 4:5].broadcast_to([P, 3]), spread_m[:, g],
                   start=True, stop=True)
                mm(ps_s[:, 1, g * 2 * DH:(g + 1) * 2 * DH], spread_m[:, g], conv[:].rearrange("p s e -> p (s e)"),
                   start=True, stop=True)
            mm(ps_k[:, 2 * P:3 * P], w_in[2][:], ident[:], start=True, stop=True)
            mm(ps_s[0:3, 0, 2 * P:3 * P], cols[:, 5:6].broadcast_to([P, 3]), ident[:], start=True, stop=True
               ).then_inc(set_up, 1)
            pe.wait_ge(moved, 1)
            for g in range(2):
                last = nc.tensor.transpose(ps_q[:, g * P:(g + 1) * P], ta[:, g], ident[:])
            last.then_inc(set_up, 1)
            pe.wait_ge(moved, 2)
            mm(ps_k[:, 0:2 * P], mirror[:], ta_t[:].rearrange("p g r -> p (g r)"), start=True, stop=True
               ).then_inc(set_up, 1)
            pe.wait_ge(step, TABLE_STEPS)

            def use_x(n, name):
                positive(pe, x_free, use(n, name))
                if name == "logits":
                    for j in range(TILES):
                        last = mm(ps_x[:, j * E:(j + 1) * E], xT[1][:, j * P:(j + 1) * P], wg[:],
                                  start=True, stop=True)
                    last.then_inc(x_ready, 1)
                    return
                half = int(name[2])
                k, m = (0, n + 1) if name[:2] == "xt" else (1, n - 1)
                pe.wait_ge(xn_done[k], TILES * m + 4 * (half + 1))
                for j in range(4):
                    c = half * HALF + j * P
                    last = nc.tensor.transpose(ps_x[:, j * P:(j + 1) * P], xn[k][:, c:c + P], ident[:])
                last.then_inc(x_ready, 1)
                if half:
                    pe.wait_ge(x_ready, use(n, name) + 1)
                    pe.sem_inc(xn_used[k], 1)

            def project(w, a, kind):
                g, half = a % 2, a // 2
                positive(pe, p_copied, 2 * w + kind)
                weights = wq[:, g] if kind else wkv[:, g * P:(g + 1) * P]
                mm(ps_q[:], weights, xT[0][:, half * HALF:half * HALF + HALF], start=True, stop=True
                   ).then_inc(p_ready, 1)

            def mix(n, half, c):
                at = 8 * n + 4 * half + c
                positive(pe, k_done, at)
                positive(pe, v_done, at)
                t = half * HALF + c * P
                mm(ps_k[:, 0:MIX_COLS], xT[0][:, t:t + P], wkv[:], start=True, stop=False)
                mm(ps_k[:, 0:MIX_COLS], ones3[:], bias_rows[:], start=False, stop=True).then_inc(k_ready, 1)

            def score(w, a, c):
                positive(pe, inner_done, 4 * w + c - 1)
                pe.wait_ge(tables_used, 6 * w + (c + 3 if c else 2))
                mm(ps_s[:, c % 2], k_chan[:, a % 2, c * P:(c + 1) * P], q_wide[:, a % 2, c], start=True, stop=True
                   ).then_inc(s_ready, 1)

            def chunk(n, a, c):
                w = 4 * n + a
                g, half, cc = a % 2, a // 2, 4 * (a // 2) + c
                s_now = start[:, g] if cc == 0 else state[:, g, cc % 2]
                at = state_index(n, a, c)
                if cc:
                    before = state_index(n, a, c - 1) if c else state_index(n, a - 2, CHUNKS - 1)
                    pe.wait_ge(st_done, before + 1)
                if c == 0:
                    pe.wait_ge(v_done, 8 * n + 4 * half + 4)
                    pe.wait_ge(k_done, 8 * n + 4 * half + 4)
                if at is not None:
                    positive(pe, st_done, at)
                    mm(ps_st[:], turn_m[:, g], s_now, start=True, stop=False)
                    mm(ps_st[:], k_tok[:, half, c, g * P:(g + 1) * P],
                       v_tok[:, half, c, g * GH:(g + 1) * GH].rearrange("p h x -> p (h x)"),
                       start=False, stop=True).then_inc(st_ready, 1)
                if c == 0:
                    positive(pe, o_copied, w)
                if c == 0:
                    pe.wait_ge(tables_used, 6 * w + 3)
                o = ps_o[:, c * P:(c + 1) * P]
                mm(o, s_now, q_state[:, a % 2, c * P:(c + 1) * P], start=True, stop=False, skip_group_check=True)
                pe.wait_ge(inner_done, 4 * w + c + 1)
                for j in range(GH):
                    last = mm(ps_o[32 * j:32 * j + 32, c * P:(c + 1) * P], v_tok[:, half, c, g * GH + j],
                              inner[:, c % 2, j * P:(j + 1) * P], start=False, stop=True, skip_group_check=True)
                last.then_inc(chunk_done, 1)

            def turn_item(w, a):
                pe.wait_ge(o_copied, w + 1)
                positive(pe, t_added, w)
                for c in range(CHUNKS):
                    last = nc.tensor.transpose(ps_t[:, c * P:(c + 1) * P], o_chan[:, a % 2, c * P:(c + 1) * P],
                                               ident[:])
                last.then_inc(o_turned, 1)

            def body(n):
                finish, prepare, _ = parts_of(n)
                if isinstance(n, int) and n < 0:
                    use_x(n, "xt0")
                    use_x(n, "xt1")
                for a, c, steps, nxt in slots(n):
                    w = 4 * n + a
                    if steps and c < CHUNKS - 1:
                        score(w, a, c + 1)
                    elif c == CHUNKS - 1 and nxt:
                        score(w + 1, (a + 1) % 4, 0)
                    if nxt and (a, c) == (3, 0):
                        pe.wait_ge(x_free, use(n, "xt1") + 1)
                    if nxt and c < 2:
                        project(w + 1, (a + 1) % 4, c)
                    if nxt and a % 2:
                        if a == 1:
                            mix(n, 1, c)
                        else:
                            mix(n + 1, 0, c)
                    if c == 1 and (finish if a == 0 else steps):
                        turn_item(w - 1, (a - 1) % 4)
                    for name in filled_at(n, a, c):
                        if not (isinstance(n, int) and n < 0):
                            use_x(n, name)
                    if steps:
                        chunk(n, a, c)

            images(pe, body)


def conv_attention_mixtures(nc, dram, out):
    with ExitStack() as ctx:
        sb, _, sem = allocator(nc, ctx)
        T = sb("tokens", [P, TOK])
        gates = sb("gates", [P, TILES * IMAGES * E])
        ident = sb("ident", [P, P])
        xT_dram = nc.dram_tensor("normalised_t", (P, TOK), F32, kind="Internal").ap()
        ident_zero = sem("ident_zero")

        with nc.Block() as block:
            @block.gpsimd
            def _(pool):
                nc.gpsimd.memset(ident[:], 0.0).then_inc(ident_zero, 1)
                pool.wait_ge(ident_zero, 1)
                nc.gpsimd.affine_select(out=ident[:], in_=ident[:], compare_op=ALU.not_equal, fill=1.0, base=0,
                                        pattern=[[-1, P]], channel_multiplier=1).then_inc(ident_zero, 1)
                pool.wait_ge(ident_zero, 2)

        convolution_stage(nc, T, ident, dram)
        attention_stage(nc, T, xT_dram, gates, ident, dram)
        mixture_stage(nc, T, xT_dram, gates, ident, dram["L2_ffn_W1"], dram["L2_ffn_b1"], dram["L2_ffn_W2"],
                      dram["L2_ffn_b2"], gated=True)
        decay_stage(nc, T, xT_dram, gates, ident, dram)
        mixture_stage(nc, T, xT_dram, gates, ident, dram["L3_ffn_W1"], dram["L3_ffn_b1"], dram["L3_ffn_W2"],
                      dram["L3_ffn_b2"], gated=False, out=out)


_INS = ["x", "L0_conv_w_channel", "L0_conv_w_spatial", "L0_conv_w_temporal", "L1_conv_w1", "L1_conv_w2",
        "L1_conv_fc1_w", "L1_conv_fc2_w", "L2_attn_Wq", "L2_attn_Wk", "L2_attn_Wv", "L2_attn_Wo", "L2_ffn_Wg",
        "L2_ffn_bg", "L2_ffn_W1", "L2_ffn_b1", "L2_ffn_W2", "L2_ffn_b2", "L3_attn_wq_w", "L3_attn_wq_b",
        "L3_attn_wk_w", "L3_attn_wk_b", "L3_attn_wv_w", "L3_attn_wv_b", "L3_attn_phazor_re",
        "L3_attn_phazor_im", "L3_attn_amplitude", "L3_attn_last_conv_re", "L3_attn_last_conv_im", "L3_ffn_Wg",
        "L3_ffn_bg", "L3_ffn_W1", "L3_ffn_b1", "L3_ffn_W2", "L3_ffn_b2"]
_OUTS = [((IMAGES, C, SIDE, SIDE), "float32")]


def kernel(**inputs):
    import numpy as _np
    import concourse.bacc as _bacc
    from concourse import mybir as _mybir
    from concourse.bass_utils import run_bass_kernel_spmd as _run

    nc = _bacc.Bacc("TRN2", target_bir_lowering=False, num_devices=1)
    arrays, dram, outs = {}, {}, []
    for name in _INS:
        a = _np.ascontiguousarray(inputs[name])
        arrays[f"in_{name}_dram"] = a
        dram[name] = nc.dram_tensor(f"in_{name}_dram", a.shape, _mybir.dt.from_np(a.dtype), kind="ExternalInput").ap()
    for i, (shape, dtype) in enumerate(_OUTS):
        dt = _mybir.dt.from_np(_np.dtype(dtype))
        outs.append(nc.dram_tensor(f"out_{i}_dram", shape, dt, kind="ExternalOutput").ap())
    conv_attention_mixtures(nc, dram, outs[0])
    r = _run(nc, [arrays], core_ids=[0])
    got = tuple(r.results[0][f"out_{i}_dram"] for i in range(len(_OUTS)))
    return got[0]
```
